# Optimizing a Trainium2 kernel written in Bass

```python
import numpy as np
import jax
import jax.numpy as jnp

def _softmax(x, axis=-1):
    return jax.nn.softmax(x, axis=axis)

def _gelu(x):
    return jax.nn.gelu(x, approximate=True)

def _silu(x):
    return jax.nn.silu(x)

def _sigmoid(x):
    return jax.nn.sigmoid(x)

def _layernorm(x, axis=-1, eps=1e-05):
    m = jnp.mean(x, axis=axis, keepdims=True)
    v = jnp.var(x, axis=axis, keepdims=True)
    return (x - m) / jnp.sqrt(v + eps)

def _scatter_add(tgt, idx, src, axis=0):
    return tgt.at[idx].add(src)

def _segment_sum(src, seg, n):
    return jax.ops.segment_sum(src, seg, n)
kernel_name = 'mk_conv_seq_d4_conv_nchw128_r2_268997'

def setup_inputs(seed: int=0):
    np.random.seed(seed)
    _w = jnp.asarray

    def _rec_inputs():
        import jax
        import jax.numpy as jnp
        _gk = jax.random.key(seed)
        x = -0.0002928 + 1 * jax.random.normal(jax.random.fold_in(_gk, 1), (8, 64, 32, 32), jnp.float32)
        return x
    x = _rec_inputs()

    def _L0_conv_setup():
        import jax, jax.numpy as jnp
        import numpy as np
        DIM = 64
        HEADS = 8
        K_RATIO = 0.5
        LAYER_SCALE = 0.1
        EPS = 1e-06

        def _group_norm(x, g, b, groups):
            B, C, H, W = x.shape
            xg = x.reshape(B, groups, -1)
            mu = xg.mean(-1, keepdims=True)
            var = xg.var(-1, keepdims=True)
            xn = ((xg - mu) * jax.lax.rsqrt(var + EPS)).reshape(B, C, H, W)
            return xn * g[:, None, None] + b[:, None, None]

        def _conv1x1(x, w):
            return jnp.einsum('oc,bchw->bohw', w, x)

        def _l2norm(t):
            return t / jnp.maximum(jnp.linalg.norm(t, axis=-1, keepdims=True), 1e-12)

        def _sparse_attn(ll, qkv_w, proj_w, g, b):
            B, C, H, W = ll.shape
            N = H * W
            nh = HEADS
            hd = C // nh
            scale = hd ** (-0.5)
            qkv = _conv1x1(ll, qkv_w).reshape(B, 3, nh, hd, N)
            q = jnp.swapaxes(qkv[:, 0], -1, -2)
            k = jnp.swapaxes(qkv[:, 1], -1, -2)
            v = jnp.swapaxes(qkv[:, 2], -1, -2)
            q = _l2norm(q)
            k = _l2norm(k)
            attn = jnp.einsum('bhnd,bhmd->bhnm', q, k) * scale
            attn = jnp.clip(attn, -32.0, 32.0)
            k_num = max(int(N * K_RATIO), 1)
            if k_num < N:
                _, idx = jax.lax.top_k(attn, k_num)
                flat_attn = attn.reshape(-1, N)
                rows = jnp.arange(flat_attn.shape[0])[:, None]
                mask = jnp.zeros(flat_attn.shape, dtype=bool).at[rows, idx.reshape(-1, k_num)].set(True)
                attn = jnp.where(mask.reshape(attn.shape), attn, jnp.float32(-1000000000.0))
            attn = jax.nn.softmax(attn, axis=-1)
            out = jnp.einsum('bhnm,bhmd->bhnd', attn, v)
            out = jnp.swapaxes(out, 2, 3).reshape(B, C, H, W)
            out = _conv1x1(out, proj_w)
            return _group_norm(out, g, b, min(32, C // 4))

        def _high_enhance(h, dw_w, g1, b1, pw_w, g2, b2, alpha):
            C = h.shape[1]
            groups = min(32, C // 8)
            y = jax.lax.conv_general_dilated(h, dw_w, window_strides=(1, 1), padding='SAME', feature_group_count=C, dimension_numbers=('NCHW', 'OIHW', 'NCHW'))
            y = jax.nn.silu(_group_norm(y, g1, b1, groups))
            y = _group_norm(_conv1x1(y, pw_w), g2, b2, groups)
            return h + alpha[0] * y

        def _iwt(ll, lh, hl, hh):
            a = ll - lh - hl + hh
            bq = ll - lh + hl - hh
            c = ll + lh - hl - hh
            d = ll + lh + hl + hh
            B, C, H, W = ll.shape
            row_even = jnp.stack([a, c], axis=-1)
            row_odd = jnp.stack([bq, d], axis=-1)
            h = jnp.stack([row_even, row_odd], axis=3)
            return h.reshape(B, C, 2 * H, 2 * W)

        def _ffn(x, w1, g1, b1, w2, g2, b2):
            d = x.shape[1]
            groups = min(32, d // 4)
            y = _group_norm(_conv1x1(x, w1), g1, b1, groups)
            y = jax.nn.gelu(y, approximate=False)
            return _group_norm(_conv1x1(y, w2), g2, b2, groups)
        key = jax.random.key(seed)
        ks = jax.random.split(key, 18)
        d = DIM
        hd3 = d * 3
        f = lambda k, shape, s=0.05: jax.random.normal(k, shape, dtype=jnp.float32) * s
        return {'x': jax.random.normal(ks[0], (8, d, 32, 32), dtype=jnp.float32), 'qkv_w': f(ks[1], (3 * d, d)), 'proj_w': f(ks[2], (d, d)), 'attn_gn_g': 1.0 + f(ks[3], (d,)), 'attn_gn_b': f(ks[4], (d,)), 'he_dw_w': f(ks[5], (hd3, 1, 3, 3)), 'he_gn1_g': 1.0 + f(ks[6], (hd3,)), 'he_gn1_b': f(ks[7], (hd3,)), 'he_pw_w': f(ks[8], (hd3, hd3)), 'he_gn2_g': 1.0 + f(ks[9], (hd3,)), 'he_gn2_b': f(ks[10], (hd3,)), 'alpha': jnp.array([0.1], dtype=jnp.float32), 'ffn_w1': f(ks[11], (2 * d, d)), 'ffn_gn1_g': 1.0 + f(ks[12], (2 * d,)), 'ffn_gn1_b': f(ks[13], (2 * d,)), 'ffn_w2': f(ks[14], (d, 2 * d)), 'ffn_gn2_g': 1.0 + f(ks[15], (d,)), 'ffn_gn2_b': f(ks[16], (d,))}
    _L0_conv_all = _L0_conv_setup()
    _L0_conv_in = {k: v for k, v in _L0_conv_all.items() if k in ('qkv_w', 'proj_w', 'attn_gn_g', 'attn_gn_b', 'he_dw_w', 'he_gn1_g', 'he_gn1_b', 'he_pw_w', 'he_gn2_g', 'he_gn2_b', 'alpha', 'ffn_w1', 'ffn_gn1_g', 'ffn_gn1_b', 'ffn_w2', 'ffn_gn2_g', 'ffn_gn2_b')}
    del _L0_conv_all

    def _L1_conv_setup():
        import jax, jax.numpy as jnp
        import numpy as np
        EPS = 1e-05

        def _conv3x3(x, w, stride=1):
            return jax.lax.conv_general_dilated(x, w, (stride, stride), ((1, 1), (1, 1)), dimension_numbers=('NCHW', 'OIHW', 'NCHW'))

        def _adder3x3(x, w):
            N, C, H, W = x.shape
            xp = jnp.pad(x, ((0, 0), (0, 0), (1, 1), (1, 1)))
            patches = jnp.stack([xp[:, :, i:i + H, j:j + W] for i in range(3) for j in range(3)], axis=2)
            patches = patches.reshape(N, C * 9, H, W).transpose(0, 2, 3, 1)
            wf = w.reshape(w.shape[0], -1)

            def per_co(wc):
                return -jnp.sum(jnp.abs(patches - wc), axis=-1)
            out = jax.lax.map(per_co, wf)
            return jnp.transpose(out, (1, 0, 2, 3))

        def _bn_train(x, gamma, beta):
            mean = jnp.mean(x, axis=(0, 2, 3), keepdims=True)
            var = jnp.var(x, axis=(0, 2, 3), keepdims=True)
            xn = (x - mean) * jax.lax.rsqrt(var + EPS)
            return xn * gamma[None, :, None, None] + beta[None, :, None, None]
        key = jax.random.key(seed)
        ks = jax.random.split(key, 5)
        N, C, H, W = (32, 64, 28, 28)
        x = jax.random.normal(ks[0], (N, C, H, W), dtype=jnp.float32)
        conv1_w = jax.random.normal(ks[1], (C, C, 3, 3), dtype=jnp.float32) * 0.05
        add1_w = jax.random.normal(ks[2], (C, C, 3, 3), dtype=jnp.float32) * 0.05
        conv2_w = jax.random.normal(ks[3], (C, C, 3, 3), dtype=jnp.float32) * 0.05
        add2_w = jax.random.normal(ks[4], (C, C, 3, 3), dtype=jnp.float32) * 0.05
        bn1_g = jnp.ones((C,), jnp.float32)
        bn1_b = jnp.zeros((C,), jnp.float32)
        bn2_g = jnp.ones((C,), jnp.float32)
        bn2_b = jnp.zeros((C,), jnp.float32)
        return {'x': x, 'conv1_w': conv1_w, 'add1_w': add1_w, 'bn1_g': bn1_g, 'bn1_b': bn1_b, 'conv2_w': conv2_w, 'add2_w': add2_w, 'bn2_g': bn2_g, 'bn2_b': bn2_b}
    _L1_conv_all = _L1_conv_setup()
    _L1_conv_in = {k: v for k, v in _L1_conv_all.items() if k in ('conv1_w', 'add1_w', 'bn1_g', 'bn1_b', 'conv2_w', 'add2_w', 'bn2_g', 'bn2_b')}
    del _L1_conv_all

    def _L2_conv_setup():
        import jax, jax.numpy as jnp
        import numpy as np
        EPS = 1e-05
        A_BIT = 4
        W_BIT = 4

        def ste_round(x):
            return x + jax.lax.stop_gradient(jnp.round(x) - x)

        def quantize_weight(w, w_bit):
            n = 2.0 ** w_bit - 1.0
            wt = jnp.tanh(w)
            wt = wt / (2.0 * jnp.max(jnp.abs(wt))) + 0.5
            return 2.0 * ste_round(wt * n) / n - 1.0

        def quantize_act(x, a_bit):
            n = 2.0 ** a_bit - 1.0
            return ste_round(jnp.clip(x, 0.0, 1.0) * n) / n

        def conv3x3(x, w, stride):
            return jax.lax.conv_general_dilated(x, w, window_strides=(stride, stride), padding=((1, 1), (1, 1)), dimension_numbers=('NCHW', 'OIHW', 'NCHW'))

        def batchnorm(x, gamma, beta, mean, var):
            inv = jax.lax.rsqrt(var + EPS)
            scale = (gamma * inv)[None, :, None, None]
            shift = (beta - mean * gamma * inv)[None, :, None, None]
            return x * scale + shift
        key = jax.random.key(seed)
        ks = jax.random.split(key, 8)
        B, C, H, W = (32, 64, 56, 56)
        return {'x': jax.random.normal(ks[0], (B, C, H, W), jnp.float32), 'w1': jax.random.normal(ks[1], (C, C, 3, 3), jnp.float32) * 0.05, 'w2': jax.random.normal(ks[2], (C, C, 3, 3), jnp.float32) * 0.05, 'gamma1': jnp.ones((C,), jnp.float32), 'beta1': jnp.zeros((C,), jnp.float32), 'mean1': jax.random.normal(ks[3], (C,), jnp.float32) * 0.1, 'var1': jax.random.uniform(ks[4], (C,), jnp.float32, 0.5, 1.5), 'gamma2': jnp.ones((C,), jnp.float32), 'beta2': jnp.zeros((C,), jnp.float32), 'mean2': jax.random.normal(ks[5], (C,), jnp.float32) * 0.1, 'var2': jax.random.uniform(ks[6], (C,), jnp.float32, 0.5, 1.5)}
    _L2_conv_all = _L2_conv_setup()
    _L2_conv_in = {k: v for k, v in _L2_conv_all.items() if k in ('w1', 'w2', 'gamma1', 'beta1', 'mean1', 'var1', 'gamma2', 'beta2', 'mean2', 'var2')}
    del _L2_conv_all

    def _L3_conv_setup():
        import jax, jax.numpy as jnp
        import numpy as np
        from jax import lax
        B, C, H, W = (4, 64, 64, 64)
        DG = 2
        K = 9
        EPS = 1e-05

        def conv2d(x, w, stride=1, pad=1):
            return lax.conv_general_dilated(x, w, (stride, stride), [(pad, pad), (pad, pad)], dimension_numbers=('NCHW', 'OIHW', 'NCHW'))

        def bn(x, p):
            g, b, m, v = (p[0], p[1], p[2], p[3])
            inv = g / jnp.sqrt(v + EPS)
            return x * inv[:, None, None] + (b - m * inv)[:, None, None]

        def deform_sample(x, py, px):
            Bb, Cc, Hh, Ww = x.shape
            Cg = Cc // DG
            xg = x.reshape(Bb, DG, Cg, Hh * Ww)
            y0 = jnp.floor(py)
            x0 = jnp.floor(px)
            fy = py - y0
            fx = px - x0
            y0i = y0.astype(jnp.int32)
            x0i = x0.astype(jnp.int32)

            def corner(yi, xi, wgt):
                valid = (yi >= 0) & (yi < Hh) & (xi >= 0) & (xi < Ww)
                idx = (jnp.clip(yi, 0, Hh - 1) * Ww + jnp.clip(xi, 0, Ww - 1)).reshape(Bb, DG, -1)
                v = jnp.take_along_axis(xg, idx[:, :, None, :], axis=3)
                return v * (wgt * valid).reshape(Bb, DG, 1, -1)
            val = corner(y0i, x0i, (1 - fy) * (1 - fx)) + corner(y0i, x0i + 1, (1 - fy) * fx) + corner(y0i + 1, x0i, fy * (1 - fx)) + corner(y0i + 1, x0i + 1, fy * fx)
            return val.reshape(Bb, DG, Cg, K, Hh, Ww)

        def modulated_deform_conv(x, off_w, off_b, dc_w, dc_b):
            Bb, Cc, Hh, Ww = x.shape
            off_out = conv2d(x, off_w) + off_b[None, :, None, None]
            o = off_out[:, :2 * DG * K].reshape(Bb, DG, K, 2, Hh, Ww)
            mask = jax.nn.sigmoid(off_out[:, 2 * DG * K:]).reshape(Bb, DG, K, Hh, Ww)
            ky = (jnp.arange(K) // 3 - 1).astype(x.dtype)
            kx = (jnp.arange(K) % 3 - 1).astype(x.dtype)
            iy = jnp.arange(Hh, dtype=x.dtype)[:, None]
            ix = jnp.arange(Ww, dtype=x.dtype)[None, :]
            py = o[:, :, :, 0] + iy + ky[None, None, :, None, None]
            px = o[:, :, :, 1] + ix + kx[None, None, :, None, None]
            g = deform_sample(x, py, px) * mask[:, :, None]
            wr = dc_w.reshape(dc_w.shape[0], DG, Cc // DG, K)
            out = jnp.einsum('odck,bdckhw->bohw', wr, g)
            return out + dc_b[None, :, None, None]
        key = jax.random.key(seed)
        ks = jax.random.split(key, 16)
        s3 = 1.0 / np.sqrt(C * 9)
        s1 = 1.0 / np.sqrt(C)

        def bn_params(k):
            k1, k2, k3, k4 = jax.random.split(k, 4)
            return jnp.stack([jax.random.uniform(k1, (C,)) + 0.5, jax.random.normal(k2, (C,)) * 0.1, jax.random.normal(k3, (C,)) * 0.1, jax.random.uniform(k4, (C,)) + 0.5])
        return {'x': jax.random.normal(ks[0], (B, C, H, W), jnp.float32), 'rb_w1': jax.random.normal(ks[1], (C, C, 3, 3), jnp.float32) * s3, 'rb_b1': jax.random.normal(ks[2], (C,), jnp.float32) * 0.01, 'rb_bn1': bn_params(ks[3]), 'rb_w2': jax.random.normal(ks[4], (C, C, 3, 3), jnp.float32) * s3, 'rb_b2': jax.random.normal(ks[5], (C,), jnp.float32) * 0.01, 'rb_bn2': bn_params(ks[6]), 'off_w': jax.random.normal(ks[7], (3 * DG * K, C, 3, 3), jnp.float32) * s3 * 0.1, 'off_b': jax.random.normal(ks[8], (3 * DG * K,), jnp.float32) * 0.01, 'dc_w': jax.random.normal(ks[9], (C, C, 3, 3), jnp.float32) * s3, 'dc_b': jax.random.normal(ks[10], (C,), jnp.float32) * 0.01, 'bn1': bn_params(ks[11]), 'cv2_w': jax.random.normal(ks[12], (C, C, 1, 1), jnp.float32) * s1, 'bn2': bn_params(ks[13])}
    _L3_conv_all = _L3_conv_setup()
    _L3_conv_in = {k: v for k, v in _L3_conv_all.items() if k in ('rb_w1', 'rb_b1', 'rb_bn1', 'rb_w2', 'rb_b2', 'rb_bn2', 'off_w', 'off_b', 'dc_w', 'dc_b', 'bn1', 'cv2_w', 'bn2')}
    del _L3_conv_all
    return {'x': x, 'L0_conv_qkv_w': _L0_conv_in['qkv_w'], 'L0_conv_proj_w': _L0_conv_in['proj_w'], 'L0_conv_attn_gn_g': _L0_conv_in['attn_gn_g'], 'L0_conv_attn_gn_b': _L0_conv_in['attn_gn_b'], 'L0_conv_he_dw_w': _L0_conv_in['he_dw_w'], 'L0_conv_he_gn1_g': _L0_conv_in['he_gn1_g'], 'L0_conv_he_gn1_b': _L0_conv_in['he_gn1_b'], 'L0_conv_he_pw_w': _L0_conv_in['he_pw_w'], 'L0_conv_he_gn2_g': _L0_conv_in['he_gn2_g'], 'L0_conv_he_gn2_b': _L0_conv_in['he_gn2_b'], 'L0_conv_alpha': _L0_conv_in['alpha'], 'L0_conv_ffn_w1': _L0_conv_in['ffn_w1'], 'L0_conv_ffn_gn1_g': _L0_conv_in['ffn_gn1_g'], 'L0_conv_ffn_gn1_b': _L0_conv_in['ffn_gn1_b'], 'L0_conv_ffn_w2': _L0_conv_in['ffn_w2'], 'L0_conv_ffn_gn2_g': _L0_conv_in['ffn_gn2_g'], 'L0_conv_ffn_gn2_b': _L0_conv_in['ffn_gn2_b'], 'L1_conv_conv1_w': _L1_conv_in['conv1_w'], 'L1_conv_add1_w': _L1_conv_in['add1_w'], 'L1_conv_bn1_g': _L1_conv_in['bn1_g'], 'L1_conv_bn1_b': _L1_conv_in['bn1_b'], 'L1_conv_conv2_w': _L1_conv_in['conv2_w'], 'L1_conv_add2_w': _L1_conv_in['add2_w'], 'L1_conv_bn2_g': _L1_conv_in['bn2_g'], 'L1_conv_bn2_b': _L1_conv_in['bn2_b'], 'L2_conv_w1': _L2_conv_in['w1'], 'L2_conv_w2': _L2_conv_in['w2'], 'L2_conv_gamma1': _L2_conv_in['gamma1'], 'L2_conv_beta1': _L2_conv_in['beta1'], 'L2_conv_mean1': _L2_conv_in['mean1'], 'L2_conv_var1': _L2_conv_in['var1'], 'L2_conv_gamma2': _L2_conv_in['gamma2'], 'L2_conv_beta2': _L2_conv_in['beta2'], 'L2_conv_mean2': _L2_conv_in['mean2'], 'L2_conv_var2': _L2_conv_in['var2'], 'L3_conv_rb_w1': _L3_conv_in['rb_w1'], 'L3_conv_rb_b1': _L3_conv_in['rb_b1'], 'L3_conv_rb_bn1': _L3_conv_in['rb_bn1'], 'L3_conv_rb_w2': _L3_conv_in['rb_w2'], 'L3_conv_rb_b2': _L3_conv_in['rb_b2'], 'L3_conv_rb_bn2': _L3_conv_in['rb_bn2'], 'L3_conv_off_w': _L3_conv_in['off_w'], 'L3_conv_off_b': _L3_conv_in['off_b'], 'L3_conv_dc_w': _L3_conv_in['dc_w'], 'L3_conv_dc_b': _L3_conv_in['dc_b'], 'L3_conv_bn1': _L3_conv_in['bn1'], 'L3_conv_cv2_w': _L3_conv_in['cv2_w'], 'L3_conv_bn2': _L3_conv_in['bn2']}

def reference(x, L0_conv_qkv_w, L0_conv_proj_w, L0_conv_attn_gn_g, L0_conv_attn_gn_b, L0_conv_he_dw_w, L0_conv_he_gn1_g, L0_conv_he_gn1_b, L0_conv_he_pw_w, L0_conv_he_gn2_g, L0_conv_he_gn2_b, L0_conv_alpha, L0_conv_ffn_w1, L0_conv_ffn_gn1_g, L0_conv_ffn_gn1_b, L0_conv_ffn_w2, L0_conv_ffn_gn2_g, L0_conv_ffn_gn2_b, L1_conv_conv1_w, L1_conv_add1_w, L1_conv_bn1_g, L1_conv_bn1_b, L1_conv_conv2_w, L1_conv_add2_w, L1_conv_bn2_g, L1_conv_bn2_b, L2_conv_w1, L2_conv_w2, L2_conv_gamma1, L2_conv_beta1, L2_conv_mean1, L2_conv_var1, L2_conv_gamma2, L2_conv_beta2, L2_conv_mean2, L2_conv_var2, L3_conv_rb_w1, L3_conv_rb_b1, L3_conv_rb_bn1, L3_conv_rb_w2, L3_conv_rb_b2, L3_conv_rb_bn2, L3_conv_off_w, L3_conv_off_b, L3_conv_dc_w, L3_conv_dc_b, L3_conv_bn1, L3_conv_cv2_w, L3_conv_bn2):
    import jax
    import jax.numpy as jnp

    def _L0_conv_ref(x, qkv_w, proj_w, attn_gn_g, attn_gn_b, he_dw_w, he_gn1_g, he_gn1_b, he_pw_w, he_gn2_g, he_gn2_b, alpha, ffn_w1, ffn_gn1_g, ffn_gn1_b, ffn_w2, ffn_gn2_g, ffn_gn2_b):
        import jax, jax.numpy as jnp
        import numpy as np
        DIM = 64
        HEADS = 8
        K_RATIO = 0.5
        LAYER_SCALE = 0.1
        EPS = 1e-06

        def _group_norm(x, g, b, groups):
            B, C, H, W = x.shape
            xg = x.reshape(B, groups, -1)
            mu = xg.mean(-1, keepdims=True)
            var = xg.var(-1, keepdims=True)
            xn = ((xg - mu) * jax.lax.rsqrt(var + EPS)).reshape(B, C, H, W)
            return xn * g[:, None, None] + b[:, None, None]

        def _conv1x1(x, w):
            return jnp.einsum('oc,bchw->bohw', w, x)

        def _l2norm(t):
            return t / jnp.maximum(jnp.linalg.norm(t, axis=-1, keepdims=True), 1e-12)

        def _sparse_attn(ll, qkv_w, proj_w, g, b):
            B, C, H, W = ll.shape
            N = H * W
            nh = HEADS
            hd = C // nh
            scale = hd ** (-0.5)
            qkv = _conv1x1(ll, qkv_w).reshape(B, 3, nh, hd, N)
            q = jnp.swapaxes(qkv[:, 0], -1, -2)
            k = jnp.swapaxes(qkv[:, 1], -1, -2)
            v = jnp.swapaxes(qkv[:, 2], -1, -2)
            q = _l2norm(q)
            k = _l2norm(k)
            attn = jnp.einsum('bhnd,bhmd->bhnm', q, k) * scale
            attn = jnp.clip(attn, -32.0, 32.0)
            k_num = max(int(N * K_RATIO), 1)
            if k_num < N:
                _, idx = jax.lax.top_k(attn, k_num)
                flat_attn = attn.reshape(-1, N)
                rows = jnp.arange(flat_attn.shape[0])[:, None]
                mask = jnp.zeros(flat_attn.shape, dtype=bool).at[rows, idx.reshape(-1, k_num)].set(True)
                attn = jnp.where(mask.reshape(attn.shape), attn, jnp.float32(-1000000000.0))
            attn = jax.nn.softmax(attn, axis=-1)
            out = jnp.einsum('bhnm,bhmd->bhnd', attn, v)
            out = jnp.swapaxes(out, 2, 3).reshape(B, C, H, W)
            out = _conv1x1(out, proj_w)
            return _group_norm(out, g, b, min(32, C // 4))

        def _high_enhance(h, dw_w, g1, b1, pw_w, g2, b2, alpha):
            C = h.shape[1]
            groups = min(32, C // 8)
            y = jax.lax.conv_general_dilated(h, dw_w, window_strides=(1, 1), padding='SAME', feature_group_count=C, dimension_numbers=('NCHW', 'OIHW', 'NCHW'))
            y = jax.nn.silu(_group_norm(y, g1, b1, groups))
            y = _group_norm(_conv1x1(y, pw_w), g2, b2, groups)
            return h + alpha[0] * y

        def _iwt(ll, lh, hl, hh):
            a = ll - lh - hl + hh
            bq = ll - lh + hl - hh
            c = ll + lh - hl - hh
            d = ll + lh + hl + hh
            B, C, H, W = ll.shape
            row_even = jnp.stack([a, c], axis=-1)
            row_odd = jnp.stack([bq, d], axis=-1)
            h = jnp.stack([row_even, row_odd], axis=3)
            return h.reshape(B, C, 2 * H, 2 * W)

        def _ffn(x, w1, g1, b1, w2, g2, b2):
            d = x.shape[1]
            groups = min(32, d // 4)
            y = _group_norm(_conv1x1(x, w1), g1, b1, groups)
            y = jax.nn.gelu(y, approximate=False)
            return _group_norm(_conv1x1(y, w2), g2, b2, groups)
        x1 = x[:, :, 0::2, 0::2]
        x2 = x[:, :, 1::2, 0::2]
        x3 = x[:, :, 0::2, 1::2]
        x4 = x[:, :, 1::2, 1::2]
        ll = (x1 + x2 + x3 + x4) * 0.5
        lh = (-x1 - x2 + x3 + x4) * 0.5
        hl = (-x1 + x2 - x3 + x4) * 0.5
        hh = (x1 - x2 - x3 + x4) * 0.5
        high = jnp.concatenate([lh, hl, hh], axis=1)
        ll_out = _sparse_attn(ll, qkv_w, proj_w, attn_gn_g, attn_gn_b)
        high_out = _high_enhance(high, he_dw_w, he_gn1_g, he_gn1_b, he_pw_w, he_gn2_g, he_gn2_b, alpha)
        C = ll.shape[1]
        x_rec = _iwt(ll + ll_out, high_out[:, :C], high_out[:, C:2 * C], high_out[:, 2 * C:])
        out = x + LAYER_SCALE * x_rec
        out = out + LAYER_SCALE * _ffn(out, ffn_w1, ffn_gn1_g, ffn_gn1_b, ffn_w2, ffn_gn2_g, ffn_gn2_b)
        return out

    def _L1_conv_ref(x, conv1_w, add1_w, bn1_g, bn1_b, conv2_w, add2_w, bn2_g, bn2_b):
        import jax, jax.numpy as jnp
        import numpy as np
        EPS = 1e-05

        def _conv3x3(x, w, stride=1):
            return jax.lax.conv_general_dilated(x, w, (stride, stride), ((1, 1), (1, 1)), dimension_numbers=('NCHW', 'OIHW', 'NCHW'))

        def _adder3x3(x, w):
            N, C, H, W = x.shape
            xp = jnp.pad(x, ((0, 0), (0, 0), (1, 1), (1, 1)))
            patches = jnp.stack([xp[:, :, i:i + H, j:j + W] for i in range(3) for j in range(3)], axis=2)
            patches = patches.reshape(N, C * 9, H, W).transpose(0, 2, 3, 1)
            wf = w.reshape(w.shape[0], -1)

            def per_co(wc):
                return -jnp.sum(jnp.abs(patches - wc), axis=-1)
            out = jax.lax.map(per_co, wf)
            return jnp.transpose(out, (1, 0, 2, 3))

        def _bn_train(x, gamma, beta):
            mean = jnp.mean(x, axis=(0, 2, 3), keepdims=True)
            var = jnp.var(x, axis=(0, 2, 3), keepdims=True)
            xn = (x - mean) * jax.lax.rsqrt(var + EPS)
            return xn * gamma[None, :, None, None] + beta[None, :, None, None]
        out = _adder3x3(_conv3x3(x, conv1_w, stride=1), add1_w)
        out = jax.nn.relu(_bn_train(out, bn1_g, bn1_b))
        out = _adder3x3(_conv3x3(out, conv2_w, stride=1), add2_w)
        out = _bn_train(out, bn2_g, bn2_b)
        return jax.nn.relu(out + x)

    def _L2_conv_ref(x, w1, w2, gamma1, beta1, mean1, var1, gamma2, beta2, mean2, var2):
        import jax, jax.numpy as jnp
        import numpy as np
        EPS = 1e-05
        A_BIT = 4
        W_BIT = 4

        def ste_round(x):
            return x + jax.lax.stop_gradient(jnp.round(x) - x)

        def quantize_weight(w, w_bit):
            n = 2.0 ** w_bit - 1.0
            wt = jnp.tanh(w)
            wt = wt / (2.0 * jnp.max(jnp.abs(wt))) + 0.5
            return 2.0 * ste_round(wt * n) / n - 1.0

        def quantize_act(x, a_bit):
            n = 2.0 ** a_bit - 1.0
            return ste_round(jnp.clip(x, 0.0, 1.0) * n) / n

        def conv3x3(x, w, stride):
            return jax.lax.conv_general_dilated(x, w, window_strides=(stride, stride), padding=((1, 1), (1, 1)), dimension_numbers=('NCHW', 'OIHW', 'NCHW'))

        def batchnorm(x, gamma, beta, mean, var):
            inv = jax.lax.rsqrt(var + EPS)
            scale = (gamma * inv)[None, :, None, None]
            shift = (beta - mean * gamma * inv)[None, :, None, None]
            return x * scale + shift
        out = conv3x3(x, quantize_weight(w1, W_BIT), 1)
        out = batchnorm(out, gamma1, beta1, mean1, var1)
        out = quantize_act(out, A_BIT)
        out = conv3x3(out, quantize_weight(w2, W_BIT), 1)
        out = batchnorm(out, gamma2, beta2, mean2, var2)
        out = out + x
        out = quantize_act(out, A_BIT)
        return out

    def _L3_conv_ref(x, rb_w1, rb_b1, rb_bn1, rb_w2, rb_b2, rb_bn2, off_w, off_b, dc_w, dc_b, bn1, cv2_w, bn2):
        import jax, jax.numpy as jnp
        import numpy as np
        from jax import lax
        B, C, H, W = (4, 64, 64, 64)
        DG = 2
        K = 9
        EPS = 1e-05

        def conv2d(x, w, stride=1, pad=1):
            return lax.conv_general_dilated(x, w, (stride, stride), [(pad, pad), (pad, pad)], dimension_numbers=('NCHW', 'OIHW', 'NCHW'))

        def bn(x, p):
            g, b, m, v = (p[0], p[1], p[2], p[3])
            inv = g / jnp.sqrt(v + EPS)
            return x * inv[:, None, None] + (b - m * inv)[:, None, None]

        def deform_sample(x, py, px):
            Bb, Cc, Hh, Ww = x.shape
            Cg = Cc // DG
            xg = x.reshape(Bb, DG, Cg, Hh * Ww)
            y0 = jnp.floor(py)
            x0 = jnp.floor(px)
            fy = py - y0
            fx = px - x0
            y0i = y0.astype(jnp.int32)
            x0i = x0.astype(jnp.int32)

            def corner(yi, xi, wgt):
                valid = (yi >= 0) & (yi < Hh) & (xi >= 0) & (xi < Ww)
                idx = (jnp.clip(yi, 0, Hh - 1) * Ww + jnp.clip(xi, 0, Ww - 1)).reshape(Bb, DG, -1)
                v = jnp.take_along_axis(xg, idx[:, :, None, :], axis=3)
                return v * (wgt * valid).reshape(Bb, DG, 1, -1)
            val = corner(y0i, x0i, (1 - fy) * (1 - fx)) + corner(y0i, x0i + 1, (1 - fy) * fx) + corner(y0i + 1, x0i, fy * (1 - fx)) + corner(y0i + 1, x0i + 1, fy * fx)
            return val.reshape(Bb, DG, Cg, K, Hh, Ww)

        def modulated_deform_conv(x, off_w, off_b, dc_w, dc_b):
            Bb, Cc, Hh, Ww = x.shape
            off_out = conv2d(x, off_w) + off_b[None, :, None, None]
            o = off_out[:, :2 * DG * K].reshape(Bb, DG, K, 2, Hh, Ww)
            mask = jax.nn.sigmoid(off_out[:, 2 * DG * K:]).reshape(Bb, DG, K, Hh, Ww)
            ky = (jnp.arange(K) // 3 - 1).astype(x.dtype)
            kx = (jnp.arange(K) % 3 - 1).astype(x.dtype)
            iy = jnp.arange(Hh, dtype=x.dtype)[:, None]
            ix = jnp.arange(Ww, dtype=x.dtype)[None, :]
            py = o[:, :, :, 0] + iy + ky[None, None, :, None, None]
            px = o[:, :, :, 1] + ix + kx[None, None, :, None, None]
            g = deform_sample(x, py, px) * mask[:, :, None]
            wr = dc_w.reshape(dc_w.shape[0], DG, Cc // DG, K)
            out = jnp.einsum('odck,bdckhw->bohw', wr, g)
            return out + dc_b[None, :, None, None]
        h = jax.nn.relu(bn(conv2d(x, rb_w1) + rb_b1[None, :, None, None], rb_bn1))
        h = bn(conv2d(h, rb_w2) + rb_b2[None, :, None, None], rb_bn2)
        h = jax.nn.relu(h + x)
        h = modulated_deform_conv(h, off_w, off_b, dc_w, dc_b)
        h = jax.nn.leaky_relu(bn(h, bn1), 0.1)
        h = jax.nn.leaky_relu(bn(conv2d(h, cv2_w, pad=0), bn2), 0.1)
        return x + h

    def _gn(v, G=32, eps=1e-05):
        B_, C_, H_, W_ = v.shape
        g = v.reshape(B_, G, C_ // G, H_, W_)
        m = jnp.mean(g, axis=(2, 3, 4), keepdims=True)
        s = jnp.var(g, axis=(2, 3, 4), keepdims=True)
        return ((g - m) / jnp.sqrt(s + eps)).reshape(v.shape)

    def _ln_c(v, eps=1e-06):
        m = jnp.mean(v, axis=1, keepdims=True)
        s = jnp.var(v, axis=1, keepdims=True)
        return (v - m) / jnp.sqrt(s + eps)

    def _ln_t(v, eps=1e-05):
        m = jnp.mean(v, axis=-1, keepdims=True)
        s = jnp.var(v, axis=-1, keepdims=True)
        return (v - m) / jnp.sqrt(s + eps)

    def _to_tokens(v):
        B_, C_, H_, W_ = v.shape
        return v.reshape(B_, C_, H_ * W_).transpose(0, 2, 1)

    def _from_tokens(t, like):
        B_, C_, H_, W_ = like.shape
        return t.transpose(0, 2, 1).reshape(B_, C_, H_, W_)
    x = _L0_conv_ref(x, L0_conv_qkv_w, L0_conv_proj_w, L0_conv_attn_gn_g, L0_conv_attn_gn_b, L0_conv_he_dw_w, L0_conv_he_gn1_g, L0_conv_he_gn1_b, L0_conv_he_pw_w, L0_conv_he_gn2_g, L0_conv_he_gn2_b, L0_conv_alpha, L0_conv_ffn_w1, L0_conv_ffn_gn1_g, L0_conv_ffn_gn1_b, L0_conv_ffn_w2, L0_conv_ffn_gn2_g, L0_conv_ffn_gn2_b)
    x = _L1_conv_ref(x, L1_conv_conv1_w, L1_conv_add1_w, L1_conv_bn1_g, L1_conv_bn1_b, L1_conv_conv2_w, L1_conv_add2_w, L1_conv_bn2_g, L1_conv_bn2_b)
    x = _L2_conv_ref(x, L2_conv_w1, L2_conv_w2, L2_conv_gamma1, L2_conv_beta1, L2_conv_mean1, L2_conv_var1, L2_conv_gamma2, L2_conv_beta2, L2_conv_mean2, L2_conv_var2)
    x = _L3_conv_ref(x, L3_conv_rb_w1, L3_conv_rb_b1, L3_conv_rb_bn1, L3_conv_rb_w2, L3_conv_rb_b2, L3_conv_rb_bn2, L3_conv_off_w, L3_conv_off_b, L3_conv_dc_w, L3_conv_dc_b, L3_conv_bn1, L3_conv_cv2_w, L3_conv_bn2)
    return x

_drawn_inputs = setup_inputs


def setup_inputs(seed=0):
    import zlib

    import numpy as np

    out = dict(_drawn_inputs(seed))
    spreads = {'L1_conv_bn1_g': (1.0, 0.6),
     'L1_conv_bn1_b': (0.0, 0.32),
     'L1_conv_bn2_g': (1.0, 0.2),
     'L1_conv_bn2_b': (0.0, 0.1),
     'L2_conv_gamma1': (1.0, 0.2),
     'L2_conv_beta1': (0.0, 0.1),
     'L2_conv_gamma2': (1.0, 0.2),
     'L2_conv_beta2': (0.0, 0.1)}
    factors = {'L0_conv_attn_gn_g': 2.911,
     'L0_conv_attn_gn_b': 3.131,
     'L0_conv_he_gn1_g': 17.921,
     'L0_conv_he_gn1_b': 18.965,
     'L0_conv_he_gn2_g': 19.328,
     'L0_conv_he_gn2_b': 20.285,
     'L0_conv_ffn_gn1_g': 3.272,
     'L0_conv_ffn_gn1_b': 3.314,
     'L0_conv_ffn_gn2_g': 3.305,
     'L0_conv_ffn_gn2_b': 2.98,
     'L1_conv_add1_w': 20.09,
     'L1_conv_add2_w': 4.079,
     'L3_conv_rb_b1': 26.616,
     'L3_conv_rb_b2': 8.0,
     'L3_conv_off_b': 23.599,
     'L3_conv_dc_b': 7.391}
    for name, (base, spread) in spreads.items():
        noise = np.random.default_rng([zlib.crc32(name.encode()), seed]).standard_normal(out[name].shape)
        drawn = base * np.exp(spread * noise) if base else spread * noise
        out[name] = jnp.asarray(drawn.astype(out[name].dtype))
    for name, factor in factors.items():
        out[name] = (out[name] * factor).astype(out[name].dtype)
    return out
```

```python
from contextlib import ExitStack

import numpy as np
import concourse.bass as bass
from concourse import mybir

F32 = mybir.dt.float32
BF16 = mybir.dt.bfloat16
I32 = mybir.dt.int32
ALU = mybir.AluOpType
ACT = mybir.ActivationFunctionType
AX = mybir.AxisListType
ds = bass.ds

B, CH, H, W = 8, 64, 32, 32
HALVES = 2
NB = B // HALVES
PX = H * W
HP, WP = H + 2, W + 2
TAPS = 9
BANK = 512
NBANK = NB * PX // BANK
HW2 = H // 2
NTOK = HW2 * HW2
HEADS, HD = 8, 8
TOPK = NTOK // 2
ROUNDS = 3
AIM = TOPK - 4 * ROUNDS
STEP = 0.0085
TAKEN = -1.0e30
MAGIC = 12582912.0
DG = 2
CG = CH // DG
TP = H + 2
NENT = TP * TP
TILES = NB * PX // 128
GK = DG * TAPS
CHUNK = 2

NJ, NI = 4, 16


def constants():
    p = np.arange(128)
    half, ch = p // CH, p % CH
    pj, ph, pi = p // 32, (p % 32) // NI, p % NI
    pch = NI * pj + pi
    c = {}
    c["ident"] = np.eye(128)
    c["mean8"] = (p[:, None] // 8 == p[None] // 8) / 8.0
    c["mean4"] = (p[:, None] // 4 == p[None] // 4) / 4.0
    c["sum8"] = (p[:, None] // 8 == p[None] // 8) * 1.0
    c["mean_pair"] = (pch[:, None] == pch[None]) / 2.0
    c["half_nat"] = (half[:, None] == np.arange(2)[None]) * 1.0
    c["half_perm"] = (ph[:, None] == np.arange(2)[None]) * 1.0
    c["head"] = (p[:, None] // HD == np.arange(HALVES * HEADS)[None]) * 1.0
    slot = np.arange(32)
    one = [((slot[None] == NI * half[:, None] + i) * -2.0) for i in range(NI)]
    c["slots"] = np.tile(np.arange(8 * ROUNDS), 4)[None].repeat(128, 0)
    c["adder_out"] = np.concatenate(one, 1)
    c["adder_x"] = (half[:, None] == ph[None]) * 1.0
    c["to_nat"] = ((pch[:, None] == ch[None]) & (ph[:, None] == half[None])) * 1.0
    t = np.arange(TILES)
    y = 4 * (t[None] % 8) + p[:, None] // 32
    x = np.broadcast_to(p[:, None] % 32, y.shape)
    k = np.arange(TAPS)
    gy = y[:, :, None, None, None] + (k // 3 - 1)
    gx = x[:, :, None, None, None] + (k % 3 - 1)
    q = (2 * (t // 8)[:, None] + np.arange(2)[None])[:, :, None] * DG + np.arange(DG)
    full = (128, TILES, HALVES, DG, TAPS)
    c["grid_y"] = np.broadcast_to(gy, full).reshape(128, -1)
    c["grid_x"] = np.broadcast_to(gx, full).reshape(128, -1)
    c["grid_base"] = np.broadcast_to((q * NENT + TP + 1)[None, :, :, :, None], full).reshape(128, -1)
    return {n: np.ascontiguousarray(a, dtype=np.float32) for n, a in c.items()}


SMALL = ["ident", "mean8", "mean4", "sum8", "mean_pair", "half_nat", "half_perm", "head", "slots", "adder_out", "adder_x",
         "to_nat"]
GRIDS = ["grid_y", "grid_x", "grid_base"]


def halves(ap):
    return ap.rearrange("(c one) -> c one", one=1)


class Stats:

    def __init__(self, sem, sb, name, m, ps):
        self.m, self.ps, self.n = m, ps, 0
        self.to_pe, self.from_pe = sem(name + "_to_pe"), sem(name + "_from_pe")
        self.to_act, self.from_act = sem(name + "_to_act"), sem(name + "_from_act")
        self.mv = sb(name + "_mv", [128, m, 2])
        self.mean, self.dev, self.var = (sb(name + x, [128, m]) for x in ("_mean", "_dev", "_var"))
        self.scale, self.bias = sb(name + "_scale", [128, m]), sb(name + "_bias", [128, m])
        self.eps = None

    def dve(self, v, m, gamma, beta, eps, n=0):
        mean, dev, var, scale, bias = (t[:, 0:m] for t in (self.mean, self.dev, self.var, self.scale, self.bias))
        v.drain().then_inc(self.to_pe, 1)
        v.wait_ge(self.from_pe, 2 * n + 1)
        v.tensor_copy(mean, self.ps[:, 0:m])
        v.drain()
        v.tensor_tensor(dev, self.mv[:, 0:m, 0], mean, ALU.subtract)
        v.drain()
        v.tensor_tensor(dev, dev, dev, ALU.mult)
        v.drain()
        v.tensor_tensor(var, self.mv[:, 0:m, 1], dev, ALU.add)
        v.drain().then_inc(self.to_pe, 1)
        v.wait_ge(self.from_pe, 2 * n + 2)
        v.tensor_scalar(dev, self.ps[:, 64:64 + m], eps, None, ALU.add)
        v.drain().then_inc(self.to_act, 1)
        v.wait_ge(self.from_act, n + 1)
        v.reciprocal(scale, var)
        v.drain()
        v.tensor_tensor(scale, scale, gamma, ALU.mult)
        v.drain()
        v.tensor_tensor(dev, mean, scale, ALU.mult)
        v.drain()
        v.tensor_tensor(bias, beta, dev, ALU.subtract)
        v.drain()

    def pe(self, t, m, matrix, n=0):
        t.wait_ge(self.to_pe, 2 * n + 1)
        t.matmul(self.ps[:, 0:m], matrix, self.mv[:, 0:m, 0], start=True, stop=True).then_inc(self.from_pe, 1)
        t.wait_ge(self.to_pe, 2 * n + 2)
        t.matmul(self.ps[:, 64:64 + m], matrix, self.var[:, 0:m], start=True, stop=True).then_inc(self.from_pe, 1)

    def act(self, a, m, n=0):
        a.wait_ge(self.to_act, n + 1)
        a.activation(self.var[:, 0:m], self.dev[:, 0:m], ACT.Sqrt).then_inc(self.from_act, 1)


def program(nc, A, C, out, stop_after=99):
    table = nc.dram_tensor("neighbours", [B * DG * NENT, 4 * CG], F32).ap()
    outer = ExitStack()
    with outer:
        def osb(n, s, d=F32):
            return outer.enter_context(nc.sbuf_tensor(n, s, d))

        K = {n: osb("c_" + n, [128, C[n].shape[1]]) for n in SMALL}
        X = osb("X", [128, NB * PX])
        XP = osb("XP", [128, NB, HP, WP])
        PS = outer.enter_context(nc.psum_tensor("PS", [128, NBANK, BANK], F32))
        X4 = X[:, :].rearrange("p (b y x) -> p b y x", b=NB, y=H)
        XPin = XP[:, :, 1:H + 1, 1:W + 1]

        def px_bank(t, k):
            return t[:, k // 2, 16 * (k % 2):16 * (k % 2) + 16, :]

        def patch(t, k, tap):
            y = 16 * (k % 2) + tap // 3
            return t[:, k // 2, y:y + 16, tap % 3:tap % 3 + W]

        def bank(k):
            return PS[:, k, :]

        def bank2(k):
            return PS[:, k, :].rearrange("p (y x) -> p y x", x=W)

        phase_names = []

        def phase(fn):
            phase_names.append(fn.__name__)
            if len(phase_names) > stop_after:
                return
            with ExitStack() as st:
                def sb(n, s, d=F32):
                    return st.enter_context(nc.sbuf_tensor(f"{fn.__name__}_{n}", s, d))

                def sem(n):
                    return st.enter_context(nc.semaphore(f"{fn.__name__}_{n}"))
                fn(st, sb, sem)

        lay0 = ExitStack()
        outer.enter_context(lay0)
        LL = lay0.enter_context(nc.sbuf_tensor("LL", [128, NB * NTOK], F32))
        HI = lay0.enter_context(nc.sbuf_tensor("HI", [128, 3, NB, HW2 + 2, HW2 + 2], F32))
        W0 = lay0.enter_context(nc.sbuf_tensor("W0", [128, 17, 128], F32))
        V0 = lay0.enter_context(nc.sbuf_tensor("V0", [128, 24], F32))
        vec = {}
        for name, n in (("attn_gn_g", 1), ("attn_gn_b", 1), ("he_gn1_g", 3), ("he_gn1_b", 3), ("he_gn2_g", 3),
                        ("he_gn2_b", 3), ("ffn_gn1_g", 2), ("ffn_gn1_b", 2), ("ffn_gn2_g", 1), ("ffn_gn2_b", 1),
                        ("alpha", 1)):
            vec[name] = (sum(x[1] for x in vec.values()), n)
        HE = lay0.enter_context(nc.sbuf_tensor("HE", [128, 3, TAPS], F32))

        def v0(name, rep):
            o, n = vec[name]
            return V0[:, o:o + n].unsqueeze(2).broadcast_to([128, n, rep])

        V12t = lay0.enter_context(nc.sbuf_tensor("V12", [128, 4, 3, NB], F32))
        V12 = {n: V12t[:, i, :, :].rearrange("p s b -> p (s b)") for i, n in enumerate(("g", "b", "g2", "b2"))}
        VFt = lay0.enter_context(nc.sbuf_tensor("VF", [128, 2, 2, NB], F32))
        VF = {n: VFt[:, i, :, :].rearrange("p s b -> p (s b)") for i, n in enumerate("gb")}

        atn = ExitStack()
        outer.enter_context(atn)

        def asb(n, shape, d=F32):
            return atn.enter_context(nc.sbuf_tensor(n, shape, d))

        GROUPS = NB * HEADS
        qk_all = asb("qk", [128, 2, (NB + 1) * NTOK])
        VT = asb("VT", [128, NB * HALVES, HEADS, 2, HD])
        VTf = VT[:, :, :, :, :].rearrange("p a b c d -> p (a b c d)")
        O = asb("O", [128, 2, NB * HALVES * CH])
        START, SLOPE = asb("START", [128, 4 * GROUPS]), asb("SLOPE", [128, 4 * GROUPS])
        COUNT = asb("COUNT", [128, 4 * GROUPS])
        REDO = asb("REDO", [128, 1], I32)

        def attention(st, sb, sem):
            loads, ll_done, w_ps, w_sb = sem("loads"), sem("ll_done"), sem("w_ps"), sem("w_sb")
            raws = sem("raws")
            qk_ps, qk_sq, qk_ns, qk_nrm, qk_done = (sem(n) for n in ("qk_ps", "qk_sq", "qk_ns", "qk_nrm", "qk_done"))
            v_ps, v_done = sem("v_ps"), sem("v_done")
            kt_ps, kt_sb, cov_ps, cov_sb, cq_ps, cq_sb, row_ps, dev_in, dev_done = (
                sem(n) for n in ("kt_ps", "kt_sb", "cov_ps", "cov_sb", "cq_ps", "cq_sb", "row_ps", "dev_in",
                                 "dev_done"))
            rawq = sb("rawq", [64, 3, 2, 64])
            rawp = sb("rawp", [64, 2, 64])
            rawpw = sb("rawpw", [64, 3, 2, 3, 64])
            rawf1 = sb("rawf1", [64, 2, 2, 64])
            rawf2 = sb("rawf2", [64, 2, 2, 64])
            xh = sb("xh", [128, NB, H, W])
            su = [sb(f"su{i}", [128, NB, HW2, HW2]) for i in range(4)]
            qk = qk_all[:, :, 0:NB * NTOK]
            sq = sb("sq", [128, 2, NB * NTOK])
            KT = sb("KT", [128, NB, 2, 128])
            COV = sb("COV", [128, NB, 128])
            QCQ = sb("QCQ", [128, NB * NTOK])
            ksum = sb("ksum", [128, NB])
            KM = sb("KM", [128, NB, HALVES * HEADS])
            row_sq = sb("row_sq", [128, 4 * GROUPS])
            nload, nraw = [0], [0]
            rawx = sb("rawx", [64, 17, 128])

            with nc.Block() as blk:
                @blk.sync
                def _(sp):
                    def load(dst, src):
                        sp.dma_start(dst, src).then_inc(loads, 16)
                        nload[0] += 16
                    for h in range(HALVES):
                        load(X[64 * h:64 * h + 64, :].rearrange("c (b f) -> c b f", b=NB),
                             A["x"][NB * h:NB * h + NB].rearrange("b c y x -> c b (y x)"))
                    for n in SMALL:
                        load(K[n][:, :], C[n])
                    for h in range(HALVES):
                        rows = slice(64 * h, 64 * h + 64)
                        for name, (o, n) in vec.items():
                            if name == "alpha":
                                load(V0[rows, o:o + 1], A["L0_conv_alpha"].rearrange("(a b) -> a b", a=1)
                                     .broadcast_to([64, 1]))
                            else:
                                for i in range(n):
                                    load(V0[rows, o + i:o + i + 1], halves(A["L0_conv_" + name][64 * i:64 * i + 64]))
                        load(HE[rows, :, :], A["L0_conv_he_dw_w"].rearrange("(s c) one ky kx -> c s (one ky kx)", c=64))
                    sp.wait_ge(loads, nload[0])

                @blk.scalar
                def _(a):
                    def load(dst, src):
                        a.dma_start(dst, src).then_inc(raws, 16)
                        nraw[0] += 16
                    for d in range(2):
                        load(rawq[:, :, d, :], A["L0_conv_qkv_w"].rearrange("(s o) c -> o s c", o=64))
                        load(rawp[:, d, :], A["L0_conv_proj_w"])
                        for s in range(3):
                            load(rawpw[:, s, d, :, :], A["L0_conv_he_pw_w"][64 * s:64 * s + 64, :]
                                 .rearrange("o (i c) -> o i c", c=64))
                        load(rawf1[:, :, d, :], A["L0_conv_ffn_w1"].rearrange("(s o) c -> o s c", o=64))
                        load(rawf2[:, :, d, :], A["L0_conv_ffn_w2"].rearrange("o (s c) -> o s c", c=64))
                    a.wait_ge(qk_ns, 1)
                    a.activation(sq[:, :, :].rearrange("p a f -> p (a f)"),
                                 PS[:, 0:4, :].rearrange("p a f -> p (a f)"), ACT.Sqrt).then_inc(qk_nrm, 1)
                    a.wait_ge(kt_ps, 1)
                    a.activation(KT[:, :, :, :].rearrange("p b t c -> p (b t c)"),
                                 PS[:, 6:8, :].rearrange("p a f -> p (a f)"), ACT.Copy).then_inc(kt_sb, 1)
                    a.wait_ge(dev_in, 1)
                    a.activation(SLOPE[:, :], row_sq[:, :], ACT.Sqrt,
                                 scale=(STEP ** 2) / HD).then_inc(dev_done, 1)

                @blk.gpsimd
                def _(g):
                    g.memset(HI[:, :, :, :, :], 0.0)
                    g.memset(XP[:, :, :, :], 0.0)
                    g.drain().then_inc(ll_done, 1)

                @blk.tensor
                def _(t):
                    t.wait_ge(loads, nload[0])
                    t.wait_ge(raws, nraw[0])
                    t.wait_ge(w_sb, 1)
                    for s in range(17):
                        mm = t.matmul(PS[:, 5 + s // 8, 64 * (s % 8):64 * (s % 8) + 64], rawx[:, s, :],
                                      K["ident"][0:64, 0:64], start=True, stop=True)
                    mm.then_inc(w_ps, 1)
                    t.wait_ge(w_sb, 2)
                    t.wait_ge(ll_done, 2)
                    for s in range(2):
                        for k in range(2):
                            mm = t.matmul(PS[:, 2 * s + k, :], W0[:, s, :], LL[:, BANK * k:BANK * k + BANK],
                                          start=True, stop=True)
                    mm.then_inc(qk_ps, 1)
                    for b in range(NB):
                        for h in range(HALVES):
                            for mt in range(2):
                                o = (b * 2 + mt) * 64
                                mm = t.matmul(PS[:, 4 + h, o:o + 64],
                                              LL[64 * h:64 * h + 64, b * NTOK + 128 * mt:b * NTOK + 128 * mt + 128],
                                              W0[64 * h:64 * h + 64, 2, 64 * h:64 * h + 64], start=True, stop=True)
                    mm.then_inc(v_ps, 1)
                    t.wait_ge(qk_sq, 1)
                    for s in range(2):
                        for k in range(2):
                            mm = t.matmul(PS[:, 2 * s + k, :], K["sum8"][:, :],
                                          sq[:, s, BANK * k:BANK * k + BANK], start=True, stop=True)
                    mm.then_inc(qk_ns, 1)

                    t.wait_ge(qk_done, 1)
                    t.wait_ge(w_sb, 2)
                    for b in range(NB):
                        for mt in range(2):
                            c = (b * 2 + mt) * 128
                            mm = t.transpose(PS[:, 6 + c // BANK, c % BANK:c % BANK + 128],
                                             qk[:, 1, b * NTOK + mt * 128:b * NTOK + mt * 128 + 128], K["ident"][:, :])
                    mm.then_inc(kt_ps, 1)
                    t.wait_ge(kt_sb, 1)
                    for b in range(NB):
                        for mt in range(2):
                            mm = t.matmul(PS[:, 0, 128 * b:128 * b + 128], KT[:, b, mt, :], KT[:, b, mt, :],
                                          start=(mt == 0), stop=(mt == 1))
                    mm.then_inc(cov_ps, 1)
                    t.wait_ge(cov_sb, 1)
                    for b in range(NB):
                        mm = t.matmul(PS[:, 2 + b // 2, NTOK * (b % 2):NTOK * (b % 2) + NTOK], COV[:, b, :],
                                      qk[:, 0, b * NTOK:b * NTOK + NTOK], start=True, stop=True)
                    mm.then_inc(cq_ps, 1)
                    t.wait_ge(cq_sb, 1)
                    for b in range(NB):
                        for nt in range(2):
                            tok = slice(b * NTOK + 128 * nt, b * NTOK + 128 * nt + 128)
                            o = (b * 2 + nt) * 16
                            t.matmul(PS[:, 0, o:o + 16], qk[:, 0, tok], KM[:, b, :], start=True, stop=True)
                            mm = t.matmul(PS[:, 1, o:o + 16], QCQ[:, tok], K["head"][:, :], start=True, stop=True)
                    mm.then_inc(row_ps, 1)

                @blk.vector
                def _(v):
                    v.wait_ge(raws, nraw[0])
                    v.tensor_copy(rawx[:, 0:3, :].rearrange("o s (d c) -> o s d c", d=2), rawq[:, :, :, :])
                    v.tensor_copy(rawx[:, 3, :].rearrange("o (d c) -> o d c", d=2), rawp[:, :, :])
                    for so in range(3):
                        v.tensor_copy(rawx[:, 4 + 3 * so:7 + 3 * so, :].rearrange("o i (d c) -> o i d c", d=2),
                                      rawpw[:, so, :, :, :].rearrange("o d i c -> o i d c"))
                    v.tensor_copy(rawx[:, 13:15, :].rearrange("o s (d c) -> o s d c", d=2), rawf1[:, :, :, :])
                    v.tensor_copy(rawx[:, 15:17, :].rearrange("o s (d c) -> o s d c", d=2), rawf2[:, :, :, :])
                    v.drain().then_inc(w_sb, 1)
                    v.wait_ge(loads, nload[0])
                    v.tensor_scalar(xh[:, :, :, :].rearrange("p b y x -> p (b y x)"), X[:, :], 0.5, None, ALU.mult)
                    v.drain()
                    q00, q10 = xh[:, :, 0:H:2, 0:W:2], xh[:, :, 1:H:2, 0:W:2]
                    q01, q11 = xh[:, :, 0:H:2, 1:W:2], xh[:, :, 1:H:2, 1:W:2]
                    v.tensor_tensor(su[0][:, :, :, :], q00, q10, ALU.add)
                    v.tensor_tensor(su[1][:, :, :, :], q01, q11, ALU.add)
                    v.tensor_tensor(su[2][:, :, :, :], q10, q00, ALU.subtract)
                    v.tensor_tensor(su[3][:, :, :, :], q11, q01, ALU.subtract)
                    v.drain()
                    v.wait_ge(ll_done, 1)
                    inner = [HI[:, s, :, 1:HW2 + 1, 1:HW2 + 1] for s in range(3)]
                    v.tensor_tensor(LL[:, :].rearrange("p (b y x) -> p b y x", b=NB, y=HW2), su[0][:, :, :, :],
                                    su[1][:, :, :, :], ALU.add)
                    v.tensor_tensor(inner[0], su[1][:, :, :, :], su[0][:, :, :, :], ALU.subtract)
                    v.tensor_tensor(inner[1], su[2][:, :, :, :], su[3][:, :, :, :], ALU.add)
                    v.tensor_tensor(inner[2], su[3][:, :, :, :], su[2][:, :, :, :], ALU.subtract)
                    v.drain().then_inc(ll_done, 1)
                    for i, n in enumerate(("he_gn1_g", "he_gn1_b", "he_gn2_g", "he_gn2_b")):
                        v.tensor_copy(V12t[:, i, :, :], v0(n, NB))
                    for i, n in enumerate(("ffn_gn1_g", "ffn_gn1_b")):
                        v.tensor_copy(VFt[:, i, :, :], v0(n, NB))
                    v.wait_ge(w_ps, 1)
                    for h in range(HALVES):
                        for c in range(3):
                            n = min(8, 17 - 8 * c)
                            v.tensor_scalar(W0[:, 8 * c:8 * c + n, 64 * h:64 * h + 64],
                                            PS[:, 5 + c, 0:64 * n].rearrange("p (s o) -> p s o", o=64),
                                            K["half_nat"][:, h:h + 1], None, ALU.mult)
                    v.drain().then_inc(w_sb, 1)
                    v.wait_ge(qk_ps, 1)
                    v.tensor_copy(qk, PS[:, 0:4, :].rearrange("p (a k) f -> p a (k f)", k=2))
                    v.drain()
                    v.tensor_tensor(sq[:, :, :], qk[:, :, :], qk[:, :, :], ALU.mult)
                    v.drain().then_inc(qk_sq, 1)
                    v.wait_ge(v_ps, 1)
                    for h in range(HALVES):
                        for mt in range(2):
                            v.tensor_copy(VT[:, h:NB * HALVES:2, :, mt, :],
                                          PS[:, 4 + h, :].rearrange("p (n m e d) -> p n m e d", n=4, m=2, d=HD)[:, :, mt])
                    v.drain().then_inc(v_done, 1)
                    v.wait_ge(qk_nrm, 1)
                    v.tensor_scalar(sq[:, :, :], sq[:, :, :], 1e-12, None, ALU.max)
                    v.drain()
                    v.reciprocal(sq[:, :, :], sq[:, :, :])
                    v.drain()
                    v.tensor_tensor(qk[:, :, :], qk[:, :, :], sq[:, :, :], ALU.mult)
                    v.drain().then_inc(qk_done, 1)

                    for b in range(NB):
                        v.tensor_reduce(ksum[:, b:b + 1], qk[:, 1, b * NTOK:b * NTOK + NTOK], AX.X, ALU.add)
                    v.drain()
                    v.tensor_scalar(ksum[:, :], ksum[:, :], 1.0 / NTOK, None, ALU.mult)
                    v.drain()
                    for b in range(NB):
                        v.tensor_scalar(KM[:, b, :], K["head"][:, :], ksum[:, b:b + 1], None, ALU.mult)
                    v.wait_ge(cov_ps, 1)
                    v.scalar_tensor_tensor(out=COV[:, :, :], in0=PS[:, 0, :].rearrange("p (b c) -> p b c", b=NB),
                                           scalar=1.0 / NTOK,
                                           in1=K["sum8"][:, :].unsqueeze(1).broadcast_to([128, NB, 128]),
                                           op0=ALU.mult, op1=ALU.mult)
                    v.drain().then_inc(cov_sb, 1)
                    v.wait_ge(cq_ps, 1)
                    v.tensor_tensor(QCQ[:, :], qk[:, 0, :], PS[:, 2:4, :].rearrange("p a f -> p (a f)"), ALU.mult)
                    v.drain().then_inc(cq_sb, 1)
                    v.wait_ge(row_ps, 1)

                    def by_group(t, b):
                        return t[:, 32 * b:32 * b + 32].rearrange("p (h n) -> p h n", n=2)

                    def by_tile(k, b):
                        return PS[:, k, 32 * b:32 * b + 32].rearrange("p (n h) -> p h n", n=2)
                    for b in range(NB):
                        v.tensor_copy(by_group(START, b), by_tile(0, b))
                        v.tensor_copy(by_group(row_sq, b), by_tile(1, b))
                    v.drain()
                    v.tensor_tensor(COUNT[:, :], START[:, :], START[:, :], ALU.mult)
                    v.drain()
                    v.tensor_tensor(row_sq[:, :], row_sq[:, :], COUNT[:, :], ALU.subtract)
                    v.drain()
                    v.tensor_scalar(row_sq[:, :], row_sq[:, :], 0.0, None, ALU.max)
                    v.tensor_scalar(START[:, :], START[:, :], float(HD) ** -0.5, None, ALU.mult)
                    v.drain().then_inc(dev_in, 1)
                    v.wait_ge(dev_done, 1)
                    v.scalar_tensor_tensor(out=START[:, :], in0=SLOPE[:, :], scalar=float(TOPK - AIM),
                                           in1=START[:, :], op0=ALU.mult, op1=ALU.add)
                    v.drain()

        phase(attention)

        def attend(st, sb, sem, exact):
            staged, s_ps, s_sb, s_used, e_done, p_done, pt_ps, pt_sb, o_ps, o_done, redo_in, redo_ps = (
                sem(n) for n in ("staged", "s_ps", "s_sb", "s_used", "e_done", "p_done", "pt_ps", "pt_sb", "o_ps",
                                 "o_done", "redo_in", "redo_ps"))
            stage = sb("stage", [128, 2, 2, 128])
            S = sb("S", [128, 4, NTOK])
            WK = sb("WK", [128, 4, NTOK])
            E = sb("E", [128, 4, NTOK])
            P = sb("P", [128, 4, NTOK])
            PT = sb("PT", [128, 4, NTOK])
            IND = sb("IND", [128, 4, NTOK])
            signs = sb("signs", [128, 4, NTOK])
            above = sb("above", [128, 4])
            thr, neg = sb("thr", [128, 4]), sb("neg", [128, 4])
            cnt, need = sb("cnt", [128, 4]), sb("need", [128, 4])
            spare = sb("spare", [128, 4, 8 * ROUNDS])
            top = sb("top", [128, 4, 8])
            mark = sb("mark", [128, 1])
            rs = sb("rs", [128, 4])
            ri = sb("ri", [128, 4])
            missed = sb("missed", [128, 4 * GROUPS])
            n_missed = sb("n_missed", [128, 1])
            ones = sb("ones", [128, 128])

            def flat(t):
                return t[:, :, :].rearrange("p u n -> p (u n)")

            with nc.Block() as blk:
                if exact:
                    @blk.sync
                    def _(sp):
                        sp.drain()

                    @blk.gpsimd
                    def _(g):
                        g.drain()

                @blk.scalar
                def _(a):
                    def queries(g):
                        for par in range(2):
                            b, hh = (g >> 3), (g & 7)
                            a.activation(stage[:, par, :, :], qk_all[:, 0, ds(b * NTOK, NTOK)]
                                         .rearrange("p (t n) -> p t n", t=2), ACT.Copy,
                                         scale=K["head"][:, ds(hh * 2 + par, 1)])
                        a.drain().then_inc(staged, 1)
                        a.wait_ge(s_ps, g + 1)
                        a.activation(flat(S), PS[:, 0:2, :].rearrange("p a f -> p (a f)"), ACT.Copy,
                                     scale=float(HD) ** -0.5)
                        if not exact:
                            a.activation(neg[:, :], START[:, ds(g * 4, 4)], ACT.Copy, scale=-1.0)
                            a.drain()
                            for u in range(4):
                                a.activation(signs[:, u, :], S[:, u, :], ACT.Sign, bias=neg[:, u:u + 1],
                                             accum_out=above[:, u:u + 1])
                        a.drain().then_inc(s_sb, 1)

                    def probs(g, more):
                        a.wait_ge(p_done, g + 1)
                        a.activation(flat(E), flat(S), ACT.Exp)
                        a.drain().then_inc(e_done, 1)
                        a.wait_ge(s_used, g + 1)
                        if more:
                            queries(g + 1)
                        a.wait_ge(pt_ps, g + 2)
                        a.activation(flat(PT), PS[:, 2:4, :].rearrange("p a f -> p (a f)"), ACT.Copy).then_inc(pt_sb, 1)
                        a.wait_ge(o_ps, g + 1)
                        for par in range(2):
                            for nt in range(2):
                                u = 2 * par + nt
                                a.activation(O[:, nt, ds(g * 16 + par * HD, HD)], PS[:, 4, 64 * u:64 * u + HD],
                                             ACT.Copy, scale=ri[:, u:u + 1])
                        a.drain().then_inc(o_done, 1)

                    queries(0)
                    with a.Fori(0, GROUPS - 1, 1) as g:
                        probs(g, True)
                    probs(GROUPS - 1, False)

                @blk.tensor
                def _(t):
                    t.sem_inc(pt_ps, 1)
                    t.sem_inc(o_done, 1)
                    t.sem_inc(p_done, 1)

                    def scores(g):
                        t.wait_ge(staged, g + 1)
                        for par in range(2):
                            for nt in range(2):
                                mm = t.matmul(PS[:, par, NTOK * nt:NTOK * nt + NTOK], stage[:, par, nt, :],
                                              qk_all[:, 1, ds((g >> 3) * NTOK, NTOK)], start=True, stop=True)
                        mm.then_inc(s_ps, 1)

                    def values(g):
                        t.wait_ge(p_done, g + 2)
                        for u in range(4):
                            for mt in range(2):
                                c = 256 * (u % 2) + 128 * mt
                                mm = t.transpose(PS[:, 2 + u // 2, c:c + 128], P[:, u, 128 * mt:128 * mt + 128],
                                                 K["ident"][:, :])
                        mm.then_inc(pt_ps, 1)
                        t.wait_ge(pt_sb, g + 1)
                        for par in range(2):
                            for nt in range(2):
                                u = 2 * par + nt
                                for mt in range(2):
                                    mm = t.matmul(PS[:, 4, 64 * u:64 * u + HD], PT[:, u, 128 * mt:128 * mt + 128],
                                                  VTf[:, ds(g * 32 + par * 16 + mt * HD, HD)],
                                                  start=(mt == 0), stop=(mt == 1))
                        mm.then_inc(o_ps, 1)

                    scores(0)
                    with t.Fori(0, GROUPS - 1, 1) as g:
                        t.wait_ge(s_sb, g + 1)
                        scores(g + 1)
                        values(g)
                    values(GROUPS - 1)
                    if not exact:
                        t.wait_ge(redo_in, 1)
                        t.matmul(PS[:, 5, 0:1], ones[:, :], n_missed[:, :], start=True, stop=True).then_inc(redo_ps, 1)

                @blk.vector
                def _(v):
                    def take_all(g):
                        for u in range(4):
                            v.max(top[:, u, :], S[:, u, :])
                        v.drain()
                        for r in range(TOPK // 8):
                            if r:
                                for u in range(4):
                                    v.max(top[:, u, :], WK[:, u, :])
                                v.drain()
                            for u in range(4):
                                v.match_replace(out=WK[:, u, :], in_to_replace=top[:, u, :],
                                                in_values=(WK if r else S)[:, u, :], imm_value=TAKEN)
                            if r == 0:
                                v.drain().then_inc(s_used, 1)
                            else:
                                v.drain()

                    def take_above(g):
                        v.tensor_scalar(cnt[:, :], above[:, :], 0.5, float(NTOK // 2 - AIM), ALU.mult, ALU.add)
                        v.drain()
                        v.tensor_tensor(cnt[:, :], cnt[:, :], SLOPE[:, ds(g * 4, 4)], ALU.mult)
                        v.drain()
                        v.tensor_tensor(thr[:, :], START[:, ds(g * 4, 4)], cnt[:, :], ALU.add)
                        v.drain()
                        for u in range(4):
                            v.tensor_scalar(IND[:, u, :], S[:, u, :], thr[:, u:u + 1], 0.0, ALU.is_ge, ALU.add,
                                            accum_out=cnt[:, u:u + 1])
                        v.drain()
                        v.tensor_scalar(need[:, :], cnt[:, :], -1.0, float(TOPK), ALU.mult, ALU.add)
                        v.tensor_copy(COUNT[:, ds(g * 4, 4)], cnt[:, :])
                        v.scalar_tensor_tensor(out=flat(WK), in0=flat(IND), scalar=TAKEN, in1=flat(S),
                                               op0=ALU.mult, op1=ALU.add)
                        v.drain().then_inc(s_used, 1)
                        for u in range(4):
                            v.max(top[:, u, :], WK[:, u, :])
                        v.tensor_tensor(spare[:, :, :], K["slots"][:, :].rearrange("p (u s) -> p u s", u=4),
                                        need[:, :].unsqueeze(2).broadcast_to([128, 4, 8 * ROUNDS]), ALU.is_ge)
                        v.drain()
                        for r in range(ROUNDS):
                            if r:
                                for u in range(4):
                                    v.max(top[:, u, :], WK[:, u, :])
                                v.drain()
                            v.scalar_tensor_tensor(out=top[:, :, :], in0=spare[:, :, 8 * r:8 * r + 8], scalar=TAKEN,
                                                   in1=top[:, :, :], op0=ALU.mult, op1=ALU.add)
                            v.drain()
                            for u in range(4):
                                v.match_replace(out=WK[:, u, :], in_to_replace=top[:, u, :],
                                                in_values=WK[:, u, :], imm_value=TAKEN)
                            v.drain()

                    def select(g):
                        v.wait_ge(s_sb, g + 1)
                        v.memset(mark[:, :], 0.0)
                        (take_all if exact else take_above)(g)
                        v.wait_ge(e_done, g + 1)
                        v.wait_ge(pt_ps, g + 1)
                        for u in range(4):
                            v.scalar_tensor_tensor(out=P[:, u, :], in0=WK[:, u, :], scalar=TAKEN / 2,
                                                   in1=E[:, u, :], op0=ALU.is_lt, op1=ALU.mult,
                                                   accum_out=rs[:, u:u + 1])
                        v.drain()
                        v.wait_ge(o_done, g + 1)
                        v.reciprocal(ri[:, :], rs[:, :])
                        v.drain().then_inc(p_done, 1)

                    with v.Fori(0, GROUPS, 1) as g:
                        select(g)
                    if not exact:
                        v.memset(ones[:, :], 1.0)
                        v.tensor_scalar(missed[:, :], COUNT[:, :], float(TOPK), None, ALU.is_gt)
                        v.tensor_scalar(COUNT[:, :], COUNT[:, :], float(TOPK - 8 * ROUNDS), None, ALU.is_lt)
                        v.drain()
                        v.tensor_tensor(missed[:, :], missed[:, :], COUNT[:, :], ALU.add)
                        v.drain()
                        v.tensor_reduce(n_missed[:, :], missed[:, :], AX.X, ALU.add)
                        v.drain().then_inc(redo_in, 1)
                        v.wait_ge(redo_ps, 1)
                        v.tensor_scalar(REDO[:, :], PS[:, 5, 0:1], 1.0, None, ALU.min)
                        v.drain()

        def top_k(st, sb, sem):
            attend(st, sb, sem, exact=False)

        phase(top_k)

        def top_k_exact(st, sb, sem):
            attend(st, sb, sem, exact=True)

        redo = nc.values_load(REDO[0:1, 0:1], min_val=0, max_val=1,
                              skip_runtime_bounds_check_because="the chip computes it as min(count, 1)")
        with nc.If(redo):
            phase(top_k_exact)

        def projection(st, sb, sem):
            at_ps, at_sb, pr_ps = sem("at_ps"), sem("at_sb"), sem("pr_ps")
            AO = sb("AO", [128, NB * NTOK])
            Y = sb("Y", [128, NB, NTOK])
            gn = Stats(sem, sb, "gn", NB, PS[:, 7, :])
            st6 = sb("st6", [128, NB, 6])
            with nc.Block() as blk:
                @blk.scalar
                def _(a):
                    a.wait_ge(at_ps, 1)
                    a.activation(AO[:, :], PS[:, 0:2, :].rearrange("p a f -> p (a f)"), ACT.Copy).then_inc(at_sb, 1)
                    gn.act(a, NB)

                @blk.tensor
                def _(t):
                    for b in range(NB):
                        for nt in range(2):
                            c = b * NTOK + nt * 128
                            mm = t.transpose(PS[:, c // BANK, c % BANK:c % BANK + 128],
                                             O[:, nt, b * 128:b * 128 + 128], K["ident"][:, :])
                    mm.then_inc(at_ps, 1)
                    t.wait_ge(at_sb, 1)
                    for k in range(2):
                        mm = t.matmul(PS[:, 2 + k, :], W0[:, 3, :], AO[:, BANK * k:BANK * k + BANK],
                                      start=True, stop=True)
                    mm.then_inc(pr_ps, 1)
                    gn.pe(t, NB, K["mean4"][:, :])

                @blk.vector
                def _(v):
                    v.wait_ge(pr_ps, 1)
                    v.tensor_copy(Y[:, :, :].rearrange("p b f -> p (b f)"),
                                  PS[:, 2:4, :].rearrange("p a f -> p (a f)"))
                    v.drain()
                    for b in range(NB):
                        v.bn_stats(st6[:, b, :], Y[:, b, :])
                    v.drain()
                    for b in range(NB):
                        v.bn_aggr(gn.mv[:, b, :], st6[:, b, :])
                    gn.dve(v, NB, v0("attn_gn_g", NB)[:, 0, :], v0("attn_gn_b", NB)[:, 0, :], 1e-6)
                    for b in range(NB):
                        v.tensor_scalar(Y[:, b, :], Y[:, b, :], gn.scale[:, b:b + 1], gn.bias[:, b:b + 1],
                                        ALU.mult, ALU.add)
                    v.drain()
                    v.tensor_tensor(LL[:, :], LL[:, :], Y[:, :, :].rearrange("p b f -> p (b f)"), ALU.add)
                    v.drain()

        phase(projection)
        atn.close()


        def high_bands(st, sb, sem):
            dw = sb("dw", [128, 3, NB, HW2, HW2])
            dwf = dw[:, :, :, :, :].rearrange("p s b y x -> p s b (y x)")
            act = sb("act", [128, 3, NB, NTOK])
            y2 = sb("y2", [128, 3, NB, NTOK])
            st6 = sb("st6", [128, 12, 6])
            gn = Stats(sem, sb, "gn", 12, PS[:, 7, :])
            silu_in, silu_done, pw_ps = sem("silu_in"), sem("silu_done"), sem("pw_ps")

            def stats(v, t):
                for m in range(12):
                    v.bn_stats(st6[:, m, :], t[:, m // NB, m % NB, :])
                v.drain()
                for m in range(12):
                    v.bn_aggr(gn.mv[:, m, :], st6[:, m, :])

            with nc.Block() as blk:
                @blk.vector
                def _(v):
                    for tap in range(TAPS):
                        for s in range(3):
                            seen = HI[:, s, :, tap // 3:tap // 3 + HW2, tap % 3:tap % 3 + HW2]
                            if tap == 0:
                                v.tensor_scalar(dw[:, s], seen, HE[:, s, tap:tap + 1], None, ALU.mult)
                            else:
                                for b in range(NB):
                                    v.scalar_tensor_tensor(out=dw[:, s, b], in0=seen[:, b],
                                                           scalar=HE[:, s, tap:tap + 1], in1=dw[:, s, b],
                                                           op0=ALU.mult, op1=ALU.add)
                        v.drain()
                    stats(v, dwf)
                    gn.dve(v, 12, V12["g"], V12["b"], 1e-6)
                    v.drain().then_inc(silu_in, 1)
                    v.wait_ge(pw_ps, 1)
                    v.tensor_copy(y2[:, :, :, :].rearrange("p s b f -> p (s b f)"),
                                  PS[:, 0:6, :].rearrange("p a f -> p (a f)"))
                    v.drain()
                    stats(v, y2)
                    gn.dve(v, 12, V12["g2"], V12["b2"], 1e-6, n=1)
                    al = V0[:, vec["alpha"][0]:vec["alpha"][0] + 1]
                    v.tensor_scalar(gn.scale[:, :], gn.scale[:, :], al, None, ALU.mult)
                    v.tensor_scalar(gn.bias[:, :], gn.bias[:, :], al, None, ALU.mult)
                    v.drain()
                    for m in range(12):
                        t = y2[:, m // NB, m % NB, :]
                        v.tensor_scalar(t, t, gn.scale[:, m:m + 1], gn.bias[:, m:m + 1], ALU.mult, ALU.add)
                    v.drain()
                    y5 = y2[:, :, :, :].rearrange("p s b (y x) -> p s b y x", y=HW2)
                    for s in range(3):
                        v.tensor_tensor(y5[:, s], y5[:, s], HI[:, s, :, 1:HW2 + 1, 1:HW2 + 1], ALU.add)
                    v.drain()
                    ll = LL[:, :].rearrange("p (b f) -> p b f", b=NB)
                    lh, hl, hh = (y2[:, s] for s in range(3))
                    t0, t1, t2, t3 = act[:, 0], act[:, 1], act[:, 2], dwf[:, 0]
                    v.tensor_tensor(t0, ll, lh, ALU.subtract)
                    v.tensor_tensor(t1, hl, hh, ALU.subtract)
                    v.tensor_tensor(t2, ll, lh, ALU.add)
                    v.tensor_tensor(t3, hl, hh, ALU.add)
                    v.drain()
                    r = dwf[:, 1]
                    r4 = dw[:, 1]
                    for dy, dx, p, q, op in ((0, 0, t0, t1, ALU.subtract), (1, 0, t0, t1, ALU.add),
                                             (0, 1, t2, t3, ALU.subtract), (1, 1, t2, t3, ALU.add)):
                        v.tensor_tensor(r, p, q, op)
                        v.drain()
                        for b in range(NB):
                            at = X4[:, b, dy:H:2, dx:W:2]
                            v.scalar_tensor_tensor(out=at, in0=r4[:, b], scalar=0.1, in1=at, op0=ALU.mult,
                                                   op1=ALU.add)
                        v.drain()

                @blk.scalar
                def _(a):
                    gn.act(a, 12)
                    a.wait_ge(silu_in, 1)
                    for m in range(12):
                        a.activation(act[:, m // NB, m % NB, :], dwf[:, m // NB, m % NB, :], ACT.Silu,
                                     scale=gn.scale[:, m:m + 1], bias=gn.bias[:, m:m + 1])
                    a.drain().then_inc(silu_done, 1)
                    gn.act(a, 12, n=1)

                @blk.tensor
                def _(t):
                    gn.pe(t, 12, K["mean8"][:, :])
                    t.wait_ge(silu_done, 1)
                    flat = act[:, :, :, :].rearrange("p s b f -> p s (b f)")
                    for so in range(3):
                        for k in range(2):
                            for si in range(3):
                                mm = t.matmul(PS[:, 2 * so + k, :], W0[:, 4 + 3 * so + si, :],
                                              flat[:, si, BANK * k:BANK * k + BANK], start=(si == 0), stop=(si == 2))
                    mm.then_inc(pw_ps, 1)
                    gn.pe(t, 12, K["mean8"][:, :], n=1)

        phase(high_bands)

        def feed_forward(st, sb, sem):
            f1 = sb("f1", [128, 2, NB * PX])
            f2 = sb("f2", [128, NB * PX])
            st6 = sb("st6", [128, 16, 6])
            gn = Stats(sem, sb, "gn", 8, PS[:, 7, :])
            f_ps, f_sb, gelu_in, gelu_done, r_ps, r_sb = (sem(n) for n in ("f_ps", "f_sb", "gelu_in", "gelu_done",
                                                                          "r_ps", "r_sb"))
            with nc.Block() as blk:
                @blk.tensor
                def _(t):
                    for u in range(16):
                        if u >= 7:
                            t.wait_ge(f_sb, u - 6)
                        t.matmul(PS[:, u % 7, :], W0[:, 13 + u // 8, :], X[:, BANK * (u % 8):BANK * (u % 8) + BANK],
                                 start=True, stop=True).then_inc(f_ps, 1)
                    gn.pe(t, 8, K["mean8"][:, :])
                    t.wait_ge(f_sb, 16)
                    for k in range(NBANK):
                        t.wait_ge(gelu_done, k // 2 + 1)
                        if k >= 7:
                            t.wait_ge(r_sb, k - 6)
                        for e in range(2):
                            mm = t.matmul(PS[:, k % 7, :], W0[:, 15 + e, :], f1[:, e, BANK * k:BANK * k + BANK],
                                          start=(e == 0), stop=(e == 1))
                        mm.then_inc(r_ps, 1)
                    gn.pe(t, 4, K["mean4"][:, :], n=1)

                @blk.scalar
                def _(a):
                    for u in range(16):
                        a.wait_ge(f_ps, u + 1)
                        a.activation(f1[:, u // 8, BANK * (u % 8):BANK * (u % 8) + BANK], PS[:, u % 7, :],
                                     ACT.Copy).then_inc(f_sb, 1)
                    gn.act(a, 8)
                    a.wait_ge(gelu_in, 1)
                    for b in range(NB):
                        for e in range(2):
                            m = e * NB + b
                            t = f1[:, e, PX * b:PX * b + PX]
                            a.activation(t, t, ACT.Gelu, scale=gn.scale[:, m:m + 1], bias=gn.bias[:, m:m + 1])
                        a.drain().then_inc(gelu_done, 1)
                    for k in range(NBANK):
                        a.wait_ge(r_ps, k + 1)
                        a.activation(f2[:, BANK * k:BANK * k + BANK], PS[:, k % 7, :], ACT.Copy).then_inc(r_sb, 1)
                    gn.act(a, 4, n=1)

                @blk.vector
                def _(v):
                    for u in range(16):
                        v.wait_ge(f_sb, u + 1)
                        v.bn_stats(st6[:, u, :], f1[:, u // 8, BANK * (u % 8):BANK * (u % 8) + BANK])
                    v.drain()
                    for m in range(8):
                        v.bn_aggr(gn.mv[:, m, :], st6[:, 2 * m:2 * m + 2, :].rearrange("p a b -> p (a b)"))
                    gn.dve(v, 8, VF["g"], VF["b"], 1e-6)
                    v.drain().then_inc(gelu_in, 1)
                    for k in range(NBANK):
                        v.wait_ge(r_sb, k + 1)
                        v.bn_stats(st6[:, k, :], f2[:, BANK * k:BANK * k + BANK])
                    v.drain()
                    for m in range(4):
                        v.bn_aggr(gn.mv[:, m, :], st6[:, 2 * m:2 * m + 2, :].rearrange("p a b -> p (a b)"))
                    gn.dve(v, 4, v0("ffn_gn2_g", NB)[:, 0, :], v0("ffn_gn2_b", NB)[:, 0, :], 1e-6, n=1)
                    for b in range(NB):
                        t = f2[:, PX * b:PX * b + PX]
                        v.tensor_scalar(t, t, gn.scale[:, b:b + 1], gn.bias[:, b:b + 1], ALU.mult, ALU.add)
                    v.drain()
                    v.scalar_tensor_tensor(out=X[:, :], in0=f2[:, :], scalar=0.1, in1=X[:, :], op0=ALU.mult,
                                           op1=ALU.add)
                    v.drain()
                    v.tensor_copy(XPin, X4)
                    v.drain()

        phase(feed_forward)
        lay0.close()


        lay1 = ExitStack()
        outer.enter_context(lay1)

        def l1(n, s):
            return lay1.enter_context(nc.sbuf_tensor(n, s, F32))

        WC = [l1(f"WC{i}", [128, TAPS, 128]) for i in range(2)]
        AW = [l1(f"AW{i}", [128, TAPS, CH]) for i in range(2)]
        AN = [l1(f"AN{i}", [128, TAPS, CH]) for i in range(2)]
        WSUM = [l1(f"WSUM{i}", [128, 128]) for i in range(2)]
        BNV = l1("BNV", [128, 4])
        P2 = l1("P2", [128, NB, HP, WP])

        def block_weights(v, dst, ps9, masks, cols=CH):
            for h in range(HALVES):
                v.tensor_scalar(dst[:, :, 64 * h:64 * h + cols], ps9, K[masks][:, h:h + 1], None, ALU.mult)

        def adder_weights(st, sb, sem):
            loads, w_ps, w_sb, border = sem("loads"), sem("w_ps"), sem("w_sb"), sem("border")
            names = ["conv1_w", "add1_w", "conv2_w", "add2_w"]
            raw = [sb(f"raw{q}", [64, 128, TAPS]) for q in range(4)]
            total = sb("total", [128, CH])
            nload = [0]
            with nc.Block() as blk:
                @blk.sync
                def _(sp):
                    def load(dst, src):
                        sp.dma_start(dst, src).then_inc(loads, 16)
                        nload[0] += 16
                    for q, n in enumerate(names):
                        w = A["L1_conv_" + n].rearrange("o c ky kx -> o c (ky kx)")
                        for h in range(HALVES):
                            if q == 2:
                                load(raw[q][:, :, :].rearrange("o (j h i) t -> o j h (i t)", j=NJ, h=2)[:, :, h],
                                     w.rearrange("o (j i) t -> o j (i t)", i=NI))
                            else:
                                load(raw[q][:, 64 * h:64 * h + 64, :], w)
                    for i, n in enumerate(("bn1_g", "bn1_b", "bn2_g", "bn2_b")):
                        for j in range(NJ):
                            for h in range(HALVES):
                                r = 32 * j + NI * h
                                load(BNV[r:r + NI, i:i + 1], halves(A["L1_conv_" + n][NI * j:NI * j + NI]))
                    sp.wait_ge(loads, nload[0])

                @blk.gpsimd
                def _(g):
                    g.memset(P2[:, :, :, :], 0.0)
                    g.drain()

                @blk.tensor
                def _(t):
                    t.wait_ge(loads, nload[0])
                    for q in range(4):
                        for tap in range(TAPS):
                            mm = t.matmul(PS[:, 2 * q + tap // 8, 64 * (tap % 8):64 * (tap % 8) + 64],
                                          raw[q][:, :, tap], K["ident"][0:64, 0:64], start=True, stop=True)
                        mm.then_inc(w_ps, 1)

                @blk.vector
                def _(v):
                    for q in range(4):
                        ps9 = PS[:, 2 * q:2 * q + 2, :].rearrange("p a (t o) -> p (a t) o", o=CH)[:, 0:TAPS, :]
                        v.wait_ge(w_ps, q + 1)
                        i = q // 2
                        if q % 2 == 0:
                            block_weights(v, WC[i], ps9, "half_perm" if q else "half_nat")
                            continue
                        v.tensor_copy(AW[i][:, :, :], ps9)
                        v.tensor_scalar(AN[i][:, :, :], ps9, -1.0, None, ALU.mult)
                        v.drain()
                        v.tensor_reduce(total[:, :], AN[i][:, :, :].rearrange("p t o -> p o t"), AX.X, ALU.add)
                        v.drain()
                        for h in range(HALVES):
                            v.tensor_scalar(WSUM[i][:, :].rearrange("p (j h i) -> p j h i", j=NJ, h=2)[:, :, h],
                                            total[:, :].rearrange("p (j i) -> p j i", i=NI),
                                            K["half_nat"][:, h:h + 1], None, ALU.mult)
                    v.drain()

        phase(adder_weights)

        def adder_layer(layer, src):
            def run(st, sb, sem):
                CP = sb("CP", [128, NB, HP, WP])
                Z = sb("Z", [128, 2, NJ, CHUNK * PX])
                BOX = sb("BOX", [128, NB, H, W])
                SO_all = sb("SO", [128, NB * HP * W])
                rowsum = SO_all[:, :].rearrange("p (b y x) -> p b y x", b=NB, x=W)
                SO = SO_all[:, 0:NB * PX]
                st6 = sb("st6", [128, NBANK, 6])
                ones = sb("ones", [128, BANK])
                gn = Stats(sem, sb, "gn", 1, PS[:, 0, :])
                ready, c_ps, c_sb, box = sem("ready"), sem("c_ps"), sem("c_sb"), sem("box")
                z_dve, z_act = sem("z_dve"), sem("z_act")
                z_free = [sem("z_free0"), sem("z_free1")]
                s_ps, s_sb, normed, nat_ps, done = (sem(n) for n in ("s_ps", "s_sb", "normed", "nat_ps", "done"))
                CBANK = CHUNK * PX // BANK
                AWf = AW[layer][:, :, :].rearrange("p t o -> p (t o)")
                ANf = AN[layer][:, :, :].rearrange("p t o -> p (t o)")

                def by_dve(i):
                    return [0, 1] + [2] * (i % 4 == 3)

                def use(ch, ty, tx, i):
                    return (ty * 3 + tx) * (NI // 2) + (ch * TAPS * (NI // 2) + i // 2)

                def group(ch, ty, tx, i):
                    return (ty * 3 + tx) * NI + (ch * TAPS * NI + i)

                def seen(ch, ty, tx):
                    return CP[:, CHUNK * ch:CHUNK * ch + CHUNK, ds(ty, H), ds(tx, W)]

                def z(i, j):
                    return Z[:, i % 2, j, :].rearrange("p (b y x) -> p b y x", b=CHUNK, y=H)

                with nc.Block() as blk:
                    @blk.gpsimd
                    def _(g):
                        g.memset(CP[:, :, :, :], 0.0)
                        g.memset(ones[:, :], 1.0)
                        g.drain().then_inc(ready, 1)
                        g.wait_ge(c_sb, NBANK)
                        g.tensor_tensor(rowsum, CP[:, :, :, 0:W], CP[:, :, :, 1:W + 1], ALU.add).then_inc(box, 1)
                        g.wait_ge(box, 1)
                        g.tensor_tensor(rowsum, rowsum, CP[:, :, :, 2:W + 2], ALU.add).then_inc(box, 1)
                        g.wait_ge(box, 2)
                        g.tensor_tensor(BOX[:, :, :, :], rowsum[:, :, 0:H], rowsum[:, :, 1:H + 1], ALU.add)\
                         .then_inc(box, 1)
                        g.wait_ge(box, 3)
                        g.tensor_tensor(BOX[:, :, :, :], BOX[:, :, :, :], rowsum[:, :, 2:H + 2], ALU.add)\
                         .then_inc(box, 1)

                    @blk.tensor
                    def _(t):
                        t.sem_inc(z_free[0], 1)
                        t.sem_inc(z_free[1], 1)
                        for k in range(NBANK):
                            for tap in range(TAPS):
                                mm = t.matmul(bank(k), WC[layer][:, tap, :], patch(src, k, tap), start=(tap == 0),
                                              stop=(tap == TAPS - 1))
                            mm.then_inc(c_ps, 1)
                        t.wait_ge(ready, 1)
                        for ch in range(NB // CHUNK):
                            banks = range(CBANK * ch, CBANK * ch + CBANK)
                            t.wait_ge(c_sb, CBANK * ch + CBANK)
                            for k in banks:
                                t.matmul(bank(k), WSUM[layer][:, :], ones[:, :], start=True, stop=False,
                                         skip_group_check=True)
                            with t.Fori(0, 3, 1) as ty:
                                with t.Fori(0, 3, 1) as tx:
                                    for i in range(NI):
                                        t.wait_ge(z_dve, group(ch, ty, tx, i) + 1)
                                        t.wait_ge(z_act, group(ch, ty, tx, i) + 1)
                                        for k in banks:
                                            for j in range(NJ):
                                                c = BANK * (k % CBANK)
                                                mm = t.matmul(PS[32 * j:32 * j + 32, k, :],
                                                              K["adder_out"][:, 32 * i:32 * i + 32],
                                                              Z[:, i % 2, j, c:c + BANK], start=False, stop=False,
                                                              skip_group_check=True)
                                        mm.then_inc(z_free[i % 2], 1)
                            t.wait_ge(box, 4)
                            for k in banks:
                                mm = t.matmul(bank(k), K["adder_x"][:, :], px_bank(BOX, k), start=False, stop=True,
                                              skip_group_check=True)
                            mm.then_inc(s_ps, 1)
                        gn.pe(t, 1, K["mean_pair"][:, :])
                        if layer:
                            t.wait_ge(normed, 1)
                            for k in range(NBANK):
                                t.matmul(bank(k), K["to_nat"][:, :], SO[:, BANK * k:BANK * k + BANK],
                                         start=True, stop=True).then_inc(nat_ps, 1)

                    @blk.scalar
                    def _(a):
                        a.wait_ge(ready, 1)
                        for k in range(NBANK):
                            a.wait_ge(c_ps, k + 1)
                            a.activation(px_bank(CP[:, :, 1:H + 1, 1:W + 1], k), bank2(k), ACT.Copy)\
                             .then_inc(c_sb, 1)
                        a.wait_ge(c_sb, NBANK)
                        for ch in range(NB // CHUNK):
                            with a.Fori(0, 3, 1) as ty:
                                with a.Fori(0, 3, 1) as tx:
                                    for i in range(NI):
                                        a.wait_ge(z_free[i % 2], use(ch, ty, tx, i) + 1)
                                        for j in range(NJ):
                                            if j not in by_dve(i):
                                                w = ds((ty * 3 + tx) * CH + (NI * j + i), 1)
                                                op = a.activation(z(i, j), seen(ch, ty, tx), ACT.Relu, bias=ANf[:, w])
                                        op.then_inc(z_act, 1)
                            a.wait_ge(s_ps, ch + 1)
                            for k in range(CBANK * ch, CBANK * ch + CBANK):
                                a.activation(SO[:, BANK * k:BANK * k + BANK], bank(k), ACT.Copy).then_inc(s_sb, 1)
                        gn.act(a, 1)
                        if not layer:
                            a.wait_ge(normed, 1)
                            for b in range(NB):
                                a.activation(P2[:, b, 1:H + 1, 1:W + 1],
                                             SO[:, PX * b:PX * b + PX].rearrange("p (y x) -> p y x", y=H), ACT.Relu,
                                             scale=gn.scale[:, 0:1], bias=gn.bias[:, 0:1])
                            a.drain()

                    @blk.vector
                    def _(v):
                        v.wait_ge(c_sb, NBANK)
                        for ch in range(NB // CHUNK):
                            with v.Fori(0, 3, 1) as ty:
                                with v.Fori(0, 3, 1) as tx:
                                    for i in range(NI):
                                        v.wait_ge(z_free[i % 2], use(ch, ty, tx, i) + 1)
                                        for j in by_dve(i):
                                            w = ds((ty * 3 + tx) * CH + (NI * j + i), 1)
                                            op = v.tensor_scalar(z(i, j), seen(ch, ty, tx), AWf[:, w], 0.0,
                                                                 ALU.subtract, ALU.max)
                                        op.then_inc(z_dve, 1)
                        for k in range(NBANK):
                            v.wait_ge(s_sb, k + 1)
                            v.bn_stats(st6[:, k, :], SO[:, BANK * k:BANK * k + BANK])
                        v.drain()
                        v.bn_aggr(gn.mv[:, 0, :], st6[:, :, :].rearrange("p a b -> p (a b)"))
                        gn.dve(v, 1, BNV[:, 2 * layer:2 * layer + 1], BNV[:, 2 * layer + 1:2 * layer + 2], 1e-5)
                        if not layer:
                            v.drain().then_inc(normed, 1)
                            return
                        v.tensor_scalar(SO, SO, gn.scale[:, 0:1], gn.bias[:, 0:1], ALU.mult, ALU.add)
                        v.drain().then_inc(normed, 1)
                        for k in range(NBANK):
                            v.wait_ge(nat_ps, k + 1)
                            v.tensor_tensor(X[:, BANK * k:BANK * k + BANK], bank(k), X[:, BANK * k:BANK * k + BANK],
                                            ALU.add)
                        v.drain()
                        v.tensor_scalar(X[:, :], X[:, :], 0.0, None, ALU.max)
                        v.drain()
                        v.tensor_copy(XPin, X4)
                        v.drain()
            run.__name__ = f"adder_layer{layer}"
            return run

        phase(adder_layer(0, XP))
        phase(adder_layer(1, P2))
        lay1.close()


        def quantised(st, sb, sem):
            raw = [sb(f"raw{i}", [64, 128, TAPS]) for i in range(2)]
            W1 = sb("W1", [128, TAPS, 128])
            W2 = sb("W2", [128, TAPS, 128], BF16)
            AP = sb("AP", [128, NB, HP, WP], BF16)
            T = sb("T", [128, NBANK, BANK])
            bv = sb("bv", [128, 4, 2])
            inv, shift = sb("inv", [128, 2]), sb("shift", [128, 2])
            big, row, top, rcp = (sb(n, x) for n, x in (("big", [64, 2]), ("row", [1, 2, 64]), ("top", [1, 2]),
                                                        ("rcp", [128, 2])))
            one = sb("one", [1, 128])
            loads, tanh, m_sb, m_ps, q_sb, w_ps, w_sb, root, rooted, border = (
                sem(n) for n in ("loads", "tanh", "m_sb", "m_ps", "q_sb", "w_ps", "w_sb", "root", "rooted",
                                 "border"))
            c_ps, c_sb, q_done, d_ps = sem("c_ps"), sem("c_sb"), sem("q_done"), sem("d_ps")
            LEVELS = 15.0
            nload = [0]
            with nc.Block() as blk:
                @blk.sync
                def _(sp):
                    def load(dst, src):
                        sp.dma_start(dst, src).then_inc(loads, 16)
                        nload[0] += 16
                    for i in range(2):
                        for h in range(HALVES):
                            load(raw[i][:, 64 * h:64 * h + 64, :],
                                 A[f"L2_conv_w{i + 1}"].rearrange("o c ky kx -> o c (ky kx)"))
                            for f, n in enumerate(("gamma", "beta", "mean", "var")):
                                load(bv[64 * h:64 * h + 64, f, i:i + 1], halves(A[f"L2_conv_{n}{i + 1}"]))
                    sp.wait_ge(loads, nload[0])

                @blk.gpsimd
                def _(g):
                    g.memset(AP[:, :, :, :], 0.0)
                    g.memset(one[:, :], 1.0)
                    g.drain().then_inc(border, 1)

                @blk.scalar
                def _(a):
                    a.wait_ge(loads, nload[0])
                    for i in range(2):
                        a.activation(raw[i][:, :, :], raw[i][:, :, :], ACT.Tanh)
                    a.drain().then_inc(tanh, 1)
                    a.wait_ge(root, 1)
                    a.activation(shift[:, :], inv[:, :], ACT.Sqrt).then_inc(rooted, 1)
                    a.wait_ge(w_sb, 2)
                    for k in range(NBANK):
                        a.wait_ge(c_ps, k + 1)
                        a.activation(T[:, k, :], bank(k), ACT.Identity, scale=inv[:, 0:1], bias=shift[:, 0:1])\
                         .then_inc(c_sb, 1)

                @blk.tensor
                def _(t):
                    t.wait_ge(m_sb, 1)
                    for i in range(2):
                        mm = t.matmul(PS[0:1, 4, 64 * i:64 * i + 64], big[:, i:i + 1], K["ident"][0:64, 0:64],
                                      start=True, stop=True)
                    mm.then_inc(m_ps, 1)
                    t.wait_ge(m_sb, 2)
                    t.wait_ge(border, 1)
                    t.matmul(PS[:, 5, 0:2], one[:, :], top[:, :], start=True, stop=True).then_inc(m_ps, 1)
                    t.wait_ge(q_sb, 1)
                    for i in range(2):
                        for tap in range(TAPS):
                            mm = t.matmul(PS[:, 2 * i + tap // 8, 64 * (tap % 8):64 * (tap % 8) + 64],
                                          raw[i][:, :, tap], K["ident"][0:64, 0:64], start=True, stop=True)
                    mm.then_inc(w_ps, 1)
                    t.wait_ge(w_sb, 2)
                    for k in range(NBANK):
                        for tap in range(TAPS):
                            mm = t.matmul(bank(k), W1[:, tap, :], patch(XP, k, tap), start=(tap == 0),
                                          stop=(tap == TAPS - 1))
                        mm.then_inc(c_ps, 1)
                    t.wait_ge(q_done, 1)
                    for k in range(NBANK):
                        for tap in range(TAPS):
                            mm = t.matmul(bank(k), W2[:, tap, :], patch(AP, k, tap), start=(tap == 0),
                                          stop=(tap == TAPS - 1))
                        mm.then_inc(d_ps, 1)

                @blk.vector
                def _(v):
                    v.wait_ge(tanh, 1)
                    for i in range(2):
                        v.tensor_reduce(big[:, i:i + 1], raw[i][:, :, :], AX.XY, ALU.max, apply_absolute_value=True)
                    v.drain().then_inc(m_sb, 1)
                    v.wait_ge(m_ps, 1)
                    v.tensor_copy(row[:, :, :].rearrange("p a b -> p (a b)"), PS[0:1, 4, 0:128])
                    v.drain()
                    v.tensor_reduce(top[:, :], row[:, :, :], AX.X, ALU.max)
                    v.drain().then_inc(m_sb, 1)
                    v.wait_ge(m_ps, 2)
                    v.tensor_scalar(rcp[:, :], PS[:, 5, 0:2], 2.0, None, ALU.mult)
                    v.drain()
                    v.reciprocal(rcp[:, :], rcp[:, :])
                    v.drain()
                    for f, g, p, q in ((None, 0.5, ALU.mult, ALU.add), (LEVELS, MAGIC, ALU.mult, ALU.add),
                                       (MAGIC, 2.0, ALU.subtract, ALU.mult), (LEVELS, None, ALU.subtract, None)):
                        for i in range(2):
                            t = raw[i][:, :, :]
                            s = rcp[0:64, i:i + 1] if f is None else f
                            if g is None:
                                v.tensor_scalar(t, t, s, None, p)
                            else:
                                v.tensor_scalar(t, t, s, g, p, q)
                        v.drain()
                    v.drain().then_inc(q_sb, 1)
                    v.wait_ge(loads, nload[0])
                    v.tensor_scalar(inv[:, :], bv[:, 3, :], 1e-5, None, ALU.add)
                    v.drain().then_inc(root, 1)
                    v.wait_ge(rooted, 1)
                    v.reciprocal(inv[:, :], shift[:, :])
                    v.drain()
                    v.tensor_tensor(inv[:, :], inv[:, :], bv[:, 0, :], ALU.mult)
                    v.drain()
                    v.tensor_tensor(shift[:, :], inv[:, :], bv[:, 2, :], ALU.mult)
                    v.drain()
                    v.tensor_tensor(shift[:, :], bv[:, 1, :], shift[:, :], ALU.subtract)
                    v.tensor_scalar(inv[:, 0:1], inv[:, 0:1], 1.0 / LEVELS, None, ALU.mult)
                    v.tensor_scalar(inv[:, 1:2], inv[:, 1:2], 1.0 / LEVELS ** 2, None, ALU.mult)
                    v.drain().then_inc(w_sb, 1)
                    v.wait_ge(w_ps, 1)
                    for i, w in enumerate((W1, W2)):
                        block_weights(v, w, PS[:, 2 * i:2 * i + 2, :].rearrange("p a (t o) -> p (a t) o", o=CH)
                                      [:, 0:TAPS, :], "half_nat")
                    v.drain().then_inc(w_sb, 1)
                    v.wait_ge(border, 1)
                    for c in range(2):
                        v.wait_ge(c_sb, 4 * c + 4)
                        t = T[:, 4 * c:4 * c + 4, :]
                        v.tensor_scalar(t, t, 0.0, 1.0, ALU.max, ALU.min)
                        v.drain()
                        v.tensor_scalar(t, t, LEVELS, MAGIC, ALU.mult, ALU.add)
                        v.drain()
                        v.tensor_scalar(AP[:, 2 * c:2 * c + 2, 1:H + 1, 1:W + 1],
                                        t.rearrange("p (b k) (y x) -> p b (k y) x", k=2, x=W), MAGIC, None,
                                        ALU.subtract)
                    v.drain().then_inc(q_done, 1)
                    for k in range(NBANK):
                        v.wait_ge(d_ps, k + 1)
                        v.scalar_tensor_tensor(out=T[:, k, :], in0=bank(k), scalar=inv[:, 1:2],
                                               in1=X[:, BANK * k:BANK * k + BANK], op0=ALU.mult, op1=ALU.add)
                    v.drain()
                    t = T[:, :, :].rearrange("p a f -> p (a f)")
                    v.tensor_scalar(t, t, shift[:, 1:2], 0.0, ALU.add, ALU.max)
                    v.drain()
                    v.tensor_scalar(t, t, 1.0, LEVELS, ALU.min, ALU.mult)
                    v.drain()
                    v.tensor_scalar(t, t, MAGIC, MAGIC, ALU.add, ALU.subtract)
                    v.drain()
                    v.tensor_scalar(X[:, :], t, 1.0 / LEVELS, None, ALU.mult)
                    v.drain()
                    v.tensor_copy(XPin, X4)
                    v.drain()

        phase(quantised)

        lay3 = ExitStack()
        outer.enter_context(lay3)

        def l3(n, s, d=F32):
            return lay3.enter_context(nc.sbuf_tensor(n, s, d))

        INV, SHIFT = l3("INV", [128, 4]), l3("SHIFT", [128, 4])
        DC = l3("DC", [128, 5, CH])
        CV2 = l3("CV2", [128, 1, 128])
        IDX = l3("IDX", [128, TILES * HALVES, GK], I32)
        W4 = l3("W4", [128, TILES * HALVES, GK, 4])
        off_scope = ExitStack()
        outer.enter_context(off_scope)
        H2 = off_scope.enter_context(nc.sbuf_tensor("H2", [128, NB * PX], F32))
        OFF = off_scope.enter_context(nc.sbuf_tensor("OFF", [128, NB * PX], F32))
        NOFF = 3 * GK

        def residual_block(st, sb, sem):
            raw = [sb(f"raw{i}", [64, 128, TAPS]) for i in range(3)]
            rawdc = sb("rawdc", [64, CH, TAPS])
            rawcv = sb("rawcv", [64, 128])
            dcs = sb("dcs", [64, GK, CG])
            WB = [sb(f"WB{i}", [128, TAPS, 128]) for i in range(3)]
            bv = sb("bv", [128, 4, 4])
            bias = sb("bias", [128, 5])
            zero = sb("zero", [128, B * DG * NENT // 8])
            T1 = sb("T1", [128, NB, HP, WP])
            loads, cleared, w_go, w_ps, w_sb, root, rooted, filled = (
                sem(n) for n in ("loads", "cleared", "w_go", "w_ps", "w_sb", "root", "rooted", "filled"))
            a_ps, a_sb, b_ps, h_sb, o_ps = sem("a_ps"), sem("a_sb"), sem("b_ps"), sem("h_sb"), sem("o_ps")
            ws = ("rb_w1", "rb_w2", "off_w")
            nload = [0]
            with nc.Block() as blk:
                @blk.gpsimd
                def _(g):
                    g.memset(zero[:, :], 0.0)
                    g.memset(bias[:, :], 0.0)
                    g.memset(WB[2][:, :, :], 0.0)
                    g.memset(T1[:, :, :, :], 0.0)
                    g.drain().then_inc(cleared, 1)

                @blk.sync
                def _(sp):
                    def load(dst, src):
                        sp.dma_start(dst, src).then_inc(loads, 16)
                        nload[0] += 16
                    for h in range(HALVES):
                        for i, n in enumerate(ws):
                            load(raw[i][0:A["L3_conv_" + n].shape[0], 64 * h:64 * h + 64, :],
                                 A["L3_conv_" + n].rearrange("o c ky kx -> o c (ky kx)"))
                        load(rawcv[:, 64 * h:64 * h + 64], A["L3_conv_cv2_w"].rearrange("o c ky kx -> o (c ky kx)"))
                        for i, n in enumerate(("rb_bn1", "rb_bn2", "bn1", "bn2")):
                            for f in range(4):
                                load(bv[64 * h:64 * h + 64, f, i:i + 1],
                                     A["L3_conv_" + n][f:f + 1, :].rearrange("one c -> c one"))
                    load(rawdc[:, :, :], A["L3_conv_dc_w"].rearrange("o c ky kx -> o c (ky kx)"))
                    sp.wait_ge(cleared, 1)
                    for h in range(HALVES):
                        for i, n in ((0, "rb_b1"), (1, "rb_b2"), (2, "dc_b"), (4, "off_b")):
                            m = A["L3_conv_" + n].shape[0]
                            load(bias[64 * h:64 * h + m, i:i + 1], halves(A["L3_conv_" + n]))
                    for n in range(8):
                        sp.dma_start(table.rearrange("r f -> (r f)").rearrange("(n p f) -> n p f", n=8, p=128)[n],
                                     zero[:, :]).then_inc(filled, 16)
                    sp.wait_ge(loads, nload[0])
                    sp.wait_ge(filled, 128)

                @blk.tensor
                def _(t):
                    t.wait_ge(loads, nload[0])
                    t.wait_ge(w_go, 1)
                    for i in range(3):
                        m = A["L3_conv_" + ws[i]].shape[0]
                        for tap in range(TAPS):
                            mm = t.matmul(PS[:, 2 * i + tap // 8, 64 * (tap % 8):64 * (tap % 8) + m],
                                          raw[i][0:m, :, tap], K["ident"][0:m, 0:m], start=True, stop=True)
                    t.matmul(PS[:, 6, 0:64], rawcv[:, :], K["ident"][0:64, 0:64], start=True, stop=True)
                    for c in range(5):
                        n = min(4, GK - 4 * c) * CG
                        mm = t.matmul(PS[0:n, 7, 64 * c:64 * c + 64],
                                      dcs[:, :, :].rearrange("o g c -> o (g c)")[:, 128 * c:128 * c + n],
                                      K["ident"][0:64, 0:64], start=True, stop=True)
                    mm.then_inc(w_ps, 1)
                    t.wait_ge(w_sb, 1)
                    for k in range(NBANK):
                        for tap in range(TAPS):
                            mm = t.matmul(bank(k), WB[0][:, tap, :], patch(XP, k, tap), start=(tap == 0),
                                          stop=(tap == TAPS - 1))
                        mm.then_inc(a_ps, 1)
                    t.wait_ge(a_sb, NBANK)
                    for k in range(NBANK):
                        for tap in range(TAPS):
                            mm = t.matmul(bank(k), WB[1][:, tap, :], patch(T1, k, tap), start=(tap == 0),
                                          stop=(tap == TAPS - 1))
                        mm.then_inc(b_ps, 1)
                    t.wait_ge(h_sb, 1)
                    for k in range(NBANK):
                        for tap in range(TAPS):
                            mm = t.matmul(bank(k), WB[2][:, tap, :], patch(XP, k, tap), start=(tap == 0),
                                          stop=(tap == TAPS - 1))
                        mm.then_inc(o_ps, 1)

                @blk.scalar
                def _(a):
                    a.wait_ge(root, 1)
                    a.activation(SHIFT[:, :], INV[:, :], ACT.Sqrt).then_inc(rooted, 1)
                    a.wait_ge(w_sb, 1)
                    a.wait_ge(cleared, 1)
                    for k in range(NBANK):
                        a.wait_ge(a_ps, k + 1)
                        a.activation(px_bank(T1[:, :, 1:H + 1, 1:W + 1], k), bank2(k), ACT.Relu,
                                     scale=INV[:, 0:1], bias=SHIFT[:, 0:1]).then_inc(a_sb, 1)
                    for k in range(NBANK):
                        a.wait_ge(o_ps, k + 1)
                        a.activation(OFF[:, BANK * k:BANK * k + BANK], bank(k), ACT.Identity, bias=bias[:, 4:5])
                    a.drain()

                @blk.vector
                def _(v):
                    v.wait_ge(loads, nload[0])
                    for d in range(DG):
                        v.tensor_copy(dcs[:, TAPS * d:TAPS * d + TAPS, :],
                                      rawdc[:, CG * d:CG * d + CG, :].rearrange("o c k -> o k c"))
                    v.tensor_scalar(INV[:, :], bv[:, 3, :], 1e-5, None, ALU.add)
                    v.drain().then_inc(w_go, 1)
                    v.drain().then_inc(root, 1)
                    v.wait_ge(rooted, 1)
                    v.reciprocal(INV[:, :], SHIFT[:, :])
                    v.drain()
                    v.tensor_tensor(INV[:, :], INV[:, :], bv[:, 0, :], ALU.mult)
                    v.tensor_tensor(SHIFT[:, :], bias[:, 0:4], bv[:, 2, :], ALU.subtract)
                    v.drain()
                    v.tensor_tensor(SHIFT[:, :], SHIFT[:, :], INV[:, :], ALU.mult)
                    v.drain()
                    v.tensor_tensor(SHIFT[:, :], SHIFT[:, :], bv[:, 1, :], ALU.add)
                    v.wait_ge(w_ps, 1)
                    v.wait_ge(cleared, 1)
                    for i in range(3):
                        m = A["L3_conv_" + ws[i]].shape[0]
                        block_weights(v, WB[i], PS[:, 2 * i:2 * i + 2, :].rearrange("p a (t o) -> p (a t) o", o=CH)
                                      [:, 0:TAPS, 0:m], "half_nat", m)
                    block_weights(v, CV2, PS[:, 6:7, 0:64], "half_nat")
                    v.tensor_copy(DC[:, 0:4, :], PS[:, 7, 0:256].rearrange("p (a o) -> p a o", o=CH))
                    v.tensor_copy(DC[0:64, 4, :], PS[0:64, 7, 256:320])
                    v.drain().then_inc(w_sb, 1)
                    for k in range(NBANK):
                        v.wait_ge(b_ps, k + 1)
                        v.scalar_tensor_tensor(out=H2[:, BANK * k:BANK * k + BANK], in0=bank(k), scalar=INV[:, 1:2],
                                               in1=X[:, BANK * k:BANK * k + BANK], op0=ALU.mult, op1=ALU.add)
                    v.drain()
                    v.tensor_scalar(H2[:, :], H2[:, :], SHIFT[:, 1:2], 0.0, ALU.add, ALU.max)
                    v.drain()
                    v.tensor_copy(XPin, H2[:, :].rearrange("p (b y x) -> p b y x", b=NB, y=H))
                    v.drain().then_inc(h_sb, 1)

        phase(residual_block)

        def offsets(st, sb, sem):
            HT = sb("HT", [128, TILES, 128])
            OT = sb("OT", [128, TILES, 128])
            GR = sb("GR", [128, 3, TILES * HALVES * GK])
            n = TILES * HALVES * GK
            pos = sb("pos", [128, 2, n])
            low = sb("low", [128, 2, n])
            above = sb("above", [128, 2, n])
            whole = sb("whole", [128, 2, n], I32)
            mask = sb("mask", [128, TILES * HALVES, GK])
            off3 = OT[:, :, :].rearrange("p t (h c) -> p (t h) c", h=HALVES)
            ident = K["ident"][:, :]
            loads, h_ps, h_sb, o_ps, o_sb, stored, m_done = (
                sem(x) for x in ("loads", "h_ps", "h_sb", "o_ps", "o_sb", "stored", "m_done"))
            T6 = table.rearrange("(b q ey ex) (k c) -> b q ey ex k c", b=NB,
                                 q=HALVES * DG, ey=TP, k=4)

            def store(eng, b, yr):
                for dy in range(2):
                    for dx in range(2):
                        first = yr - dy + 1
                        for q in range(HALVES * DG):
                            eng.dma_start(
                                T6[b, q, first:first + 29:4, 1 - dx:1 - dx + W, 2 * dy + dx, :]
                                .rearrange("e x c -> x e c"),
                                HT[32 * yr:32 * yr + 32, 8 * b:8 * b + 8, CG * q:CG * q + CG]).then_inc(stored, 16)

            with nc.Block() as blk:
                @blk.sync
                def _(sp):
                    for i, g in enumerate(GRIDS):
                        sp.dma_start(GR[:, i, :], C[g]).then_inc(loads, 16)
                    sp.wait_ge(loads, 48)
                    for b in range(NB):
                        sp.wait_ge(h_sb, 2 * b + 2)
                        for yr in range(4):
                            store(sp, b, yr)
                    sp.wait_ge(stored, 16 * NB * 4 * 4 * HALVES * DG)

                @blk.tensor
                def _(t):
                    for k in range(NBANK):
                        for i in range(4):
                            tl = 4 * k + i
                            mm = t.transpose(PS[:, k, 128 * i:128 * i + 128], OFF[:, 128 * tl:128 * tl + 128], ident)
                        mm.then_inc(o_ps, 1)
                    for k in range(NBANK):
                        t.wait_ge(o_sb, k + 1)
                        for i in range(4):
                            tl = 4 * k + i
                            mm = t.transpose(PS[:, k, 128 * i:128 * i + 128], H2[:, 128 * tl:128 * tl + 128], ident)
                        mm.then_inc(h_ps, 1)

                @blk.scalar
                def _(a):
                    for k in range(NBANK):
                        a.wait_ge(o_ps, k + 1)
                        a.activation(OT[:, 4 * k:4 * k + 4, :], PS[:, k, :].rearrange("p (a c) -> p a c", c=128),
                                     ACT.Copy).then_inc(o_sb, 1)
                    for k in range(NBANK):
                        a.wait_ge(h_ps, k + 1)
                        a.activation(HT[:, 4 * k:4 * k + 4, :], PS[:, k, :].rearrange("p (a c) -> p a c", c=128),
                                     ACT.Copy).then_inc(h_sb, 1)
                    a.wait_ge(o_sb, NBANK)
                    a.activation(mask[:, :, :], off3[:, :, 2 * GK:3 * GK], ACT.Sigmoid).then_inc(m_done, 1)

                @blk.vector
                def _(v):
                    p3 = pos[:, :, :].rearrange("p a (t k) -> p a t k", k=GK)
                    v.wait_ge(loads, 48)
                    v.wait_ge(o_sb, NBANK)
                    for a in range(2):
                        v.tensor_tensor(p3[:, a], off3[:, :, a:2 * GK:2],
                                        GR[:, a, :].rearrange("p (t k) -> p t k", k=GK), ALU.add)
                    v.drain()
                    v.tensor_scalar(pos[:, :, :], pos[:, :, :], -1.0, float(H), ALU.max, ALU.min)
                    v.drain()
                    v.tensor_copy(whole[:, :, :], pos[:, :, :])
                    v.drain()
                    v.tensor_copy(low[:, :, :], whole[:, :, :])
                    v.drain()
                    v.tensor_tensor(above[:, :, :], low[:, :, :], pos[:, :, :], ALU.is_gt)
                    v.drain()
                    v.tensor_tensor(low[:, :, :], low[:, :, :], above[:, :, :], ALU.subtract)
                    v.drain()
                    v.tensor_tensor(pos[:, :, :], pos[:, :, :], low[:, :, :], ALU.subtract)
                    v.drain()
                    v.tensor_tensor(low[:, 1, :], low[:, 1, :], GR[:, 2, :], ALU.add)
                    v.drain()
                    v.scalar_tensor_tensor(out=low[:, 0, :], in0=low[:, 0, :], scalar=float(TP), in1=low[:, 1, :],
                                           op0=ALU.mult, op1=ALU.add)
                    v.tensor_scalar(above[:, :, :], pos[:, :, :], -1.0, 1.0, ALU.mult, ALU.add)
                    v.drain()
                    v.tensor_copy(IDX[:, :, :].rearrange("p t k -> p (t k)"), low[:, 0, :])
                    v.wait_ge(m_done, 1)
                    mk = mask[:, :, :].rearrange("p t k -> p (t k)")
                    w4 = W4[:, :, :, :].rearrange("p t k c -> p (t k) c")
                    v.tensor_tensor(above[:, 0, :], above[:, 0, :], mk, ALU.mult)
                    v.tensor_tensor(pos[:, 0, :], pos[:, 0, :], mk, ALU.mult)
                    v.drain()
                    for c, (wy, wx) in enumerate(((above, above), (above, pos), (pos, above), (pos, pos))):
                        v.tensor_tensor(w4[:, :, c], wy[:, 0, :], wx[:, 1, :], ALU.mult)
                    v.drain()

        phase(offsets)
        off_scope.close()

        def sampling(st, sb, sem):
            RING = 3
            G = [sb(f"G{i}", [128, GK, 4 * CG]) for i in range(RING)]
            VAL = sb("VAL", [128, 2, GK, CG])
            VT = sb("VT", [128, 2, 5, 128])
            Y = sb("Y", [128, 2, BANK])
            U = sb("U", [128, 2, BANK])
            arrived = [sem(f"arrived{i}") for i in range(RING)]
            used, val, t_ps, t_sb, d_ps, d_sb, leaky, e_ps, e_sb = (
                sem(n) for n in ("used", "val", "t_ps", "t_sb", "d_ps", "d_sb", "leaky", "e_ps", "e_sb"))
            stored = sem("stored")
            NTH = TILES * HALVES
            with nc.Block() as blk:
                @blk.gpsimd
                def _(g):
                    for th in range(NTH):
                        if th >= RING:
                            g.wait_ge(used, th - RING + 1)
                        for k in range(GK):
                            g.indirect_dma_start(G[th % RING][:, k, :], None, table,
                                                 bass.IndirectOffsetOnAxis(ap=IDX[:, th, k:k + 1], axis=0))\
                             .then_inc(arrived[th % RING], 16)

                @blk.vector
                def _(v):
                    for th in range(NTH):
                        gt = G[th % RING]
                        v.wait_ge(arrived[th % RING], 16 * GK * (th // RING + 1))
                        g3 = gt[:, :, :].rearrange("p k (q c) -> p (k q) c", q=4)
                        v.tensor_tensor(g3, g3, W4[:, th, :, :].rearrange("p k q -> p (k q)").unsqueeze(2)
                                        .broadcast_to([128, GK * 4, CG]), ALU.mult)
                        v.drain()
                        if th >= 2:
                            v.wait_ge(t_ps, th - 1)
                        v.tensor_reduce(VAL[:, th % 2, :, :], gt[:, :, :].rearrange("p k (q c) -> p k c q", q=4),
                                        AX.X, ALU.add)
                        v.drain().then_inc(val, 1)
                        v.sem_inc(used, 1)
                        if th % 8 == 7:
                            k = th // 8
                            y, u, x = Y[:, k % 2, :], U[:, k % 2, :], X[:, BANK * k:BANK * k + BANK]
                            v.wait_ge(d_sb, k + 1)
                            v.scalar_tensor_tensor(out=y, in0=y, scalar=0.1, in1=y, op0=ALU.mult, op1=ALU.max)
                            v.drain().then_inc(leaky, 1)
                            v.wait_ge(e_sb, k + 1)
                            v.scalar_tensor_tensor(out=u, in0=u, scalar=0.1, in1=u, op0=ALU.mult, op1=ALU.max)
                            v.drain()
                            v.tensor_tensor(x, x, u, ALU.add)
                    v.drain()

                @blk.tensor
                def _(t):
                    for th in range(NTH):
                        tl, h, k = th // 2, th % 2, th // 8
                        p = 2 * (th % 2)
                        t.wait_ge(val, th + 1)
                        if th >= 2:
                            t.wait_ge(t_sb, th - 1)
                        flat = VAL[:, th % 2, :, :].rearrange("p k c -> p (k c)")
                        for c in range(5):
                            n = min(128, GK * CG - 128 * c)
                            mm = t.transpose(PS[0:n, p + c // 4, 128 * (c % 4):128 * (c % 4) + 128],
                                             flat[:, 128 * c:128 * c + n], K["ident"][:, :])
                        mm.then_inc(t_ps, 1)
                        t.wait_ge(t_sb, th + 1)
                        if th % 8 == 0 and k >= 2:
                            t.wait_ge(d_sb, k - 1)
                        for c in range(5):
                            n = min(128, GK * CG - 128 * c)
                            mm = t.matmul(PS[64 * h:64 * h + 64, 4 + k % 2, 128 * (tl % 4):128 * (tl % 4) + 128],
                                          DC[0:n, c, :], VT[0:n, th % 2, c, :], start=(c == 0), stop=(c == 4))
                        if th % 8 == 7:
                            mm.then_inc(d_ps, 1)
                            t.wait_ge(leaky, k + 1)
                            t.matmul(bank(6), CV2[:, 0, :], Y[:, k % 2, :], start=True, stop=True).then_inc(e_ps, 1)

                @blk.scalar
                def _(a):
                    for th in range(NTH):
                        k = th // 8
                        p = 2 * (th % 2)
                        a.wait_ge(t_ps, th + 1)
                        a.activation(VT[:, th % 2, 0:4, :], PS[:, p, :].rearrange("p (a c) -> p a c", c=128), ACT.Copy)
                        a.activation(VT[0:64, th % 2, 4, :], PS[0:64, p + 1, 0:128], ACT.Copy)
                        a.drain().then_inc(t_sb, 1)
                        if th % 8 == 7:
                            a.wait_ge(d_ps, k + 1)
                            a.activation(Y[:, k % 2, :], bank(4 + k % 2), ACT.Identity, scale=INV[:, 2:3],
                                         bias=SHIFT[:, 2:3]).then_inc(d_sb, 1)
                            a.wait_ge(e_ps, k + 1)
                            a.activation(U[:, k % 2, :], bank(6), ACT.Identity, scale=INV[:, 3:4],
                                         bias=SHIFT[:, 3:4]).then_inc(e_sb, 1)

        phase(sampling)
        lay3.close()

        def finish(st, sb, sem):
            stored = sem("stored")
            with nc.Block() as blk:
                @blk.sync
                def _(sp):
                    for h in range(HALVES):
                        sp.dma_start(out[NB * h:NB * h + NB].rearrange("b c y x -> c b (y x)"),
                                     X[64 * h:64 * h + 64, :].rearrange("c (b f) -> c b f", b=NB))\
                          .then_inc(stored, 16)
                    sp.wait_ge(stored, 32)
        stop_after = 99
        phase(finish)


def kernel(**inputs):
    import numpy as _np
    import concourse.bacc as _bacc
    from concourse import mybir as _mybir
    from concourse.bass_utils import run_bass_kernel_spmd as _run

    nc = _bacc.Bacc("TRN2", target_bir_lowering=False, num_devices=1)
    arrays, args, consts = {}, {}, {}
    for name, value in inputs.items():
        a = _np.ascontiguousarray(value)
        arrays["in_" + name] = a
        args[name] = nc.dram_tensor("in_" + name, a.shape, _mybir.dt.from_np(a.dtype), kind="ExternalInput").ap()
    for name, a in constants().items():
        arrays["const_" + name] = a
        consts[name] = nc.dram_tensor("const_" + name, a.shape, _mybir.dt.from_np(a.dtype), kind="ExternalInput").ap()
    out = nc.dram_tensor("out", (B, CH, H, W), F32, kind="ExternalOutput").ap()
    program(nc, args, consts, out)
    r = _run(nc, [arrays], core_ids=[0])
    return r.results[0]["out"]
```

```python
from contextlib import ExitStack

import numpy as np
import concourse.bass as bass
from concourse import mybir

F32 = mybir.dt.float32
BF16 = mybir.dt.bfloat16
I32 = mybir.dt.int32
ALU = mybir.AluOpType
ACT = mybir.ActivationFunctionType
AX = mybir.AxisListType
ds = bass.ds

B, CH, H, W = 8, 64, 32, 32
HALVES = 2
NB = B // HALVES
PX = H * W
HP, WP = H + 2, W + 2
TAPS = 9
BANK = 512
NBANK = NB * PX // BANK
HW2 = H // 2
NTOK = HW2 * HW2
HEADS, HD = 8, 8
TOPK = NTOK // 2
ROUNDS = 3
AIM = TOPK - 4 * ROUNDS
STEP = 0.0085
TAKEN = -1.0e30
MAGIC = 12582912.0
DG = 2
CG = CH // DG
TP = H + 2
NENT = TP * TP
TILES = PX // 128
STEPS = TILES * HALVES
GK = DG * TAPS
CHUNK = 2
SLOTS = 3

NJ, NI = 4, 16

CHAIN = [(0, 1), (0, 1), (), (0, 1)]
COST_DVE, COST_CHAIN, COST_ACT = 1.2, 2.66, 1.9


def adder_rows():
    rows = []
    for q, chain in enumerate(CHAIN):
        n = 3 * NJ - len(chain[1:])
        tiles = []
        for j in range(NJ):
            maps = [(4 * q + i, (tx,)) for i in range(4) for tx in range(3) if i != j or tx not in chain]
            if chain:
                maps.insert((2 * j + 1) * n // (2 * NJ), (4 * q + j, chain))
            tiles.append(maps)
        rows += [list(r) for r in zip(*tiles)]
    dve = act = 0.0
    out = []
    for row in rows:
        plan = [None] * NJ
        for j in sorted(range(NJ), key=lambda j: -len(row[j][1])):
            i, taps = row[j]
            by_dve = len(taps) > 1 or dve + COST_DVE <= act + COST_ACT
            if by_dve:
                dve += COST_DVE + COST_CHAIN * (len(taps) - 1)
            else:
                act += COST_ACT
            plan[j] = (i, taps, "dve" if by_dve else "act")
        out.append(plan)
    return out


def constants():
    p = np.arange(128)
    half, ch = p // CH, p % CH
    pj, ph, pi = p // 32, (p % 32) // NI, p % NI
    pch = NI * pj + pi
    c = {}
    c["ident"] = np.eye(128)
    c["mean8"] = (p[:, None] // 8 == p[None] // 8) / 8.0
    c["mean4"] = (p[:, None] // 4 == p[None] // 4) / 4.0
    c["sum8"] = (p[:, None] // 8 == p[None] // 8) * 1.0
    c["mean_pair"] = (pch[:, None] == pch[None]) / 2.0
    c["half_nat"] = (half[:, None] == np.arange(2)[None]) * 1.0
    c["half_perm"] = (ph[:, None] == np.arange(2)[None]) * 1.0
    c["head"] = (p[:, None] // HD == np.arange(HALVES * HEADS)[None]) * 1.0
    slot = np.arange(32)
    one = [((slot[None] == NI * half[:, None] + i) * -2.0) for i in range(NI)]
    c["slots"] = np.tile(np.arange(8 * ROUNDS), 4)[None].repeat(128, 0)
    c["adder_out"] = np.concatenate(one, 1)
    sign = np.ones((3, 3, NJ, NI))
    for q, chain in enumerate(CHAIN):
        for j in range(NJ):
            for tx in chain[1:]:
                sign[:, tx, j, 4 * q + j] = -1.0
    c["adder_sign"] = sign.reshape(1, -1).repeat(128, 0)
    c["adder_x"] = (half[:, None] == ph[None]) * 1.0
    c["to_nat"] = ((pch[:, None] == ch[None]) & (ph[:, None] == half[None])) * 1.0
    t = np.arange(TILES)
    y = 4 * t[None] + p[:, None] // 32
    x = np.broadcast_to(p[:, None] % 32, y.shape)
    k = np.arange(TAPS)
    gy = y[:, :, None, None, None] + (k // 3 - 1)
    gx = x[:, :, None, None, None] + (k % 3 - 1)
    q = np.arange(HALVES)[None, :, None] * DG + np.arange(DG)
    full = (128, TILES, HALVES, DG, TAPS)
    c["grid_y"] = np.broadcast_to(gy, full).reshape(128, -1)
    c["grid_x"] = np.broadcast_to(gx, full).reshape(128, -1)
    c["grid_base"] = np.broadcast_to((q * NENT + TP + 1)[None, :, :, :, None], full).reshape(128, -1)
    return {n: np.ascontiguousarray(a, dtype=np.float32) for n, a in c.items()}


SMALL = ["ident", "mean8", "mean4", "sum8", "mean_pair", "half_nat", "half_perm", "head", "slots", "adder_out", "adder_x",
         "to_nat"]
GRIDS = ["grid_y", "grid_x", "grid_base"]


def halves(ap):
    return ap.rearrange("(c one) -> c one", one=1)


class Stats:

    def __init__(self, sem, sb, name, m, ps):
        self.m, self.ps, self.n = m, ps, 0
        self.to_pe, self.from_pe = sem(name + "_to_pe"), sem(name + "_from_pe")
        self.to_act, self.from_act = sem(name + "_to_act"), sem(name + "_from_act")
        self.mv = sb(name + "_mv", [128, m, 2])
        self.mean, self.dev, self.var = (sb(name + x, [128, m]) for x in ("_mean", "_dev", "_var"))
        self.scale, self.bias = sb(name + "_scale", [128, m]), sb(name + "_bias", [128, m])
        self.eps = None

    def dve(self, v, m, gamma, beta, eps, n=0):
        mean, dev, var, scale, bias = (t[:, 0:m] for t in (self.mean, self.dev, self.var, self.scale, self.bias))
        v.drain().then_inc(self.to_pe, 1)
        v.wait_ge(self.from_pe, 2 * n + 1)
        v.tensor_copy(mean, self.ps[:, 0:m])
        v.drain()
        v.tensor_tensor(dev, self.mv[:, 0:m, 0], mean, ALU.subtract)
        v.drain()
        v.tensor_tensor(dev, dev, dev, ALU.mult)
        v.drain()
        v.tensor_tensor(var, self.mv[:, 0:m, 1], dev, ALU.add)
        v.drain().then_inc(self.to_pe, 1)
        v.wait_ge(self.from_pe, 2 * n + 2)
        v.tensor_scalar(dev, self.ps[:, 64:64 + m], eps, None, ALU.add)
        v.drain().then_inc(self.to_act, 1)
        v.wait_ge(self.from_act, n + 1)
        v.reciprocal(scale, var)
        v.drain()
        v.tensor_tensor(scale, scale, gamma, ALU.mult)
        v.drain()
        v.tensor_tensor(dev, mean, scale, ALU.mult)
        v.drain()
        v.tensor_tensor(bias, beta, dev, ALU.subtract)
        v.drain()

    def pe(self, t, m, matrix, n=0):
        t.wait_ge(self.to_pe, 2 * n + 1)
        t.matmul(self.ps[:, 0:m], matrix, self.mv[:, 0:m, 0], start=True, stop=True).then_inc(self.from_pe, 1)
        t.wait_ge(self.to_pe, 2 * n + 2)
        t.matmul(self.ps[:, 64:64 + m], matrix, self.var[:, 0:m], start=True, stop=True).then_inc(self.from_pe, 1)

    def act(self, a, m, n=0):
        a.wait_ge(self.to_act, n + 1)
        a.activation(self.var[:, 0:m], self.dev[:, 0:m], ACT.Sqrt).then_inc(self.from_act, 1)


def program(nc, A, C, out, stop_after=99):
    tables = [nc.dram_tensor(f"neighbours{b}", [HALVES * DG * NENT, 4 * CG], F32).ap() for b in range(NB)]
    outer = ExitStack()
    with outer:
        def osb(n, s, d=F32):
            return outer.enter_context(nc.sbuf_tensor(n, s, d))

        K = {n: osb("c_" + n, [128, C[n].shape[1]]) for n in SMALL}
        X = osb("X", [128, NB * PX])
        XP = osb("XP", [128, NB, HP, WP])
        PS = outer.enter_context(nc.psum_tensor("PS", [128, NBANK, BANK], F32))
        P2 = osb("P2", [128, NB, HP, WP])
        RAW2 = osb("RAW2", [64, 2, 128, TAPS])
        BNV = osb("BNV", [128, 4])
        BV2 = osb("BV2", [128, 4, 2])
        BV3 = osb("BV3", [128, 4, 4])
        BIAS3 = osb("BIAS3", [128, 5])
        RAW1 = P2[0:64, :, :, :].rearrange("p b y x -> p (b y x)")[:, 0:4 * 128 * TAPS]\
            .rearrange("p (q c t) -> p q c t", q=4, t=TAPS)
        X4 = X[:, :].rearrange("p (b y x) -> p b y x", b=NB, y=H)
        XPin = XP[:, :, 1:H + 1, 1:W + 1]

        def px_bank(t, k):
            return t[:, k // 2, 16 * (k % 2):16 * (k % 2) + 16, :]

        def patch(t, k, tap):
            y = 16 * (k % 2) + tap // 3
            return t[:, k // 2, y:y + 16, tap % 3:tap % 3 + W]

        def bank(k):
            return PS[:, k, :]

        def bank2(k):
            return PS[:, k, :].rearrange("p (y x) -> p y x", x=W)

        phase_names = []

        def phase(fn, recycle=False):
            phase_names.append(fn.__name__)
            if len(phase_names) > stop_after:
                return
            with ExitStack() as st:
                def sb(n, s, d=F32):
                    return st.enter_context(nc.sbuf_tensor(f"{fn.__name__}_{n}", s, d))

                def sem(n):
                    if recycle:
                        recycled.append(nc.alloc_semaphore(name=f"{fn.__name__}_{n}"))
                        return recycled[-1]
                    return st.enter_context(nc.semaphore(f"{fn.__name__}_{n}"))
                recycled = []
                fn(st, sb, sem)
                if recycle:
                    nc.clear_and_free_semaphores(recycled)
                    nc.all_engine_barrier()

        lay0 = ExitStack()
        outer.enter_context(lay0)
        LL = lay0.enter_context(nc.sbuf_tensor("LL", [128, NB * NTOK], F32))
        HI = lay0.enter_context(nc.sbuf_tensor("HI", [128, 3, NB, HW2 + 2, HW2 + 2], F32))
        W0 = lay0.enter_context(nc.sbuf_tensor("W0", [128, 17, 128], F32))
        V0 = lay0.enter_context(nc.sbuf_tensor("V0", [128, 24], F32))
        vec = {}
        for name, n in (("attn_gn_g", 1), ("attn_gn_b", 1), ("he_gn1_g", 3), ("he_gn1_b", 3), ("he_gn2_g", 3),
                        ("he_gn2_b", 3), ("ffn_gn1_g", 2), ("ffn_gn1_b", 2), ("ffn_gn2_g", 1), ("ffn_gn2_b", 1),
                        ("alpha", 1)):
            vec[name] = (sum(x[1] for x in vec.values()), n)
        HE = lay0.enter_context(nc.sbuf_tensor("HE", [128, 3, TAPS], F32))

        def v0(name, rep):
            o, n = vec[name]
            return V0[:, o:o + n].unsqueeze(2).broadcast_to([128, n, rep])

        V12t = lay0.enter_context(nc.sbuf_tensor("V12", [128, 4, 3, NB], F32))
        V12 = {n: V12t[:, i, :, :].rearrange("p s b -> p (s b)") for i, n in enumerate(("g", "b", "g2", "b2"))}
        VFt = lay0.enter_context(nc.sbuf_tensor("VF", [128, 2, 2, NB], F32))
        VF = {n: VFt[:, i, :, :].rearrange("p s b -> p (s b)") for i, n in enumerate("gb")}

        atn = ExitStack()
        outer.enter_context(atn)

        def asb(n, shape, d=F32):
            return atn.enter_context(nc.sbuf_tensor(n, shape, d))

        GROUPS = NB * HEADS
        qk_all = asb("qk", [128, 2, (NB + 1) * NTOK])
        VT = asb("VT", [128, NB * HALVES, HEADS, 2, HD])
        VTf = VT[:, :, :, :, :].rearrange("p a b c d -> p (a b c d)")
        O = asb("O", [128, 2, NB * HALVES * CH])
        START, SLOPE = asb("START", [128, 4 * GROUPS]), asb("SLOPE", [128, 4 * GROUPS])
        COUNT = asb("COUNT", [128, 4 * GROUPS])
        REDO = asb("REDO", [128, 1], I32)

        def attention(st, sb, sem):
            loads, ll_done, w_ps, w_sb = sem("loads"), sem("ll_done"), sem("w_ps"), sem("w_sb")
            raws = sem("raws")
            qk_ps, qk_sq, qk_ns, qk_nrm, qk_done = (sem(n) for n in ("qk_ps", "qk_sq", "qk_ns", "qk_nrm", "qk_done"))
            v_ps, v_done = sem("v_ps"), sem("v_done")
            kt_ps, kt_sb, cov_ps, cov_sb, cq_ps, cq_sb, row_ps, dev_in, dev_done = (
                sem(n) for n in ("kt_ps", "kt_sb", "cov_ps", "cov_sb", "cq_ps", "cq_sb", "row_ps", "dev_in",
                                 "dev_done"))
            rawq = sb("rawq", [64, 3, 2, 64])
            rawp = sb("rawp", [64, 2, 64])
            rawpw = sb("rawpw", [64, 3, 2, 3, 64])
            rawf1 = sb("rawf1", [64, 2, 2, 64])
            rawf2 = sb("rawf2", [64, 2, 2, 64])
            xh = sb("xh", [128, NB, H, W])
            su = [sb(f"su{i}", [128, NB, HW2, HW2]) for i in range(4)]
            qk = qk_all[:, :, 0:NB * NTOK]
            sq = sb("sq", [128, 2, NB * NTOK])
            KT = sb("KT", [128, NB, 2, 128])
            COV = sb("COV", [128, NB, 128])
            QCQ = sb("QCQ", [128, NB * NTOK])
            ksum = sb("ksum", [128, NB])
            KM = sb("KM", [128, NB, HALVES * HEADS])
            row_sq = sb("row_sq", [128, 4 * GROUPS])
            nload, nraw = [0], [0]
            rawx = sb("rawx", [64, 17, 128])

            with nc.Block() as blk:
                @blk.sync
                def _(sp):
                    def load(dst, src):
                        sp.dma_start(dst, src).then_inc(loads, 16)
                        nload[0] += 16
                    for h in range(HALVES):
                        load(X[64 * h:64 * h + 64, :].rearrange("c (b f) -> c b f", b=NB),
                             A["x"][NB * h:NB * h + NB].rearrange("b c y x -> c b (y x)"))
                    for n in SMALL:
                        load(K[n][:, :], C[n])
                    for h in range(HALVES):
                        rows = slice(64 * h, 64 * h + 64)
                        for name, (o, n) in vec.items():
                            if name == "alpha":
                                load(V0[rows, o:o + 1], A["L0_conv_alpha"].rearrange("(a b) -> a b", a=1)
                                     .broadcast_to([64, 1]))
                            else:
                                for i in range(n):
                                    load(V0[rows, o + i:o + i + 1], halves(A["L0_conv_" + name][64 * i:64 * i + 64]))
                        load(HE[rows, :, :], A["L0_conv_he_dw_w"].rearrange("(s c) one ky kx -> c s (one ky kx)", c=64))
                    sp.wait_ge(loads, nload[0])

                @blk.scalar
                def _(a):
                    def load(dst, src):
                        a.dma_start(dst, src).then_inc(raws, 16)
                        nraw[0] += 16
                    for d in range(2):
                        load(rawq[:, :, d, :], A["L0_conv_qkv_w"].rearrange("(s o) c -> o s c", o=64))
                        load(rawp[:, d, :], A["L0_conv_proj_w"])
                        for s in range(3):
                            load(rawpw[:, s, d, :, :], A["L0_conv_he_pw_w"][64 * s:64 * s + 64, :]
                                 .rearrange("o (i c) -> o i c", c=64))
                        load(rawf1[:, :, d, :], A["L0_conv_ffn_w1"].rearrange("(s o) c -> o s c", o=64))
                        load(rawf2[:, :, d, :], A["L0_conv_ffn_w2"].rearrange("o (s c) -> o s c", c=64))
                    a.wait_ge(qk_ns, 1)
                    a.activation(sq[:, :, :].rearrange("p a f -> p (a f)"),
                                 PS[:, 0:4, :].rearrange("p a f -> p (a f)"), ACT.Sqrt).then_inc(qk_nrm, 1)
                    a.wait_ge(kt_ps, 1)
                    a.activation(KT[:, :, :, :].rearrange("p b t c -> p (b t c)"),
                                 PS[:, 6:8, :].rearrange("p a f -> p (a f)"), ACT.Copy).then_inc(kt_sb, 1)
                    a.wait_ge(dev_in, 1)
                    a.activation(SLOPE[:, :], row_sq[:, :], ACT.Sqrt,
                                 scale=(STEP ** 2) / HD).then_inc(dev_done, 1)

                @blk.gpsimd
                def _(g):
                    g.memset(HI[:, :, :, :, :], 0.0)
                    g.memset(XP[:, :, :, :], 0.0)
                    g.memset(BIAS3[:, :], 0.0)
                    g.drain().then_inc(ll_done, 1)

                @blk.tensor
                def _(t):
                    t.wait_ge(loads, nload[0])
                    t.wait_ge(raws, nraw[0])
                    t.wait_ge(w_sb, 1)
                    for s in range(17):
                        mm = t.matmul(PS[:, 5 + s // 8, 64 * (s % 8):64 * (s % 8) + 64], rawx[:, s, :],
                                      K["ident"][0:64, 0:64], start=True, stop=True)
                    mm.then_inc(w_ps, 1)
                    t.wait_ge(w_sb, 2)
                    t.wait_ge(ll_done, 2)
                    for s in range(2):
                        for k in range(2):
                            mm = t.matmul(PS[:, 2 * s + k, :], W0[:, s, :], LL[:, BANK * k:BANK * k + BANK],
                                          start=True, stop=True)
                    mm.then_inc(qk_ps, 1)
                    for b in range(NB):
                        for h in range(HALVES):
                            for mt in range(2):
                                o = (b * 2 + mt) * 64
                                mm = t.matmul(PS[:, 4 + h, o:o + 64],
                                              LL[64 * h:64 * h + 64, b * NTOK + 128 * mt:b * NTOK + 128 * mt + 128],
                                              W0[64 * h:64 * h + 64, 2, 64 * h:64 * h + 64], start=True, stop=True)
                    mm.then_inc(v_ps, 1)
                    t.wait_ge(qk_sq, 1)
                    for s in range(2):
                        for k in range(2):
                            mm = t.matmul(PS[:, 2 * s + k, :], K["sum8"][:, :],
                                          sq[:, s, BANK * k:BANK * k + BANK], start=True, stop=True)
                    mm.then_inc(qk_ns, 1)

                    t.wait_ge(qk_done, 1)
                    t.wait_ge(w_sb, 2)
                    for b in range(NB):
                        for mt in range(2):
                            c = (b * 2 + mt) * 128
                            mm = t.transpose(PS[:, 6 + c // BANK, c % BANK:c % BANK + 128],
                                             qk[:, 1, b * NTOK + mt * 128:b * NTOK + mt * 128 + 128], K["ident"][:, :])
                    mm.then_inc(kt_ps, 1)
                    t.wait_ge(kt_sb, 1)
                    for b in range(NB):
                        for mt in range(2):
                            mm = t.matmul(PS[:, 0, 128 * b:128 * b + 128], KT[:, b, mt, :], KT[:, b, mt, :],
                                          start=(mt == 0), stop=(mt == 1))
                    mm.then_inc(cov_ps, 1)
                    t.wait_ge(cov_sb, 1)
                    for b in range(NB):
                        mm = t.matmul(PS[:, 2 + b // 2, NTOK * (b % 2):NTOK * (b % 2) + NTOK], COV[:, b, :],
                                      qk[:, 0, b * NTOK:b * NTOK + NTOK], start=True, stop=True)
                    mm.then_inc(cq_ps, 1)
                    t.wait_ge(cq_sb, 1)
                    for b in range(NB):
                        for nt in range(2):
                            tok = slice(b * NTOK + 128 * nt, b * NTOK + 128 * nt + 128)
                            o = (b * 2 + nt) * 16
                            t.matmul(PS[:, 0, o:o + 16], qk[:, 0, tok], KM[:, b, :], start=True, stop=True)
                            mm = t.matmul(PS[:, 1, o:o + 16], QCQ[:, tok], K["head"][:, :], start=True, stop=True)
                    mm.then_inc(row_ps, 1)

                @blk.vector
                def _(v):
                    v.wait_ge(raws, nraw[0])
                    v.tensor_copy(rawx[:, 0:3, :].rearrange("o s (d c) -> o s d c", d=2), rawq[:, :, :, :])
                    v.tensor_copy(rawx[:, 3, :].rearrange("o (d c) -> o d c", d=2), rawp[:, :, :])
                    for so in range(3):
                        v.tensor_copy(rawx[:, 4 + 3 * so:7 + 3 * so, :].rearrange("o i (d c) -> o i d c", d=2),
                                      rawpw[:, so, :, :, :].rearrange("o d i c -> o i d c"))
                    v.tensor_copy(rawx[:, 13:15, :].rearrange("o s (d c) -> o s d c", d=2), rawf1[:, :, :, :])
                    v.tensor_copy(rawx[:, 15:17, :].rearrange("o s (d c) -> o s d c", d=2), rawf2[:, :, :, :])
                    v.drain().then_inc(w_sb, 1)
                    v.wait_ge(loads, nload[0])
                    v.tensor_scalar(xh[:, :, :, :].rearrange("p b y x -> p (b y x)"), X[:, :], 0.5, None, ALU.mult)
                    v.drain()
                    q00, q10 = xh[:, :, 0:H:2, 0:W:2], xh[:, :, 1:H:2, 0:W:2]
                    q01, q11 = xh[:, :, 0:H:2, 1:W:2], xh[:, :, 1:H:2, 1:W:2]
                    v.tensor_tensor(su[0][:, :, :, :], q00, q10, ALU.add)
                    v.tensor_tensor(su[1][:, :, :, :], q01, q11, ALU.add)
                    v.tensor_tensor(su[2][:, :, :, :], q10, q00, ALU.subtract)
                    v.tensor_tensor(su[3][:, :, :, :], q11, q01, ALU.subtract)
                    v.drain()
                    v.wait_ge(ll_done, 1)
                    inner = [HI[:, s, :, 1:HW2 + 1, 1:HW2 + 1] for s in range(3)]
                    v.tensor_tensor(LL[:, :].rearrange("p (b y x) -> p b y x", b=NB, y=HW2), su[0][:, :, :, :],
                                    su[1][:, :, :, :], ALU.add)
                    v.tensor_tensor(inner[0], su[1][:, :, :, :], su[0][:, :, :, :], ALU.subtract)
                    v.tensor_tensor(inner[1], su[2][:, :, :, :], su[3][:, :, :, :], ALU.add)
                    v.tensor_tensor(inner[2], su[3][:, :, :, :], su[2][:, :, :, :], ALU.subtract)
                    v.drain().then_inc(ll_done, 1)
                    for i, n in enumerate(("he_gn1_g", "he_gn1_b", "he_gn2_g", "he_gn2_b")):
                        v.tensor_copy(V12t[:, i, :, :], v0(n, NB))
                    for i, n in enumerate(("ffn_gn1_g", "ffn_gn1_b")):
                        v.tensor_copy(VFt[:, i, :, :], v0(n, NB))
                    v.wait_ge(w_ps, 1)
                    for h in range(HALVES):
                        for c in range(3):
                            n = min(8, 17 - 8 * c)
                            v.tensor_scalar(W0[:, 8 * c:8 * c + n, 64 * h:64 * h + 64],
                                            PS[:, 5 + c, 0:64 * n].rearrange("p (s o) -> p s o", o=64),
                                            K["half_nat"][:, h:h + 1], None, ALU.mult)
                    v.drain().then_inc(w_sb, 1)
                    v.wait_ge(qk_ps, 1)
                    v.tensor_copy(qk, PS[:, 0:4, :].rearrange("p (a k) f -> p a (k f)", k=2))
                    v.drain()
                    v.tensor_tensor(sq[:, :, :], qk[:, :, :], qk[:, :, :], ALU.mult)
                    v.drain().then_inc(qk_sq, 1)
                    v.wait_ge(v_ps, 1)
                    for h in range(HALVES):
                        for mt in range(2):
                            v.tensor_copy(VT[:, h:NB * HALVES:2, :, mt, :],
                                          PS[:, 4 + h, :].rearrange("p (n m e d) -> p n m e d", n=4, m=2, d=HD)[:, :, mt])
                    v.drain().then_inc(v_done, 1)
                    v.wait_ge(qk_nrm, 1)
                    v.tensor_scalar(sq[:, :, :], sq[:, :, :], 1e-12, None, ALU.max)
                    v.drain()
                    v.reciprocal(sq[:, :, :], sq[:, :, :])
                    v.drain()
                    v.tensor_tensor(qk[:, :, :], qk[:, :, :], sq[:, :, :], ALU.mult)
                    v.drain().then_inc(qk_done, 1)

                    for b in range(NB):
                        v.tensor_reduce(ksum[:, b:b + 1], qk[:, 1, b * NTOK:b * NTOK + NTOK], AX.X, ALU.add)
                    v.drain()
                    v.tensor_scalar(ksum[:, :], ksum[:, :], 1.0 / NTOK, None, ALU.mult)
                    v.drain()
                    for b in range(NB):
                        v.tensor_scalar(KM[:, b, :], K["head"][:, :], ksum[:, b:b + 1], None, ALU.mult)
                    v.wait_ge(cov_ps, 1)
                    v.scalar_tensor_tensor(out=COV[:, :, :], in0=PS[:, 0, :].rearrange("p (b c) -> p b c", b=NB),
                                           scalar=1.0 / NTOK,
                                           in1=K["sum8"][:, :].unsqueeze(1).broadcast_to([128, NB, 128]),
                                           op0=ALU.mult, op1=ALU.mult)
                    v.drain().then_inc(cov_sb, 1)
                    v.wait_ge(cq_ps, 1)
                    v.tensor_tensor(QCQ[:, :], qk[:, 0, :], PS[:, 2:4, :].rearrange("p a f -> p (a f)"), ALU.mult)
                    v.drain().then_inc(cq_sb, 1)
                    v.wait_ge(row_ps, 1)

                    def by_group(t, b):
                        return t[:, 32 * b:32 * b + 32].rearrange("p (h n) -> p h n", n=2)

                    def by_tile(k, b):
                        return PS[:, k, 32 * b:32 * b + 32].rearrange("p (n h) -> p h n", n=2)
                    for b in range(NB):
                        v.tensor_copy(by_group(START, b), by_tile(0, b))
                        v.tensor_copy(by_group(row_sq, b), by_tile(1, b))
                    v.drain()
                    v.tensor_tensor(COUNT[:, :], START[:, :], START[:, :], ALU.mult)
                    v.drain()
                    v.tensor_tensor(row_sq[:, :], row_sq[:, :], COUNT[:, :], ALU.subtract)
                    v.drain()
                    v.tensor_scalar(row_sq[:, :], row_sq[:, :], 0.0, None, ALU.max)
                    v.tensor_scalar(START[:, :], START[:, :], float(HD) ** -0.5, None, ALU.mult)
                    v.drain().then_inc(dev_in, 1)
                    v.wait_ge(dev_done, 1)
                    v.scalar_tensor_tensor(out=START[:, :], in0=SLOPE[:, :], scalar=float(TOPK - AIM),
                                           in1=START[:, :], op0=ALU.mult, op1=ALU.add)
                    v.drain()

        phase(attention, recycle=True)

        def attend(st, sb, sem, exact):
            staged, s_ps, s_sb, s_used, e_done, p_done, pt_ps, pt_sb, o_ps, o_done, redo_in, redo_ps = (
                sem(n) for n in ("staged", "s_ps", "s_sb", "s_used", "e_done", "p_done", "pt_ps", "pt_sb", "o_ps",
                                 "o_done", "redo_in", "redo_ps"))
            stage = sb("stage", [128, 2, 2, 128])
            S = sb("S", [128, 4, NTOK])
            WK = sb("WK", [128, 4, NTOK])
            E = sb("E", [128, 4, NTOK])
            P = sb("P", [128, 4, NTOK])
            PT = sb("PT", [128, 4, NTOK])
            IND = sb("IND", [128, 4, NTOK])
            signs = sb("signs", [128, 4, NTOK])
            above = sb("above", [128, 4])
            thr, neg = sb("thr", [128, 4]), sb("neg", [128, 4])
            cnt, need = sb("cnt", [128, 4]), sb("need", [128, 4])
            spare = sb("spare", [128, 4, 8 * ROUNDS])
            top = sb("top", [128, 4, 8])
            mark = sb("mark", [128, 1])
            rs = sb("rs", [128, 4])
            ri = sb("ri", [128, 4])
            missed = sb("missed", [128, 4 * GROUPS])
            n_missed = sb("n_missed", [128, 1])
            ones = sb("ones", [128, 128])
            if not exact:
                ahead, zeroed, cleared = sem("ahead"), sem("zeroed"), sem("cleared")
                zero = sb("zero", [128, HALVES * DG * NENT * CG // 128])

            def flat(t):
                return t[:, :, :].rearrange("p u n -> p (u n)")

            with nc.Block() as blk:
                if exact:
                    @blk.sync
                    def _(sp):
                        sp.drain()

                    @blk.gpsimd
                    def _(g):
                        g.drain()
                else:
                    @blk.gpsimd
                    def _(g):
                        g.memset(zero[:, :], 0.0)
                        g.drain().then_inc(zeroed, 1)

                    @blk.sync
                    def _(sp):
                        n = [0]

                        def load(dst, src):
                            sp.dma_start(dst, src).then_inc(ahead, 16)
                            n[0] += 16
                        for q, name in enumerate(("conv1_w", "add1_w", "conv2_w", "add2_w")):
                            w = A["L1_conv_" + name].rearrange("o c ky kx -> o c (ky kx)")
                            for h in range(HALVES):
                                if q == 2:
                                    load(RAW1[:, q, :, :].rearrange("o (j h i) t -> o j h (i t)", j=NJ, h=2)[:, :, h],
                                         w.rearrange("o (j i) t -> o j (i t)", i=NI))
                                else:
                                    load(RAW1[:, q, 64 * h:64 * h + 64, :], w)
                        for i, name in enumerate(("bn1_g", "bn1_b", "bn2_g", "bn2_b")):
                            for j in range(NJ):
                                for h in range(HALVES):
                                    r = 32 * j + NI * h
                                    load(BNV[r:r + NI, i:i + 1], halves(A["L1_conv_" + name][NI * j:NI * j + NI]))
                        for h in range(HALVES):
                            for i in range(2):
                                load(RAW2[:, i, 64 * h:64 * h + 64, :],
                                     A[f"L2_conv_w{i + 1}"].rearrange("o c ky kx -> o c (ky kx)"))
                                for f, name in enumerate(("gamma", "beta", "mean", "var")):
                                    load(BV2[64 * h:64 * h + 64, f, i:i + 1], halves(A[f"L2_conv_{name}{i + 1}"]))
                            for i, name in enumerate(("rb_bn1", "rb_bn2", "bn1", "bn2")):
                                for f in range(4):
                                    load(BV3[64 * h:64 * h + 64, f, i:i + 1],
                                         A["L3_conv_" + name][f:f + 1, :].rearrange("one c -> c one"))
                            for i, name in ((0, "rb_b1"), (1, "rb_b2"), (2, "dc_b"), (4, "off_b")):
                                m = A["L3_conv_" + name].shape[0]
                                load(BIAS3[64 * h:64 * h + m, i:i + 1], halves(A["L3_conv_" + name]))
                        sp.wait_ge(zeroed, 1)
                        for table in tables:
                            for part in table.rearrange("r f -> (r f)").rearrange("(n p f) -> n p f", n=4, p=128):
                                sp.dma_start(part, zero[:, :]).then_inc(cleared, 16)
                        sp.wait_ge(ahead, n[0])
                        sp.wait_ge(cleared, 16 * 4 * NB)

                @blk.scalar
                def _(a):
                    def queries(g):
                        for par in range(2):
                            b, hh = (g >> 3), (g & 7)
                            a.activation(stage[:, par, :, :], qk_all[:, 0, ds(b * NTOK, NTOK)]
                                         .rearrange("p (t n) -> p t n", t=2), ACT.Copy,
                                         scale=K["head"][:, ds(hh * 2 + par, 1)])
                        a.drain().then_inc(staged, 1)
                        a.wait_ge(s_ps, g + 1)
                        a.activation(flat(S), PS[:, 0:2, :].rearrange("p a f -> p (a f)"), ACT.Copy,
                                     scale=float(HD) ** -0.5)
                        if not exact:
                            a.activation(neg[:, :], START[:, ds(g * 4, 4)], ACT.Copy, scale=-1.0)
                            a.drain()
                            for u in range(4):
                                a.activation(signs[:, u, :], S[:, u, :], ACT.Sign, bias=neg[:, u:u + 1],
                                             accum_out=above[:, u:u + 1])
                        a.drain().then_inc(s_sb, 1)

                    def probs(g, more):
                        a.wait_ge(p_done, g + 1)
                        a.activation(flat(E), flat(S), ACT.Exp)
                        a.drain().then_inc(e_done, 1)
                        a.wait_ge(s_used, g + 1)
                        if more:
                            queries(g + 1)
                        a.wait_ge(pt_ps, g + 2)
                        a.activation(flat(PT), PS[:, 2:4, :].rearrange("p a f -> p (a f)"), ACT.Copy).then_inc(pt_sb, 1)
                        a.wait_ge(o_ps, g + 1)
                        for par in range(2):
                            for nt in range(2):
                                u = 2 * par + nt
                                a.activation(O[:, nt, ds(g * 16 + par * HD, HD)], PS[:, 4, 64 * u:64 * u + HD],
                                             ACT.Copy, scale=ri[:, u:u + 1])
                        a.drain().then_inc(o_done, 1)

                    queries(0)
                    with a.Fori(0, GROUPS - 1, 1) as g:
                        probs(g, True)
                    probs(GROUPS - 1, False)

                @blk.tensor
                def _(t):
                    t.sem_inc(pt_ps, 1)
                    t.sem_inc(o_done, 1)
                    t.sem_inc(p_done, 1)

                    def scores(g):
                        t.wait_ge(staged, g + 1)
                        for par in range(2):
                            for nt in range(2):
                                mm = t.matmul(PS[:, par, NTOK * nt:NTOK * nt + NTOK], stage[:, par, nt, :],
                                              qk_all[:, 1, ds((g >> 3) * NTOK, NTOK)], start=True, stop=True)
                        mm.then_inc(s_ps, 1)

                    def values(g):
                        t.wait_ge(p_done, g + 2)
                        for u in range(4):
                            for mt in range(2):
                                c = 256 * (u % 2) + 128 * mt
                                mm = t.transpose(PS[:, 2 + u // 2, c:c + 128], P[:, u, 128 * mt:128 * mt + 128],
                                                 K["ident"][:, :])
                        mm.then_inc(pt_ps, 1)
                        t.wait_ge(pt_sb, g + 1)
                        for par in range(2):
                            for nt in range(2):
                                u = 2 * par + nt
                                for mt in range(2):
                                    mm = t.matmul(PS[:, 4, 64 * u:64 * u + HD], PT[:, u, 128 * mt:128 * mt + 128],
                                                  VTf[:, ds(g * 32 + par * 16 + mt * HD, HD)],
                                                  start=(mt == 0), stop=(mt == 1))
                        mm.then_inc(o_ps, 1)

                    scores(0)
                    with t.Fori(0, GROUPS - 1, 1) as g:
                        t.wait_ge(s_sb, g + 1)
                        scores(g + 1)
                        values(g)
                    values(GROUPS - 1)
                    if not exact:
                        t.wait_ge(redo_in, 1)
                        t.matmul(PS[:, 5, 0:1], ones[:, :], n_missed[:, :], start=True, stop=True).then_inc(redo_ps, 1)

                @blk.vector
                def _(v):
                    def take_all(g):
                        for u in range(4):
                            v.max(top[:, u, :], S[:, u, :])
                        v.drain()
                        for r in range(TOPK // 8):
                            if r:
                                for u in range(4):
                                    v.max(top[:, u, :], WK[:, u, :])
                                v.drain()
                            for u in range(4):
                                v.match_replace(out=WK[:, u, :], in_to_replace=top[:, u, :],
                                                in_values=(WK if r else S)[:, u, :], imm_value=TAKEN)
                            if r == 0:
                                v.drain().then_inc(s_used, 1)
                            else:
                                v.drain()

                    def take_above(g):
                        v.tensor_scalar(cnt[:, :], above[:, :], 0.5, float(NTOK // 2 - AIM), ALU.mult, ALU.add)
                        v.drain()
                        v.tensor_tensor(cnt[:, :], cnt[:, :], SLOPE[:, ds(g * 4, 4)], ALU.mult)
                        v.drain()
                        v.tensor_tensor(thr[:, :], START[:, ds(g * 4, 4)], cnt[:, :], ALU.add)
                        v.drain()
                        for u in range(4):
                            v.tensor_scalar(IND[:, u, :], S[:, u, :], thr[:, u:u + 1], 0.0, ALU.is_ge, ALU.add,
                                            accum_out=cnt[:, u:u + 1])
                        v.drain()
                        v.tensor_scalar(need[:, :], cnt[:, :], -1.0, float(TOPK), ALU.mult, ALU.add)
                        v.tensor_copy(COUNT[:, ds(g * 4, 4)], cnt[:, :])
                        v.scalar_tensor_tensor(out=flat(WK), in0=flat(IND), scalar=TAKEN, in1=flat(S),
                                               op0=ALU.mult, op1=ALU.add)
                        v.drain().then_inc(s_used, 1)
                        for u in range(4):
                            v.max(top[:, u, :], WK[:, u, :])
                        v.tensor_tensor(spare[:, :, :], K["slots"][:, :].rearrange("p (u s) -> p u s", u=4),
                                        need[:, :].unsqueeze(2).broadcast_to([128, 4, 8 * ROUNDS]), ALU.is_ge)
                        v.drain()
                        for r in range(ROUNDS):
                            if r:
                                for u in range(4):
                                    v.max(top[:, u, :], WK[:, u, :])
                                v.drain()
                            v.scalar_tensor_tensor(out=top[:, :, :], in0=spare[:, :, 8 * r:8 * r + 8], scalar=TAKEN,
                                                   in1=top[:, :, :], op0=ALU.mult, op1=ALU.add)
                            v.drain()
                            for u in range(4):
                                v.match_replace(out=WK[:, u, :], in_to_replace=top[:, u, :],
                                                in_values=WK[:, u, :], imm_value=TAKEN)
                            v.drain()

                    def select(g):
                        v.wait_ge(s_sb, g + 1)
                        v.memset(mark[:, :], 0.0)
                        (take_all if exact else take_above)(g)
                        v.wait_ge(e_done, g + 1)
                        v.wait_ge(pt_ps, g + 1)
                        for u in range(4):
                            v.scalar_tensor_tensor(out=P[:, u, :], in0=WK[:, u, :], scalar=TAKEN / 2,
                                                   in1=E[:, u, :], op0=ALU.is_lt, op1=ALU.mult,
                                                   accum_out=rs[:, u:u + 1])
                        v.drain()
                        v.wait_ge(o_done, g + 1)
                        v.reciprocal(ri[:, :], rs[:, :])
                        v.drain().then_inc(p_done, 1)

                    with v.Fori(0, GROUPS, 1) as g:
                        select(g)
                    if not exact:
                        v.memset(ones[:, :], 1.0)
                        v.tensor_scalar(missed[:, :], COUNT[:, :], float(TOPK), None, ALU.is_gt)
                        v.tensor_scalar(COUNT[:, :], COUNT[:, :], float(TOPK - 8 * ROUNDS), None, ALU.is_lt)
                        v.drain()
                        v.tensor_tensor(missed[:, :], missed[:, :], COUNT[:, :], ALU.add)
                        v.drain()
                        v.tensor_reduce(n_missed[:, :], missed[:, :], AX.X, ALU.add)
                        v.drain().then_inc(redo_in, 1)
                        v.wait_ge(redo_ps, 1)
                        v.tensor_scalar(REDO[:, :], PS[:, 5, 0:1], 1.0, None, ALU.min)
                        v.drain()

        def top_k(st, sb, sem):
            attend(st, sb, sem, exact=False)

        phase(top_k)

        def top_k_exact(st, sb, sem):
            attend(st, sb, sem, exact=True)

        redo = nc.values_load(REDO[0:1, 0:1], min_val=0, max_val=1,
                              skip_runtime_bounds_check_because="the chip computes it as min(count, 1)")
        with nc.If(redo):
            phase(top_k_exact)

        def projection(st, sb, sem):
            at_ps, at_sb, pr_ps = sem("at_ps"), sem("at_sb"), sem("pr_ps")
            AO = sb("AO", [128, NB * NTOK])
            Y = sb("Y", [128, NB, NTOK])
            gn = Stats(sem, sb, "gn", NB, PS[:, 7, :])
            st6 = sb("st6", [128, NB, 6])
            with nc.Block() as blk:
                @blk.scalar
                def _(a):
                    a.wait_ge(at_ps, 1)
                    a.activation(AO[:, :], PS[:, 0:2, :].rearrange("p a f -> p (a f)"), ACT.Copy).then_inc(at_sb, 1)
                    gn.act(a, NB)

                @blk.tensor
                def _(t):
                    for b in range(NB):
                        for nt in range(2):
                            c = b * NTOK + nt * 128
                            mm = t.transpose(PS[:, c // BANK, c % BANK:c % BANK + 128],
                                             O[:, nt, b * 128:b * 128 + 128], K["ident"][:, :])
                    mm.then_inc(at_ps, 1)
                    t.wait_ge(at_sb, 1)
                    for k in range(2):
                        mm = t.matmul(PS[:, 2 + k, :], W0[:, 3, :], AO[:, BANK * k:BANK * k + BANK],
                                      start=True, stop=True)
                    mm.then_inc(pr_ps, 1)
                    gn.pe(t, NB, K["mean4"][:, :])

                @blk.vector
                def _(v):
                    v.wait_ge(pr_ps, 1)
                    v.tensor_copy(Y[:, :, :].rearrange("p b f -> p (b f)"),
                                  PS[:, 2:4, :].rearrange("p a f -> p (a f)"))
                    v.drain()
                    for b in range(NB):
                        v.bn_stats(st6[:, b, :], Y[:, b, :])
                    v.drain()
                    for b in range(NB):
                        v.bn_aggr(gn.mv[:, b, :], st6[:, b, :])
                    gn.dve(v, NB, v0("attn_gn_g", NB)[:, 0, :], v0("attn_gn_b", NB)[:, 0, :], 1e-6)
                    for b in range(NB):
                        v.tensor_scalar(Y[:, b, :], Y[:, b, :], gn.scale[:, b:b + 1], gn.bias[:, b:b + 1],
                                        ALU.mult, ALU.add)
                    v.drain()
                    v.tensor_tensor(LL[:, :], LL[:, :], Y[:, :, :].rearrange("p b f -> p (b f)"), ALU.add)
                    v.drain()

        phase(projection)
        atn.close()


        def high_bands(st, sb, sem):
            dw = sb("dw", [128, 3, NB, HW2, HW2])
            dwf = dw[:, :, :, :, :].rearrange("p s b y x -> p s b (y x)")
            act = sb("act", [128, 3, NB, NTOK])
            y2 = sb("y2", [128, 3, NB, NTOK])
            st6 = sb("st6", [128, 12, 6])
            gn = Stats(sem, sb, "gn", 12, PS[:, 7, :])
            silu_in, silu_done, pw_ps = sem("silu_in"), sem("silu_done"), sem("pw_ps")

            def stats(v, t):
                for m in range(12):
                    v.bn_stats(st6[:, m, :], t[:, m // NB, m % NB, :])
                v.drain()
                for m in range(12):
                    v.bn_aggr(gn.mv[:, m, :], st6[:, m, :])

            with nc.Block() as blk:
                @blk.vector
                def _(v):
                    for tap in range(TAPS):
                        for s in range(3):
                            seen = HI[:, s, :, tap // 3:tap // 3 + HW2, tap % 3:tap % 3 + HW2]
                            if tap == 0:
                                v.tensor_scalar(dw[:, s], seen, HE[:, s, tap:tap + 1], None, ALU.mult)
                            else:
                                for b in range(NB):
                                    v.scalar_tensor_tensor(out=dw[:, s, b], in0=seen[:, b],
                                                           scalar=HE[:, s, tap:tap + 1], in1=dw[:, s, b],
                                                           op0=ALU.mult, op1=ALU.add)
                        v.drain()
                    stats(v, dwf)
                    gn.dve(v, 12, V12["g"], V12["b"], 1e-6)
                    v.drain().then_inc(silu_in, 1)
                    v.wait_ge(pw_ps, 1)
                    v.tensor_copy(y2[:, :, :, :].rearrange("p s b f -> p (s b f)"),
                                  PS[:, 0:6, :].rearrange("p a f -> p (a f)"))
                    v.drain()
                    stats(v, y2)
                    gn.dve(v, 12, V12["g2"], V12["b2"], 1e-6, n=1)
                    al = V0[:, vec["alpha"][0]:vec["alpha"][0] + 1]
                    v.tensor_scalar(gn.scale[:, :], gn.scale[:, :], al, None, ALU.mult)
                    v.tensor_scalar(gn.bias[:, :], gn.bias[:, :], al, None, ALU.mult)
                    v.drain()
                    for m in range(12):
                        t = y2[:, m // NB, m % NB, :]
                        v.tensor_scalar(t, t, gn.scale[:, m:m + 1], gn.bias[:, m:m + 1], ALU.mult, ALU.add)
                    v.drain()
                    y5 = y2[:, :, :, :].rearrange("p s b (y x) -> p s b y x", y=HW2)
                    for s in range(3):
                        v.tensor_tensor(y5[:, s], y5[:, s], HI[:, s, :, 1:HW2 + 1, 1:HW2 + 1], ALU.add)
                    v.drain()
                    ll = LL[:, :].rearrange("p (b f) -> p b f", b=NB)
                    lh, hl, hh = (y2[:, s] for s in range(3))
                    t0, t1, t2, t3 = act[:, 0], act[:, 1], act[:, 2], dwf[:, 0]
                    v.tensor_tensor(t0, ll, lh, ALU.subtract)
                    v.tensor_tensor(t1, hl, hh, ALU.subtract)
                    v.tensor_tensor(t2, ll, lh, ALU.add)
                    v.tensor_tensor(t3, hl, hh, ALU.add)
                    v.drain()
                    r = dwf[:, 1]
                    r4 = dw[:, 1]
                    for dy, dx, p, q, op in ((0, 0, t0, t1, ALU.subtract), (1, 0, t0, t1, ALU.add),
                                             (0, 1, t2, t3, ALU.subtract), (1, 1, t2, t3, ALU.add)):
                        v.tensor_tensor(r, p, q, op)
                        v.drain()
                        for b in range(NB):
                            at = X4[:, b, dy:H:2, dx:W:2]
                            v.scalar_tensor_tensor(out=at, in0=r4[:, b], scalar=0.1, in1=at, op0=ALU.mult,
                                                   op1=ALU.add)
                        v.drain()

                @blk.scalar
                def _(a):
                    gn.act(a, 12)
                    a.wait_ge(silu_in, 1)
                    for m in range(12):
                        a.activation(act[:, m // NB, m % NB, :], dwf[:, m // NB, m % NB, :], ACT.Silu,
                                     scale=gn.scale[:, m:m + 1], bias=gn.bias[:, m:m + 1])
                    a.drain().then_inc(silu_done, 1)
                    gn.act(a, 12, n=1)

                @blk.tensor
                def _(t):
                    gn.pe(t, 12, K["mean8"][:, :])
                    t.wait_ge(silu_done, 1)
                    flat = act[:, :, :, :].rearrange("p s b f -> p s (b f)")
                    for so in range(3):
                        for k in range(2):
                            for si in range(3):
                                mm = t.matmul(PS[:, 2 * so + k, :], W0[:, 4 + 3 * so + si, :],
                                              flat[:, si, BANK * k:BANK * k + BANK], start=(si == 0), stop=(si == 2))
                    mm.then_inc(pw_ps, 1)
                    gn.pe(t, 12, K["mean8"][:, :], n=1)

        phase(high_bands)

        def feed_forward(st, sb, sem):
            f1 = sb("f1", [128, 2, NB * PX])
            f2 = sb("f2", [128, NB * PX])
            st6 = sb("st6", [128, 16, 6])
            gn = Stats(sem, sb, "gn", 8, PS[:, 7, :])
            f_ps, f_sb, gelu_in, gelu_done, r_ps, r_sb = (sem(n) for n in ("f_ps", "f_sb", "gelu_in", "gelu_done",
                                                                          "r_ps", "r_sb"))
            with nc.Block() as blk:
                @blk.tensor
                def _(t):
                    for u in range(16):
                        if u >= 7:
                            t.wait_ge(f_sb, u - 6)
                        t.matmul(PS[:, u % 7, :], W0[:, 13 + u // 8, :], X[:, BANK * (u % 8):BANK * (u % 8) + BANK],
                                 start=True, stop=True).then_inc(f_ps, 1)
                    gn.pe(t, 8, K["mean8"][:, :])
                    t.wait_ge(f_sb, 16)
                    for k in range(NBANK):
                        t.wait_ge(gelu_done, k // 2 + 1)
                        if k >= 7:
                            t.wait_ge(r_sb, k - 6)
                        for e in range(2):
                            mm = t.matmul(PS[:, k % 7, :], W0[:, 15 + e, :], f1[:, e, BANK * k:BANK * k + BANK],
                                          start=(e == 0), stop=(e == 1))
                        mm.then_inc(r_ps, 1)
                    gn.pe(t, 4, K["mean4"][:, :], n=1)

                @blk.scalar
                def _(a):
                    for u in range(16):
                        a.wait_ge(f_ps, u + 1)
                        a.activation(f1[:, u // 8, BANK * (u % 8):BANK * (u % 8) + BANK], PS[:, u % 7, :],
                                     ACT.Copy).then_inc(f_sb, 1)
                    gn.act(a, 8)
                    a.wait_ge(gelu_in, 1)
                    for b in range(NB):
                        for e in range(2):
                            m = e * NB + b
                            t = f1[:, e, PX * b:PX * b + PX]
                            a.activation(t, t, ACT.Gelu, scale=gn.scale[:, m:m + 1], bias=gn.bias[:, m:m + 1])
                        a.drain().then_inc(gelu_done, 1)
                    for k in range(NBANK):
                        a.wait_ge(r_ps, k + 1)
                        a.activation(f2[:, BANK * k:BANK * k + BANK], PS[:, k % 7, :], ACT.Copy).then_inc(r_sb, 1)
                    gn.act(a, 4, n=1)

                @blk.vector
                def _(v):
                    for u in range(16):
                        v.wait_ge(f_sb, u + 1)
                        v.bn_stats(st6[:, u, :], f1[:, u // 8, BANK * (u % 8):BANK * (u % 8) + BANK])
                    v.drain()
                    for m in range(8):
                        v.bn_aggr(gn.mv[:, m, :], st6[:, 2 * m:2 * m + 2, :].rearrange("p a b -> p (a b)"))
                    gn.dve(v, 8, VF["g"], VF["b"], 1e-6)
                    v.drain().then_inc(gelu_in, 1)
                    for k in range(NBANK):
                        v.wait_ge(r_sb, k + 1)
                        v.bn_stats(st6[:, k, :], f2[:, BANK * k:BANK * k + BANK])
                    v.drain()
                    for m in range(4):
                        v.bn_aggr(gn.mv[:, m, :], st6[:, 2 * m:2 * m + 2, :].rearrange("p a b -> p (a b)"))
                    gn.dve(v, 4, v0("ffn_gn2_g", NB)[:, 0, :], v0("ffn_gn2_b", NB)[:, 0, :], 1e-6, n=1)
                    for b in range(NB):
                        t = f2[:, PX * b:PX * b + PX]
                        v.tensor_scalar(t, t, gn.scale[:, b:b + 1], gn.bias[:, b:b + 1], ALU.mult, ALU.add)
                    v.drain()
                    v.scalar_tensor_tensor(out=X[:, :], in0=f2[:, :], scalar=0.1, in1=X[:, :], op0=ALU.mult,
                                           op1=ALU.add)
                    v.drain()
                    v.tensor_copy(XPin, X4)
                    v.drain()

        phase(feed_forward)
        lay0.close()


        lay1 = ExitStack()
        outer.enter_context(lay1)

        def l1(n, s):
            return lay1.enter_context(nc.sbuf_tensor(n, s, F32))

        WC = [l1(f"WC{i}", [128, TAPS, 128]) for i in range(2)]
        AW = [l1(f"AW{i}", [128, TAPS, CH]) for i in range(2)]
        AN = [l1(f"AN{i}", [128, TAPS, CH]) for i in range(2)]
        WSUM = [l1(f"WSUM{i}", [128, 128]) for i in range(2)]

        def block_weights(v, dst, ps9, masks, cols=CH):
            for h in range(HALVES):
                v.tensor_scalar(dst[:, :, 64 * h:64 * h + cols], ps9, K[masks][:, h:h + 1], None, ALU.mult)

        def adder_weights(st, sb, sem):
            loads, w_ps = sem("loads"), sem("w_ps")
            total = sb("total", [128, CH])
            sign, signed = sb("sign", [128, TAPS * CH]), sb("signed", [128, TAPS, CH])
            with nc.Block() as blk:
                @blk.sync
                def _(sp):
                    sp.dma_start(sign[:, :], C["adder_sign"]).then_inc(loads, 16)
                    sp.wait_ge(loads, 16)

                @blk.gpsimd
                def _(g):
                    g.wait_ge(w_ps, 4)
                    g.memset(P2[:, :, :, :], 0.0)
                    g.drain()

                @blk.tensor
                def _(t):
                    for q in range(4):
                        for tap in range(TAPS):
                            mm = t.matmul(PS[:, 2 * q + tap // 8, 64 * (tap % 8):64 * (tap % 8) + 64],
                                          RAW1[:, q, :, tap], K["ident"][0:64, 0:64], start=True, stop=True)
                        mm.then_inc(w_ps, 1)

                @blk.vector
                def _(v):
                    for q in range(4):
                        ps9 = PS[:, 2 * q:2 * q + 2, :].rearrange("p a (t o) -> p (a t) o", o=CH)[:, 0:TAPS, :]
                        v.wait_ge(w_ps, q + 1)
                        i = q // 2
                        if q % 2 == 0:
                            block_weights(v, WC[i], ps9, "half_perm" if q else "half_nat")
                            continue
                        v.tensor_copy(AW[i][:, :, :], ps9)
                        v.tensor_scalar(AN[i][:, :, :], ps9, -1.0, None, ALU.mult)
                        v.drain()
                        v.wait_ge(loads, 16)
                        v.tensor_tensor(signed[:, :, :].rearrange("p t o -> p (t o)"),
                                        AN[i][:, :, :].rearrange("p t o -> p (t o)"), sign[:, :], ALU.mult)
                        v.drain()
                        v.tensor_reduce(total[:, :], signed[:, :, :].rearrange("p t o -> p o t"), AX.X, ALU.add)
                        v.drain()
                        for h in range(HALVES):
                            v.tensor_scalar(WSUM[i][:, :].rearrange("p (j h i) -> p j h i", j=NJ, h=2)[:, :, h],
                                            total[:, :].rearrange("p (j i) -> p j i", i=NI),
                                            K["half_nat"][:, h:h + 1], None, ALU.mult)
                    v.drain()

        phase(adder_weights)

        def adder_layer(layer, src):
            def run(st, sb, sem):
                CP = sb("CP", [128, NB, HP, WP])
                Z = sb("Z", [128, SLOTS, NJ, CHUNK * PX])
                BOX = P2[:, :, 1:H + 1, 1:W + 1]
                SO_all = XP[:, :, :, :].rearrange("p b y x -> p (b y x)")
                rowsum = SO_all[:, 0:NB * HP * W].rearrange("p (b y x) -> p b y x", b=NB, x=W)
                SO = SO_all[:, 0:NB * PX]
                st6 = sb("st6", [128, NBANK, 6])
                ones = sb("ones", [128, BANK])
                gn = Stats(sem, sb, "gn", 1, PS[:, 0, :])
                ready, c_ps, c_sb, box = sem("ready"), sem("c_ps"), sem("c_sb"), sem("box")
                z_dve, z_act = sem("z_dve"), sem("z_act")
                z_free = [sem(f"z_free{i}") for i in range(SLOTS)]
                s_ps, s_sb, normed, nat_ps, border = (sem(n) for n in ("s_ps", "s_sb", "normed", "nat_ps", "border"))
                CBANK = CHUNK * PX // BANK
                AWf = AW[layer][:, :, :].rearrange("p t o -> p (t o)")
                ANf = AN[layer][:, :, :].rearrange("p t o -> p (t o)")

                rows = adder_rows()
                mine = {e: [sum(any(m[2] == e for m in row) for row in rows[:r + 1]) for r in range(len(rows))]
                        for e in ("dve", "act")}

                def made(ch, ty, r, engine):
                    return ty * mine[engine][-1] + (ch * 3 * mine[engine][-1] + mine[engine][r])

                def use(ch, ty, r):
                    return ty * (len(rows) // SLOTS) + (ch * 3 * (len(rows) // SLOTS) + r // SLOTS + 1)

                def seen(ch, ty, tx):
                    return CP[:, CHUNK * ch:CHUNK * ch + CHUNK, ds(ty, H), tx:tx + W]

                def z(r, j):
                    return Z[:, r % SLOTS, j, :].rearrange("p (b y x) -> p b y x", b=CHUNK, y=H)

                def weight(ty, tx, j, i):
                    return ds(ty * 3 * CH + (tx * CH + NI * j + i), 1)

                with nc.Block() as blk:
                    @blk.gpsimd
                    def _(g):
                        g.memset(CP[:, :, :, :], 0.0)
                        g.memset(ones[:, :], 1.0)
                        g.drain().then_inc(ready, 1)
                        g.wait_ge(c_sb, NBANK)
                        g.tensor_tensor(rowsum, CP[:, :, :, 0:W], CP[:, :, :, 1:W + 1], ALU.add).then_inc(box, 1)
                        g.wait_ge(box, 1)
                        g.tensor_tensor(rowsum, rowsum, CP[:, :, :, 2:W + 2], ALU.add).then_inc(box, 1)
                        g.wait_ge(box, 2)
                        g.tensor_tensor(BOX[:, :, :, :], rowsum[:, :, 0:H], rowsum[:, :, 1:H + 1], ALU.add)\
                         .then_inc(box, 1)
                        g.wait_ge(box, 3)
                        g.tensor_tensor(BOX[:, :, :, :], BOX[:, :, :, :], rowsum[:, :, 2:H + 2], ALU.add)\
                         .then_inc(box, 1)
                        if layer:
                            g.wait_ge(nat_ps, NBANK)
                            g.memset(XP[:, :, :, :], 0.0)
                            g.drain().then_inc(border, 1)

                    @blk.tensor
                    def _(t):
                        for slot in range(SLOTS):
                            t.sem_inc(z_free[slot], 1)
                        for k in range(NBANK):
                            for tap in range(TAPS):
                                mm = t.matmul(bank(k), WC[layer][:, tap, :], patch(src, k, tap), start=(tap == 0),
                                              stop=(tap == TAPS - 1))
                            mm.then_inc(c_ps, 1)
                        t.wait_ge(ready, 1)
                        for ch in range(NB // CHUNK):
                            banks = range(CBANK * ch, CBANK * ch + CBANK)
                            t.wait_ge(c_sb, CBANK * ch + CBANK)
                            for k in banks:
                                t.matmul(bank(k), WSUM[layer][:, :], ones[:, :], start=True, stop=False,
                                         skip_group_check=True)
                            with t.Fori(0, 3, 1) as ty:
                                for r, row in enumerate(rows):
                                    t.wait_ge(z_dve, made(ch, ty, r, "dve"))
                                    t.wait_ge(z_act, made(ch, ty, r, "act"))
                                    for k in banks:
                                        for j, (i, _, _) in enumerate(row):
                                            c = BANK * (k % CBANK)
                                            mm = t.matmul(PS[32 * j:32 * j + 32, k, :],
                                                          K["adder_out"][:, 32 * i:32 * i + 32],
                                                          Z[:, r % SLOTS, j, c:c + BANK], start=False, stop=False,
                                                          skip_group_check=True)
                                    mm.then_inc(z_free[r % SLOTS], 1)
                            t.wait_ge(box, 4)
                            for k in banks:
                                mm = t.matmul(bank(k), K["adder_x"][:, :], px_bank(BOX, k), start=False, stop=True,
                                              skip_group_check=True)
                            mm.then_inc(s_ps, 1)
                        gn.pe(t, 1, K["mean_pair"][:, :])
                        if layer:
                            t.wait_ge(normed, 1)
                            for k in range(NBANK):
                                t.matmul(bank(k), K["to_nat"][:, :], SO[:, BANK * k:BANK * k + BANK],
                                         start=True, stop=True).then_inc(nat_ps, 1)

                    @blk.scalar
                    def _(a):
                        a.wait_ge(ready, 1)
                        for k in range(NBANK):
                            a.wait_ge(c_ps, k + 1)
                            a.activation(px_bank(CP[:, :, 1:H + 1, 1:W + 1], k), bank2(k), ACT.Copy)\
                             .then_inc(c_sb, 1)
                        a.wait_ge(c_sb, NBANK)
                        for ch in range(NB // CHUNK):
                            with a.Fori(0, 3, 1) as ty:
                                for r, row in enumerate(rows):
                                    maps = [(j, i, taps[0]) for j, (i, taps, e) in enumerate(row) if e == "act"]
                                    if not maps:
                                        continue
                                    a.wait_ge(z_free[r % SLOTS], use(ch, ty, r))
                                    for j, i, tx in maps:
                                        op = a.activation(z(r, j), seen(ch, ty, tx), ACT.Relu,
                                                          bias=ANf[:, weight(ty, tx, j, i)])
                                    op.then_inc(z_act, 1)
                            a.wait_ge(s_ps, ch + 1)
                            for k in range(CBANK * ch, CBANK * ch + CBANK):
                                a.activation(SO[:, BANK * k:BANK * k + BANK], bank(k), ACT.Copy).then_inc(s_sb, 1)
                        gn.act(a, 1)
                        if not layer:
                            a.wait_ge(normed, 1)
                            for b in range(NB):
                                a.activation(P2[:, b, 1:H + 1, 1:W + 1],
                                             SO[:, PX * b:PX * b + PX].rearrange("p (y x) -> p y x", y=H), ACT.Relu,
                                             scale=gn.scale[:, 0:1], bias=gn.bias[:, 0:1])
                            a.drain()

                    @blk.vector
                    def _(v):
                        v.wait_ge(c_sb, NBANK)
                        for ch in range(NB // CHUNK):
                            with v.Fori(0, 3, 1) as ty:
                                for r, row in enumerate(rows):
                                    maps = [(j, i, taps) for j, (i, taps, e) in enumerate(row) if e == "dve"]
                                    if not maps:
                                        continue
                                    v.wait_ge(z_free[r % SLOTS], use(ch, ty, r))
                                    for j, i, taps in maps:
                                        op = v.tensor_scalar(z(r, j), seen(ch, ty, taps[0]),
                                                             AWf[:, weight(ty, taps[0], j, i)], 0.0,
                                                             ALU.subtract, ALU.max)
                                    for j, i, taps in maps:
                                        for tx in taps[1:]:
                                            v.drain()
                                            for b in range(CHUNK):
                                                op = v.scalar_tensor_tensor(
                                                    out=z(r, j)[:, b], in0=seen(ch, ty, tx)[:, b],
                                                    scalar=AWf[:, weight(ty, tx, j, i)], in1=z(r, j)[:, b],
                                                    op0=ALU.max, op1=ALU.add)
                                    op.then_inc(z_dve, 1)
                        for k in range(NBANK):
                            v.wait_ge(s_sb, k + 1)
                            v.bn_stats(st6[:, k, :], SO[:, BANK * k:BANK * k + BANK])
                        v.drain()
                        v.bn_aggr(gn.mv[:, 0, :], st6[:, :, :].rearrange("p a b -> p (a b)"))
                        gn.dve(v, 1, BNV[:, 2 * layer:2 * layer + 1], BNV[:, 2 * layer + 1:2 * layer + 2], 1e-5)
                        if not layer:
                            v.drain().then_inc(normed, 1)
                            return
                        v.tensor_scalar(SO, SO, gn.scale[:, 0:1], gn.bias[:, 0:1], ALU.mult, ALU.add)
                        v.drain().then_inc(normed, 1)
                        for k in range(NBANK):
                            v.wait_ge(nat_ps, k + 1)
                            v.tensor_tensor(X[:, BANK * k:BANK * k + BANK], bank(k), X[:, BANK * k:BANK * k + BANK],
                                            ALU.add)
                        v.drain()
                        v.tensor_scalar(X[:, :], X[:, :], 0.0, None, ALU.max)
                        v.drain()
                        v.wait_ge(border, 1)
                        v.tensor_copy(XPin, X4)
                        v.drain()
            run.__name__ = f"adder_layer{layer}"
            return run

        phase(adder_layer(0, XP))
        phase(adder_layer(1, P2))
        lay1.close()


        lay3 = ExitStack()
        outer.enter_context(lay3)

        def l3(n, s, d=F32):
            return lay3.enter_context(nc.sbuf_tensor(n, s, d))

        LEVELS = 15.0
        W1 = l3("W1", [128, TAPS, 128])
        W2 = l3("W2", [128, TAPS, 128], BF16)
        INV2, SHIFT2 = l3("INV2", [128, 2]), l3("SHIFT2", [128, 2])
        WB = [l3(f"WB{i}", [128, TAPS, 128]) for i in range(3)]
        INV, SHIFT = l3("INV", [128, 4]), l3("SHIFT", [128, 4])
        DC = l3("DC", [128, 5, CH])
        CV2 = l3("CV2", [128, 1, 128])
        AP = l3("AP", [128, NB, HP, WP], BF16)
        T1 = P2
        NG = STEPS * GK
        GR = l3("GR", [128, 3, NG])
        NOFF = 3 * GK

        def sampler_weights(st, sb, sem):
            raw = [sb(f"raw{i}", [64, 128, TAPS]) for i in range(3)]
            rawdc = sb("rawdc", [64, CH, TAPS])
            rawcv = sb("rawcv", [64, 128])
            dcs = sb("dcs", [64, GK, CG])
            big, row, top, rcp = (sb(n, x) for n, x in (("big", [64, 2]), ("row", [1, 2, 64]), ("top", [1, 2]),
                                                        ("rcp", [128, 2])))
            one = sb("one", [1, 128])
            root2, root3 = sb("root2", [128, 2]), sb("root3", [128, 4])
            loads, cleared, tanh, m_sb, m_ps, q_sb, root, rooted, split, w3_ps, w3_sb, w2_ps = (
                sem(n) for n in ("loads", "cleared", "tanh", "m_sb", "m_ps", "q_sb", "root", "rooted", "split",
                                 "w3_ps", "w3_sb", "w2_ps"))
            ws = ("rb_w1", "rb_w2", "off_w")
            nload = [0]
            with nc.Block() as blk:
                @blk.sync
                def _(sp):
                    def load(dst, src):
                        sp.dma_start(dst, src).then_inc(loads, 16)
                        nload[0] += 16
                    load(rawdc[:, :, :], A["L3_conv_dc_w"].rearrange("o c ky kx -> o c (ky kx)"))
                    for h in range(HALVES):
                        for i, n in enumerate(ws):
                            load(raw[i][0:A["L3_conv_" + n].shape[0], 64 * h:64 * h + 64, :],
                                 A["L3_conv_" + n].rearrange("o c ky kx -> o c (ky kx)"))
                        load(rawcv[:, 64 * h:64 * h + 64], A["L3_conv_cv2_w"].rearrange("o c ky kx -> o (c ky kx)"))
                    for i, g in enumerate(GRIDS):
                        load(GR[:, i, :], C[g])
                    sp.wait_ge(loads, nload[0])

                @blk.gpsimd
                def _(g):
                    g.memset(one[:, :], 1.0)
                    g.memset(WB[2][:, :, :], 0.0)
                    g.drain().then_inc(cleared, 1)
                    g.memset(AP[:, :, :, :], 0.0)
                    g.drain()

                @blk.scalar
                def _(a):
                    for i in range(2):
                        a.activation(RAW2[:, i, :, :], RAW2[:, i, :, :], ACT.Tanh)
                    a.drain().then_inc(tanh, 1)
                    a.wait_ge(root, 1)
                    a.activation(root2[:, :], INV2[:, :], ACT.Sqrt)
                    a.activation(root3[:, :], INV[:, :], ACT.Sqrt)
                    a.drain().then_inc(rooted, 1)

                @blk.tensor
                def _(t):
                    t.wait_ge(m_sb, 1)
                    for i in range(2):
                        mm = t.matmul(PS[0:1, 4, 64 * i:64 * i + 64], big[:, i:i + 1], K["ident"][0:64, 0:64],
                                      start=True, stop=True)
                    mm.then_inc(m_ps, 1)
                    t.wait_ge(m_sb, 2)
                    t.wait_ge(cleared, 1)
                    t.matmul(PS[:, 5, 0:2], one[:, :], top[:, :], start=True, stop=True).then_inc(m_ps, 1)
                    t.wait_ge(q_sb, 1)
                    for i in range(2):
                        for tap in range(TAPS):
                            mm = t.matmul(PS[:, 2 * i + tap // 8, 64 * (tap % 8):64 * (tap % 8) + 64],
                                          RAW2[:, i, :, tap], K["ident"][0:64, 0:64], start=True, stop=True)
                    mm.then_inc(w2_ps, 1)
                    t.wait_ge(w3_sb, 1)
                    t.wait_ge(loads, nload[0])
                    t.wait_ge(split, 1)
                    for i in range(3):
                        m = A["L3_conv_" + ws[i]].shape[0]
                        for tap in range(TAPS):
                            mm = t.matmul(PS[:, 2 * i + tap // 8, 64 * (tap % 8):64 * (tap % 8) + m],
                                          raw[i][0:m, :, tap], K["ident"][0:m, 0:m], start=True, stop=True)
                    t.matmul(PS[:, 6, 0:64], rawcv[:, :], K["ident"][0:64, 0:64], start=True, stop=True)
                    for c in range(5):
                        n = min(4, GK - 4 * c) * CG
                        mm = t.matmul(PS[0:n, 7, 64 * c:64 * c + 64],
                                      dcs[:, :, :].rearrange("o g c -> o (g c)")[:, 128 * c:128 * c + n],
                                      K["ident"][0:64, 0:64], start=True, stop=True)
                    mm.then_inc(w3_ps, 1)

                @blk.vector
                def _(v):
                    v.tensor_scalar(INV2[:, :], BV2[:, 3, :], 1e-5, None, ALU.add)
                    v.tensor_scalar(INV[:, :], BV3[:, 3, :], 1e-5, None, ALU.add)
                    v.drain().then_inc(root, 1)
                    v.wait_ge(tanh, 1)
                    for i in range(2):
                        v.tensor_reduce(big[:, i:i + 1], RAW2[:, i, :, :], AX.XY, ALU.max,
                                        apply_absolute_value=True)
                    v.drain().then_inc(m_sb, 1)
                    v.wait_ge(m_ps, 1)
                    v.tensor_copy(row[:, :, :].rearrange("p a b -> p (a b)"), PS[0:1, 4, 0:128])
                    v.drain()
                    v.tensor_reduce(top[:, :], row[:, :, :], AX.X, ALU.max)
                    v.drain().then_inc(m_sb, 1)
                    v.wait_ge(m_ps, 2)
                    v.tensor_scalar(rcp[:, :], PS[:, 5, 0:2], 2.0, None, ALU.mult)
                    v.drain()
                    v.reciprocal(rcp[:, :], rcp[:, :])
                    v.drain()
                    for f, g, p, q in ((None, 0.5, ALU.mult, ALU.add), (LEVELS, MAGIC, ALU.mult, ALU.add),
                                       (MAGIC, 2.0, ALU.subtract, ALU.mult), (LEVELS, None, ALU.subtract, None)):
                        for i in range(2):
                            t = RAW2[:, i, :, :]
                            s = rcp[0:64, i:i + 1] if f is None else f
                            if g is None:
                                v.tensor_scalar(t, t, s, None, p)
                            else:
                                v.tensor_scalar(t, t, s, g, p, q)
                        v.drain()
                    v.drain().then_inc(q_sb, 1)
                    v.wait_ge(loads, nload[0])
                    for d in range(DG):
                        v.tensor_copy(dcs[:, TAPS * d:TAPS * d + TAPS, :],
                                      rawdc[:, CG * d:CG * d + CG, :].rearrange("o c k -> o k c"))
                    v.drain().then_inc(split, 1)
                    v.wait_ge(rooted, 1)
                    v.reciprocal(INV2[:, :], root2[:, :])
                    v.reciprocal(INV[:, :], root3[:, :])
                    v.tensor_tensor(SHIFT[:, :], BIAS3[:, 0:4], BV3[:, 2, :], ALU.subtract)
                    v.drain()
                    v.tensor_tensor(INV2[:, :], INV2[:, :], BV2[:, 0, :], ALU.mult)
                    v.tensor_tensor(INV[:, :], INV[:, :], BV3[:, 0, :], ALU.mult)
                    v.drain()
                    v.tensor_tensor(SHIFT2[:, :], INV2[:, :], BV2[:, 2, :], ALU.mult)
                    v.tensor_tensor(SHIFT[:, :], SHIFT[:, :], INV[:, :], ALU.mult)
                    v.drain()
                    v.tensor_tensor(SHIFT2[:, :], BV2[:, 1, :], SHIFT2[:, :], ALU.subtract)
                    v.tensor_tensor(SHIFT[:, :], SHIFT[:, :], BV3[:, 1, :], ALU.add)
                    v.tensor_scalar(INV2[:, 0:1], INV2[:, 0:1], 1.0 / LEVELS, None, ALU.mult)
                    v.tensor_scalar(INV2[:, 1:2], INV2[:, 1:2], 1.0 / LEVELS ** 2, None, ALU.mult)
                    v.wait_ge(w2_ps, 1)
                    for i, w in enumerate((W1, W2)):
                        block_weights(v, w, PS[:, 2 * i:2 * i + 2, :].rearrange("p a (t o) -> p (a t) o", o=CH)
                                      [:, 0:TAPS, :], "half_nat")
                    v.drain().then_inc(w3_sb, 1)
                    v.wait_ge(w3_ps, 1)
                    v.wait_ge(cleared, 1)
                    for i in range(3):
                        m = A["L3_conv_" + ws[i]].shape[0]
                        block_weights(v, WB[i], PS[:, 2 * i:2 * i + 2, :].rearrange("p a (t o) -> p (a t) o", o=CH)
                                      [:, 0:TAPS, 0:m], "half_nat", m)
                    block_weights(v, CV2, PS[:, 6:7, 0:64], "half_nat")
                    v.tensor_copy(DC[:, 0:4, :], PS[:, 7, 0:256].rearrange("p (a o) -> p a o", o=CH))
                    v.tensor_copy(DC[0:64, 4, :], PS[0:64, 7, 256:320])
                    v.drain()

        phase(sampler_weights)

        def sampler(st, sb, sem):
            STAGES = 7
            AT_STEP = {0: 0, 1: 1, 3: 2, 4: 3, 6: 4, 7: 5, 8: 6}
            RING = 4
            G = [sb(f"G{i}", [128, GK, 4 * CG]) for i in range(RING)]
            VAL = sb("VAL", [128, 2, GK, CG])
            VT = sb("VT", [128, 2, 5, 128])
            Y = sb("Y", [128, 2, BANK])
            U = sb("U", [128, 2, BANK])
            T = sb("T", [128, PX])
            H2, OFF = sb("H2", [128, PX]), sb("OFF", [128, PX])
            HT, OT = sb("HT", [128, TILES, 128]), sb("OT", [128, TILES, 128])
            pos, low, above = sb("pos", [128, 2, NG]), sb("low", [128, 2, NG]), sb("above", [128, 2, NG])
            whole = sb("whole", [128, 2, NG], I32)
            mask = sb("mask", [128, STEPS, GK])
            IDX = sb("IDX", [128, 2, STEPS, GK], I32)
            W4 = sb("W4", [128, 2, STEPS, GK, 4])
            quant_ps, quant_sb, acts, layer2_ps, layer2 = (
                sem(n) for n in ("quant_ps", "quant_sb", "acts", "layer2_ps", "layer2"))
            block1_ps, block1, block2_ps, block2 = (sem(n) for n in ("block1_ps", "block1", "block2_ps", "block2"))
            off_ps, off_sb, off_t_ps, off_t, h_t_ps, h_t, masked, indexed = (
                sem(n) for n in ("off_ps", "off_sb", "off_t_ps", "off_t", "h_t_ps", "h_t", "masked", "indexed"))
            stored = [sem(f"stored{b}") for b in range(NB)]
            arrived = [sem(f"arrived{i}") for i in range(RING)]
            used, val, t_ps, t_sb, d_ps, d_sb, leaky, e_ps, e_sb, final, written = (
                sem(n) for n in ("used", "val", "t_ps", "t_sb", "d_ps", "d_sb", "leaky", "e_ps", "e_sb", "final",
                                 "written"))
            off3 = OT[:, :, :].rearrange("p t (h c) -> p (t h) c", h=HALVES)
            PRE = PS[:, 6:8, :]
            PREf = PRE.rearrange("p k f -> p (k f)")
            PREimg = PRE.rearrange("p k (y x) -> p (k y) x", x=W)
            NSTORE = 4 * 4 * HALVES * DG
            per_bank = 4 * HALVES

            def image(b):
                return slice(PX * b, PX * b + PX)

            def inner(t, b):
                return t[:, b, 1:H + 1, 1:W + 1]

            def square(t):
                return t.rearrange("p (y x) -> p y x", x=W)

            def convolve(t, w, src, b):
                for k in range(2):
                    for tap in range(TAPS):
                        mm = t.matmul(PS[:, 6 + k, :], w[:, tap, :], patch(src, 2 * b + k, tap), start=(tap == 0),
                                      stop=(tap == TAPS - 1))
                return mm

            def turn(t, src):
                for tl in range(TILES):
                    mm = t.transpose(PS[:, 6 + tl // 4, 128 * (tl % 4):128 * (tl % 4) + 128],
                                     src[:, 128 * tl:128 * tl + 128], K["ident"][:, :])
                return mm

            def stage_pe(t, b, s):
                if s == 0:
                    if b:
                        t.wait_ge(h_t, b)
                    convolve(t, W1, XP, b).then_inc(quant_ps, 1)
                elif s == 1:
                    t.wait_ge(acts, b + 1)
                    convolve(t, W2, AP, b).then_inc(layer2_ps, 1)
                elif s == 2:
                    t.wait_ge(layer2, b + 1)
                    convolve(t, WB[0], XP, b).then_inc(block1_ps, 1)
                elif s == 3:
                    t.wait_ge(block1, b + 1)
                    convolve(t, WB[1], T1, b).then_inc(block2_ps, 1)
                elif s == 4:
                    t.wait_ge(block2, b + 1)
                    convolve(t, WB[2], XP, b).then_inc(off_ps, 1)
                elif s == 5:
                    t.wait_ge(off_sb, b + 1)
                    turn(t, OFF).then_inc(off_t_ps, 1)
                else:
                    t.wait_ge(off_t, b + 1)
                    turn(t, H2).then_inc(h_t_ps, 1)

            def stage_act(a, b, s):
                if s == 0:
                    a.wait_ge(quant_ps, b + 1)
                    a.activation(T[:, :], PREf, ACT.Identity, scale=INV2[:, 0:1], bias=SHIFT2[:, 0:1])\
                     .then_inc(quant_sb, 1)
                elif s == 2:
                    a.wait_ge(block1_ps, b + 1)
                    a.activation(inner(T1, b), PREimg, ACT.Relu, scale=INV[:, 0:1], bias=SHIFT[:, 0:1])\
                     .then_inc(block1, 1)
                elif s == 4:
                    a.wait_ge(off_ps, b + 1)
                    a.activation(OFF[:, :], PREf, ACT.Identity, bias=BIAS3[:, 4:5]).then_inc(off_sb, 1)
                elif s == 5:
                    a.wait_ge(off_t_ps, b + 1)
                    a.activation(OT[:, :, :].rearrange("p t c -> p (t c)"), PREf, ACT.Copy)
                    a.drain().then_inc(off_t, 1)
                    a.activation(mask[:, :, :], off3[:, :, 2 * GK:3 * GK], ACT.Sigmoid).then_inc(masked, 1)
                elif s == 6:
                    a.wait_ge(h_t_ps, b + 1)
                    if b:
                        a.wait_ge(stored[b - 1], 16 * NSTORE)
                    a.activation(HT[:, :, :].rearrange("p t c -> p (t c)"), PREf, ACT.Copy).then_inc(h_t, 1)

            def stage_dve(v, b, s):
                if s == 0:
                    v.wait_ge(quant_sb, b + 1)
                    v.tensor_scalar(T[:, :], T[:, :], 0.0, 1.0, ALU.max, ALU.min)
                    v.drain()
                    v.tensor_scalar(T[:, :], T[:, :], LEVELS, MAGIC, ALU.mult, ALU.add)
                    v.drain()
                    v.tensor_scalar(inner(AP, b), square(T[:, :]), MAGIC, None, ALU.subtract)
                    v.drain().then_inc(acts, 1)
                elif s == 1:
                    v.wait_ge(layer2_ps, b + 1)
                    v.scalar_tensor_tensor(out=T[:, :], in0=PREf, scalar=INV2[:, 1:2], in1=X[:, image(b)],
                                           op0=ALU.mult, op1=ALU.add)
                    v.drain()
                    v.tensor_scalar(T[:, :], T[:, :], SHIFT2[:, 1:2], 0.0, ALU.add, ALU.max)
                    v.drain()
                    v.tensor_scalar(T[:, :], T[:, :], 1.0, LEVELS, ALU.min, ALU.mult)
                    v.drain()
                    v.tensor_scalar(T[:, :], T[:, :], MAGIC, MAGIC, ALU.add, ALU.subtract)
                    v.drain()
                    v.tensor_scalar(X[:, image(b)], T[:, :], 1.0 / LEVELS, None, ALU.mult)
                    v.tensor_scalar(inner(XP, b), square(T[:, :]), 1.0 / LEVELS, None, ALU.mult)
                    v.drain().then_inc(layer2, 1)
                elif s == 3:
                    v.wait_ge(block2_ps, b + 1)
                    v.scalar_tensor_tensor(out=H2[:, :], in0=PREf, scalar=INV[:, 1:2], in1=X[:, image(b)],
                                           op0=ALU.mult, op1=ALU.add)
                    v.drain()
                    v.tensor_scalar(H2[:, :], H2[:, :], SHIFT[:, 1:2], 0.0, ALU.add, ALU.max)
                    v.drain()
                    v.tensor_copy(inner(XP, b), square(H2[:, :]))
                    v.drain().then_inc(block2, 1)
                elif s == 5:
                    v.wait_ge(off_t, b + 1)
                    p3 = pos[:, :, :].rearrange("p a (t k) -> p a t k", k=GK)
                    for axis in range(2):
                        v.tensor_tensor(p3[:, axis], off3[:, :, axis:2 * GK:2],
                                        GR[:, axis, :].rearrange("p (t k) -> p t k", k=GK), ALU.add)
                    v.drain()
                    v.tensor_scalar(pos[:, :, :], pos[:, :, :], -1.0, float(H), ALU.max, ALU.min)
                    v.drain()
                    v.tensor_copy(whole[:, :, :], pos[:, :, :])
                    v.drain()
                    v.tensor_copy(low[:, :, :], whole[:, :, :])
                    v.drain()
                    v.tensor_tensor(above[:, :, :], low[:, :, :], pos[:, :, :], ALU.is_gt)
                    v.drain()
                    v.tensor_tensor(low[:, :, :], low[:, :, :], above[:, :, :], ALU.subtract)
                    v.drain()
                    v.tensor_tensor(pos[:, :, :], pos[:, :, :], low[:, :, :], ALU.subtract)
                    v.drain()
                    v.tensor_tensor(low[:, 1, :], low[:, 1, :], GR[:, 2, :], ALU.add)
                    v.tensor_scalar(above[:, :, :], pos[:, :, :], -1.0, 1.0, ALU.mult, ALU.add)
                    v.drain()
                    v.scalar_tensor_tensor(out=low[:, 0, :], in0=low[:, 0, :], scalar=float(TP), in1=low[:, 1, :],
                                           op0=ALU.mult, op1=ALU.add)
                    v.drain()
                    v.tensor_copy(IDX[:, b % 2].rearrange("p t k -> p (t k)"), low[:, 0, :])
                    v.drain().then_inc(indexed, 1)
                    v.wait_ge(masked, b + 1)
                    mk = mask[:, :, :].rearrange("p t k -> p (t k)")
                    w4 = W4[:, b % 2].rearrange("p t k c -> p (t k) c")
                    v.tensor_tensor(above[:, 0, :], above[:, 0, :], mk, ALU.mult)
                    v.tensor_tensor(pos[:, 0, :], pos[:, 0, :], mk, ALU.mult)
                    v.drain()
                    for c, (wy, wx) in enumerate(((above, above), (above, pos), (pos, above), (pos, pos))):
                        v.tensor_tensor(w4[:, :, c], wy[:, 0, :], wx[:, 1, :], ALU.mult)
                    v.drain()

            def steps(engine, stage, sample):
                for s in range(STAGES):
                    stage(engine, 0, s)
                for th in range(NB * STEPS):
                    sample(th)
                    b, step = th // STEPS, th % STEPS
                    if b + 1 < NB and step in AT_STEP:
                        stage(engine, b + 1, AT_STEP[step])

            with nc.Block() as blk:
                @blk.gpsimd
                def _(g):
                    for th in range(NB * STEPS):
                        b, step = th // STEPS, th % STEPS
                        if step == 0:
                            g.wait_ge(indexed, b + 1)
                            g.wait_ge(stored[b], 16 * NSTORE)
                        if th >= RING:
                            g.wait_ge(used, th - RING + 1)
                        for k in range(GK):
                            g.indirect_dma_start(G[th % RING][:, k, :], None, tables[b],
                                                 bass.IndirectOffsetOnAxis(ap=IDX[:, b % 2, step, k:k + 1], axis=0))\
                             .then_inc(arrived[th % RING], 16)

                @blk.sync
                def _(sp):
                    def write(b):
                        for h in range(HALVES):
                            sp.dma_start(out[NB * h + b].rearrange("c y x -> c (y x)"),
                                         X[64 * h:64 * h + 64, image(b)]).then_inc(written, 16)

                    for b in range(NB):
                        table = tables[b].rearrange("(q ey ex) (k c) -> q ey ex k c", q=HALVES * DG, ey=TP, k=4)
                        sp.wait_ge(h_t, b + 1)
                        for yr in range(4):
                            for dy in range(2):
                                for dx in range(2):
                                    first = yr - dy + 1
                                    for q in range(HALVES * DG):
                                        sp.dma_start(
                                            table[q, first:first + 29:4, 1 - dx:1 - dx + W, 2 * dy + dx, :]
                                            .rearrange("e x c -> x e c"),
                                            HT[32 * yr:32 * yr + 32, :, CG * q:CG * q + CG])\
                                          .then_inc(stored[b], 16)
                        if b:
                            sp.wait_ge(final, 2 * b)
                            write(b - 1)
                    sp.wait_ge(final, 2 * NB)
                    write(NB - 1)
                    sp.wait_ge(written, 16 * HALVES * NB)
                    for b in range(NB):
                        sp.wait_ge(stored[b], 16 * NSTORE)

                @blk.vector
                def _(v):
                    def sample(th):
                        gt, w4 = G[th % RING], W4[:, (th // STEPS) % 2, th % STEPS]
                        v.wait_ge(arrived[th % RING], 16 * GK * (th // RING + 1))
                        g3 = gt[:, :, :].rearrange("p k (q c) -> p (k q) c", q=4)
                        v.tensor_tensor(g3, g3, w4.rearrange("p k q -> p (k q)").unsqueeze(2)
                                        .broadcast_to([128, GK * 4, CG]), ALU.mult)
                        v.drain()
                        if th >= 2:
                            v.wait_ge(t_ps, th - 1)
                        v.tensor_reduce(VAL[:, th % 2, :, :], gt[:, :, :].rearrange("p k (q c) -> p k c q", q=4),
                                        AX.X, ALU.add)
                        v.drain().then_inc(val, 1)
                        v.sem_inc(used, 1)
                        if th % per_bank == per_bank - 1:
                            k = th // per_bank
                            y, u, x = Y[:, k % 2, :], U[:, k % 2, :], X[:, BANK * k:BANK * k + BANK]
                            v.wait_ge(d_sb, k + 1)
                            v.scalar_tensor_tensor(out=y, in0=y, scalar=0.1, in1=y, op0=ALU.mult, op1=ALU.max)
                            v.drain().then_inc(leaky, 1)
                            v.wait_ge(e_sb, k + 1)
                            v.scalar_tensor_tensor(out=u, in0=u, scalar=0.1, in1=u, op0=ALU.mult, op1=ALU.max)
                            v.drain()
                            v.tensor_tensor(x, x, u, ALU.add)
                            v.drain().then_inc(final, 1)
                    steps(v, stage_dve, sample)

                @blk.tensor
                def _(t):
                    def sample(th):
                        tl, h, k = th // 2, th % 2, th // per_bank
                        t.wait_ge(val, th + 1)
                        if th >= 2:
                            t.wait_ge(t_sb, th - 1)
                        flat = VAL[:, th % 2, :, :].rearrange("p k c -> p (k c)")
                        for c in range(5):
                            n = min(128, GK * CG - 128 * c)
                            o = 128 * c if c < 4 else 128 * (th % 2)
                            mm = t.transpose(PS[0:n, th % 2 if c < 4 else 2, o:o + 128],
                                             flat[:, 128 * c:128 * c + n], K["ident"][:, :])
                        mm.then_inc(t_ps, 1)
                        t.wait_ge(t_sb, th + 1)
                        if th % per_bank == 0 and k >= 2:
                            t.wait_ge(d_sb, k - 1)
                        for c in range(5):
                            n = min(128, GK * CG - 128 * c)
                            mm = t.matmul(PS[64 * h:64 * h + 64, 3 + k % 2, 128 * (tl % 4):128 * (tl % 4) + 128],
                                          DC[0:n, c, :], VT[0:n, th % 2, c, :], start=(c == 0), stop=(c == 4))
                        if th % per_bank == per_bank - 1:
                            mm.then_inc(d_ps, 1)
                            t.wait_ge(leaky, k + 1)
                            t.matmul(bank(5), CV2[:, 0, :], Y[:, k % 2, :], start=True, stop=True).then_inc(e_ps, 1)
                    steps(t, stage_pe, sample)

                @blk.scalar
                def _(a):
                    def sample(th):
                        k = th // per_bank
                        a.wait_ge(t_ps, th + 1)
                        a.activation(VT[:, th % 2, 0:4, :], PS[:, th % 2, :].rearrange("p (a c) -> p a c", c=128),
                                     ACT.Copy)
                        a.activation(VT[0:64, th % 2, 4, :], PS[0:64, 2, 128 * (th % 2):128 * (th % 2) + 128], ACT.Copy)
                        a.drain().then_inc(t_sb, 1)
                        if th % per_bank == per_bank - 1:
                            a.wait_ge(d_ps, k + 1)
                            a.activation(Y[:, k % 2, :], bank(3 + k % 2), ACT.Identity, scale=INV[:, 2:3],
                                         bias=SHIFT[:, 2:3]).then_inc(d_sb, 1)
                            a.wait_ge(e_ps, k + 1)
                            a.activation(U[:, k % 2, :], bank(5), ACT.Identity, scale=INV[:, 3:4],
                                         bias=SHIFT[:, 3:4]).then_inc(e_sb, 1)
                    steps(a, stage_act, sample)

        phase(sampler)
        lay3.close()


def kernel(**inputs):
    import numpy as _np
    import concourse.bacc as _bacc
    from concourse import mybir as _mybir
    from concourse.bass_utils import run_bass_kernel_spmd as _run

    nc = _bacc.Bacc("TRN2", target_bir_lowering=False, num_devices=1)
    arrays, args, consts = {}, {}, {}
    for name, value in inputs.items():
        a = _np.ascontiguousarray(value)
        arrays["in_" + name] = a
        args[name] = nc.dram_tensor("in_" + name, a.shape, _mybir.dt.from_np(a.dtype), kind="ExternalInput").ap()
    for name, a in constants().items():
        arrays["const_" + name] = a
        consts[name] = nc.dram_tensor("const_" + name, a.shape, _mybir.dt.from_np(a.dtype), kind="ExternalInput").ap()
    out = nc.dram_tensor("out", (B, CH, H, W), F32, kind="ExternalOutput").ap()
    program(nc, args, consts, out)
    r = _run(nc, [arrays], core_ids=[0])
    return r.results[0]["out"]
```

```python
from contextlib import ExitStack

import numpy as np
import concourse.bass as bass
from concourse import mybir

F32 = mybir.dt.float32
BF16 = mybir.dt.bfloat16
I32 = mybir.dt.int32
ALU = mybir.AluOpType
ACT = mybir.ActivationFunctionType
AX = mybir.AxisListType
ds = bass.ds

B, CH, H, W = 8, 64, 32, 32
HALVES = 2
NB = B // HALVES
PX = H * W
HP, WP = H + 2, W + 2
TAPS = 9
BANK = 512
NBANK = NB * PX // BANK
HW2 = H // 2
NTOK = HW2 * HW2
HEADS, HD = 8, 8
TOPK = NTOK // 2
ROUNDS = 3
AIM = TOPK - 4 * ROUNDS
STEP = 0.0085
TAKEN = -1.0e30
MAGIC = 12582912.0
LEVELS = 15.0
DG = 2
CG = CH // DG
TP = H + 2
NENT = TP * TP
TILES = PX // 128
STEPS = TILES * HALVES
GK = DG * TAPS
CHUNK = 2
SLOTS = 3

NJ, NI = 4, 16

CHAIN = [(0, 1)] * 4
COST_DVE, COST_CHAIN, COST_ACT = 1.2, 2.66, 1.9


def adder_rows():
    rows = []
    for q, chain in enumerate(CHAIN):
        n = 3 * NJ - len(chain[1:])
        tiles = []
        for j in range(NJ):
            maps = [(4 * q + i, (tx,)) for i in range(4) for tx in range(3) if i != j or tx not in chain]
            if chain:
                maps.insert((2 * j + 1) * n // (2 * NJ), (4 * q + j, chain))
            tiles.append(maps)
        rows += [list(r) for r in zip(*tiles)]
    dve = act = 0.0
    out = []
    for row in rows:
        plan = [None] * NJ
        for j in sorted(range(NJ), key=lambda j: -len(row[j][1])):
            i, taps = row[j]
            by_dve = len(taps) > 1 or dve + COST_DVE <= act + COST_ACT
            if by_dve:
                dve += COST_DVE + COST_CHAIN * (len(taps) - 1)
            else:
                act += COST_ACT
            plan[j] = (i, taps, "dve" if by_dve else "act")
        out.append(plan)
    return out


def constants():
    p = np.arange(128)
    half, ch = p // CH, p % CH
    pj, ph, pi = p // 32, (p % 32) // NI, p % NI
    pch = NI * pj + pi
    c = {}
    c["ident"] = np.eye(128)
    c["mean8"] = (p[:, None] // 8 == p[None] // 8) / 8.0
    c["mean4"] = (p[:, None] // 4 == p[None] // 4) / 4.0
    c["sum8"] = (p[:, None] // 8 == p[None] // 8) * 1.0
    c["mean_pair"] = (pch[:, None] == pch[None]) / 2.0
    c["half_nat"] = (half[:, None] == np.arange(2)[None]) * 1.0
    c["half_perm"] = (ph[:, None] == np.arange(2)[None]) * 1.0
    c["head"] = (p[:, None] // HD == np.arange(HALVES * HEADS)[None]) * 1.0
    slot = np.arange(32)
    one = [((slot[None] == NI * half[:, None] + i) * -2.0) for i in range(NI)]
    c["slots"] = np.tile(np.arange(8 * ROUNDS), 4)[None].repeat(128, 0)
    c["adder_out"] = np.concatenate(one, 1)
    sign = np.ones((3, 3, NJ, NI))
    for q, chain in enumerate(CHAIN):
        for j in range(NJ):
            for tx in chain[1:]:
                sign[:, tx, j, 4 * q + j] = -1.0
    c["adder_sign"] = sign.reshape(1, -1).repeat(128, 0)
    c["adder_x"] = (half[:, None] == ph[None]) * 1.0
    c["to_nat"] = ((pch[:, None] == ch[None]) & (ph[:, None] == half[None])) * 1.0
    t = np.arange(TILES)
    y = 4 * t[None] + p[:, None] // 32
    x = np.broadcast_to(p[:, None] % 32, y.shape)
    k = np.arange(TAPS)
    gy = y[:, :, None, None, None] + (k // 3 - 1)
    gx = x[:, :, None, None, None] + (k % 3 - 1)
    q = np.arange(HALVES)[None, :, None] * DG + np.arange(DG)
    full = (128, TILES, HALVES, DG, TAPS)
    c["grid_y"] = np.broadcast_to(gy, full).reshape(128, -1)
    c["grid_x"] = np.broadcast_to(gx, full).reshape(128, -1)
    c["grid_base"] = np.broadcast_to((q * NENT + TP + 1)[None, :, :, :, None], full).reshape(128, -1)
    return {n: np.ascontiguousarray(a, dtype=np.float32) for n, a in c.items()}


SMALL = ["ident", "mean8", "mean4", "sum8", "mean_pair", "half_nat", "half_perm", "head", "slots", "adder_out",
         "adder_x", "to_nat"]
GRIDS = ["grid_y", "grid_x", "grid_base"]


def halves(ap):
    return ap.rearrange("(c one) -> c one", one=1)


class Stats:

    def __init__(self, sem, sb, name, m, ps):
        self.m, self.ps, self.n = m, ps, 0
        self.to_pe, self.from_pe = sem(name + "_to_pe"), sem(name + "_from_pe")
        self.to_act, self.from_act = sem(name + "_to_act"), sem(name + "_from_act")
        self.mv = sb(name + "_mv", [128, m, 2])
        self.mean, self.dev, self.var = (sb(name + x, [128, m]) for x in ("_mean", "_dev", "_var"))
        self.scale, self.bias = sb(name + "_scale", [128, m]), sb(name + "_bias", [128, m])
        self.eps = None

    def dve(self, v, m, gamma, beta, eps, n=0):
        mean, dev, var, scale, bias = (t[:, 0:m] for t in (self.mean, self.dev, self.var, self.scale, self.bias))
        v.drain().then_inc(self.to_pe, 1)
        v.wait_ge(self.from_pe, 2 * n + 1)
        v.tensor_copy(mean, self.ps[:, 0:m])
        v.drain()
        v.tensor_tensor(dev, self.mv[:, 0:m, 0], mean, ALU.subtract)
        v.drain()
        v.tensor_tensor(dev, dev, dev, ALU.mult)
        v.drain()
        v.tensor_tensor(var, self.mv[:, 0:m, 1], dev, ALU.add)
        v.drain().then_inc(self.to_pe, 1)
        v.wait_ge(self.from_pe, 2 * n + 2)
        v.tensor_scalar(dev, self.ps[:, 64:64 + m], eps, None, ALU.add)
        v.drain().then_inc(self.to_act, 1)
        v.wait_ge(self.from_act, n + 1)
        v.reciprocal(scale, var)
        v.drain()
        v.tensor_tensor(scale, scale, gamma, ALU.mult)
        v.drain()
        v.tensor_tensor(dev, mean, scale, ALU.mult)
        v.drain()
        v.tensor_tensor(bias, beta, dev, ALU.subtract)
        v.drain()

    def pe(self, t, m, matrix, n=0):
        t.wait_ge(self.to_pe, 2 * n + 1)
        t.matmul(self.ps[:, 0:m], matrix, self.mv[:, 0:m, 0], start=True, stop=True).then_inc(self.from_pe, 1)
        t.wait_ge(self.to_pe, 2 * n + 2)
        t.matmul(self.ps[:, 64:64 + m], matrix, self.var[:, 0:m], start=True, stop=True).then_inc(self.from_pe, 1)

    def act(self, a, m, n=0):
        a.wait_ge(self.to_act, n + 1)
        a.activation(self.var[:, 0:m], self.dev[:, 0:m], ACT.Sqrt).then_inc(self.from_act, 1)


def program(nc, A, C, out):
    tables = [nc.dram_tensor(f"neighbours{b}", [HALVES * DG * NENT, 4 * CG], F32).ap() for b in range(NB)]
    outer = ExitStack()
    with outer:
        def osb(n, s, d=F32):
            return outer.enter_context(nc.sbuf_tensor(n, s, d))

        K = {n: osb("c_" + n, [128, C[n].shape[1]]) for n in SMALL}
        X = osb("X", [128, NB * PX])
        XP = osb("XP", [128, NB, HP, WP])
        PS = outer.enter_context(nc.psum_tensor("PS", [128, NBANK, BANK], F32))
        P2 = osb("P2", [128, NB, HP, WP])
        RAW2 = osb("RAW2", [64, 2, 128, TAPS])
        BNV = osb("BNV", [128, 4])
        BV2 = osb("BV2", [128, 4, 2])
        BV3 = osb("BV3", [128, 4, 4])
        BIAS3 = osb("BIAS3", [128, 5])
        W1 = osb("W1", [128, TAPS, 128])
        W2 = osb("W2", [128, TAPS, 128], BF16)
        RAW1 = P2[0:64, :, :, :].rearrange("p b y x -> p (b y x)")[:, 0:4 * 128 * TAPS]\
            .rearrange("p (q c t) -> p q c t", q=4, t=TAPS)
        X4 = X[:, :].rearrange("p (b y x) -> p b y x", b=NB, y=H)
        XPin = XP[:, :, 1:H + 1, 1:W + 1]

        def px_bank(t, k):
            return t[:, k // 2, 16 * (k % 2):16 * (k % 2) + 16, :]

        def patch(t, k, tap):
            y = 16 * (k % 2) + tap // 3
            return t[:, k // 2, y:y + 16, tap % 3:tap % 3 + W]

        def bank(k):
            return PS[:, k, :]

        def bank2(k):
            return PS[:, k, :].rearrange("p (y x) -> p y x", x=W)

        def phase(fn, recycle=False):
            with ExitStack() as st:
                def sb(n, s, d=F32):
                    return st.enter_context(nc.sbuf_tensor(f"{fn.__name__}_{n}", s, d))

                def sem(n):
                    if recycle:
                        recycled.append(nc.alloc_semaphore(name=f"{fn.__name__}_{n}"))
                        return recycled[-1]
                    return st.enter_context(nc.semaphore(f"{fn.__name__}_{n}"))
                recycled = []
                fn(st, sb, sem)
                if recycle:
                    nc.clear_and_free_semaphores(recycled)
                    nc.all_engine_barrier()

        lay0 = ExitStack()
        outer.enter_context(lay0)
        LL = lay0.enter_context(nc.sbuf_tensor("LL", [128, NB * NTOK], F32))
        HI = lay0.enter_context(nc.sbuf_tensor("HI", [128, 3, NB, HW2 + 2, HW2 + 2], F32))
        W0 = lay0.enter_context(nc.sbuf_tensor("W0", [128, 17, 128], F32))
        V0 = lay0.enter_context(nc.sbuf_tensor("V0", [128, 24], F32))
        vec = {}
        for name, n in (("attn_gn_g", 1), ("attn_gn_b", 1), ("he_gn1_g", 3), ("he_gn1_b", 3), ("he_gn2_g", 3),
                        ("he_gn2_b", 3), ("ffn_gn1_g", 2), ("ffn_gn1_b", 2), ("ffn_gn2_g", 1), ("ffn_gn2_b", 1),
                        ("alpha", 1)):
            vec[name] = (sum(x[1] for x in vec.values()), n)
        DW = lay0.enter_context(nc.sbuf_tensor("DW", [128, 3, NB, HW2, HW2], F32))
        HE = lay0.enter_context(nc.sbuf_tensor("HE", [128, 3, TAPS], F32))

        def v0(name, rep):
            o, n = vec[name]
            return V0[:, o:o + n].unsqueeze(2).broadcast_to([128, n, rep])

        V12t = lay0.enter_context(nc.sbuf_tensor("V12", [128, 4, 3, NB], F32))
        V12 = {n: V12t[:, i, :, :].rearrange("p s b -> p (s b)") for i, n in enumerate(("g", "b", "g2", "b2"))}
        VFt = lay0.enter_context(nc.sbuf_tensor("VF", [128, 2, 2, NB], F32))
        VF = {n: VFt[:, i, :, :].rearrange("p s b -> p (s b)") for i, n in enumerate("gb")}

        atn = ExitStack()
        outer.enter_context(atn)

        def asb(n, shape, d=F32):
            return atn.enter_context(nc.sbuf_tensor(n, shape, d))

        GROUPS = NB * HEADS
        qk_all = asb("qk", [128, 2, (NB + 1) * NTOK])
        VT = asb("VT", [128, NB * HALVES, HEADS, 2, HD + 1])
        VTf = VT[:, :, :, :, :].rearrange("p a b c d -> p (a b c d)")
        SUMS = asb("SUMS", [128, GROUPS, 2, 2, HD + 1])
        START = asb("START", [128, 4 * GROUPS])
        SLOPE = asb("SLOPE", [128, 4 * GROUPS])
        NEXT = asb("NEXT", [128, 4 * GROUPS])
        COUNT = asb("COUNT", [128, 4 * GROUPS])
        REDO = asb("REDO", [128, 1], I32)

        def attention(st, sb, sem):
            loads, vecs, ll_done, w_ps, w_sb = (sem(n) for n in ("loads", "vecs", "ll_done", "w_ps", "w_sb"))
            raws = sem("raws")
            qk_ps, qk_sq, qk_ns, qk_nrm, qk_done = (sem(n) for n in ("qk_ps", "qk_sq", "qk_ns", "qk_nrm", "qk_done"))
            v_ps, v_done = sem("v_ps"), sem("v_done")
            kt_ps, kt_sb, cov_ps, cov_sb, cq_ps, cq_sb, row_ps, dev_in, dev_done = (
                sem(n) for n in ("kt_ps", "kt_sb", "cov_ps", "cov_sb", "cq_ps", "cq_sb", "row_ps", "dev_in",
                                 "dev_done"))
            rawq = sb("rawq", [64, 3, 2, 64])
            rawp = sb("rawp", [64, 2, 64])
            rawpw = sb("rawpw", [64, 3, 2, 3, 64])
            rawf1 = sb("rawf1", [64, 2, 2, 64])
            rawf2 = sb("rawf2", [64, 2, 2, 64])
            xh = sb("xh", [128, NB, H, W])
            su = [sb(f"su{i}", [128, NB, HW2, HW2]) for i in range(4)]
            qk = qk_all[:, :, 0:NB * NTOK]
            sq = sb("sq", [128, 2, NB * NTOK])
            KT = sb("KT", [128, NB, 2, 128])
            COV = sb("COV", [128, NB, 128])
            QCQ = sb("QCQ", [128, NB * NTOK])
            ksum = sb("ksum", [128, NB])
            KM = sb("KM", [128, NB, HALVES * HEADS])
            row_sq = sb("row_sq", [128, 4 * GROUPS])
            nload, nraw, nvec = [0], [0], [0]
            rawx = sb("rawx", [64, 17, 128])

            with nc.Block() as blk:
                @blk.sync
                def _(sp):
                    def load(dst, src, done=loads):
                        sp.dma_start(dst, src).then_inc(done, 16)
                        (nload if done is loads else nvec)[0] += 16
                    for b in range(NB):
                        for h in range(HALVES):
                            load(X[64 * h:64 * h + 64, PX * b:PX * b + PX],
                                 A["x"][NB * h + b].rearrange("c y x -> c (y x)"))
                    for n in SMALL:
                        load(K[n][:, :], C[n])
                    for h in range(HALVES):
                        rows = slice(64 * h, 64 * h + 64)
                        load(HE[rows, :, :], A["L0_conv_he_dw_w"].rearrange("(s c) one ky kx -> c s (one ky kx)", c=64),
                             vecs)
                        for name, (o, n) in vec.items():
                            if name == "alpha":
                                load(V0[rows, o:o + 1], A["L0_conv_alpha"].rearrange("(a b) -> a b", a=1)
                                     .broadcast_to([64, 1]), vecs)
                            else:
                                for i in range(n):
                                    load(V0[rows, o + i:o + i + 1], halves(A["L0_conv_" + name][64 * i:64 * i + 64]),
                                         vecs)
                    sp.wait_ge(vecs, nvec[0])
                    sp.wait_ge(loads, nload[0])

                @blk.scalar
                def _(a):
                    def load(dst, src):
                        a.dma_start(dst, src).then_inc(raws, 16)
                        nraw[0] += 16
                    for d in range(2):
                        load(rawq[:, :, d, :], A["L0_conv_qkv_w"].rearrange("(s o) c -> o s c", o=64))
                        load(rawp[:, d, :], A["L0_conv_proj_w"])
                        for s in range(3):
                            load(rawpw[:, s, d, :, :], A["L0_conv_he_pw_w"][64 * s:64 * s + 64, :]
                                 .rearrange("o (i c) -> o i c", c=64))
                        load(rawf1[:, :, d, :], A["L0_conv_ffn_w1"].rearrange("(s o) c -> o s c", o=64))
                        load(rawf2[:, :, d, :], A["L0_conv_ffn_w2"].rearrange("o (s c) -> o s c", c=64))
                    a.wait_ge(qk_ns, 1)
                    a.activation(sq[:, :, :].rearrange("p a f -> p (a f)"),
                                 PS[:, 0:4, :].rearrange("p a f -> p (a f)"), ACT.Sqrt).then_inc(qk_nrm, 1)
                    a.wait_ge(kt_ps, 1)
                    a.activation(KT[:, :, :, :].rearrange("p b t c -> p (b t c)"),
                                 PS[:, 6:8, :].rearrange("p a f -> p (a f)"), ACT.Copy).then_inc(kt_sb, 1)
                    a.wait_ge(dev_in, 1)
                    a.activation(SLOPE[:, :], row_sq[:, :], ACT.Sqrt,
                                 scale=(STEP ** 2) / HD).then_inc(dev_done, 1)

                @blk.gpsimd
                def _(g):
                    g.memset(HI[:, :, :, :, :], 0.0)
                    g.memset(XP[:, :, :, :], 0.0)
                    g.memset(BIAS3[:, :], 0.0)
                    g.memset(VT[:, :, :, :, :], 1.0)
                    g.drain().then_inc(ll_done, 1)

                @blk.tensor
                def _(t):
                    t.wait_ge(loads, nload[0])
                    t.wait_ge(raws, nraw[0])
                    t.wait_ge(w_sb, 1)
                    for s in range(17):
                        mm = t.matmul(PS[:, 5 + s // 8, 64 * (s % 8):64 * (s % 8) + 64], rawx[:, s, :],
                                      K["ident"][0:64, 0:64], start=True, stop=True)
                    mm.then_inc(w_ps, 1)
                    t.wait_ge(w_sb, 2)
                    t.wait_ge(ll_done, 2)
                    for s in range(2):
                        for k in range(2):
                            mm = t.matmul(PS[:, 2 * s + k, :], W0[:, s, :], LL[:, BANK * k:BANK * k + BANK],
                                          start=True, stop=True)
                    mm.then_inc(qk_ps, 1)
                    for b in range(NB):
                        for h in range(HALVES):
                            for mt in range(2):
                                o = (b * 2 + mt) * 64
                                mm = t.matmul(PS[:, 4 + h, o:o + 64],
                                              LL[64 * h:64 * h + 64, b * NTOK + 128 * mt:b * NTOK + 128 * mt + 128],
                                              W0[64 * h:64 * h + 64, 2, 64 * h:64 * h + 64], start=True, stop=True)
                    mm.then_inc(v_ps, 1)
                    t.wait_ge(qk_sq, 1)
                    for s in range(2):
                        for k in range(2):
                            mm = t.matmul(PS[:, 2 * s + k, :], K["sum8"][:, :],
                                          sq[:, s, BANK * k:BANK * k + BANK], start=True, stop=True)
                    mm.then_inc(qk_ns, 1)

                    t.wait_ge(qk_done, 1)
                    t.wait_ge(w_sb, 2)
                    for b in range(NB):
                        for mt in range(2):
                            c = (b * 2 + mt) * 128
                            mm = t.transpose(PS[:, 6 + c // BANK, c % BANK:c % BANK + 128],
                                             qk[:, 1, b * NTOK + mt * 128:b * NTOK + mt * 128 + 128], K["ident"][:, :])
                    mm.then_inc(kt_ps, 1)
                    t.wait_ge(kt_sb, 1)
                    for b in range(NB):
                        for mt in range(2):
                            mm = t.matmul(PS[:, 0, 128 * b:128 * b + 128], KT[:, b, mt, :], KT[:, b, mt, :],
                                          start=(mt == 0), stop=(mt == 1))
                    mm.then_inc(cov_ps, 1)
                    t.wait_ge(cov_sb, 1)
                    for b in range(NB):
                        mm = t.matmul(PS[:, 2 + b // 2, NTOK * (b % 2):NTOK * (b % 2) + NTOK], COV[:, b, :],
                                      qk[:, 0, b * NTOK:b * NTOK + NTOK], start=True, stop=True)
                    mm.then_inc(cq_ps, 1)
                    t.wait_ge(cq_sb, 1)
                    for b in range(NB):
                        for nt in range(2):
                            tok = slice(b * NTOK + 128 * nt, b * NTOK + 128 * nt + 128)
                            o = (b * 2 + nt) * 16
                            t.matmul(PS[:, 0, o:o + 16], qk[:, 0, tok], KM[:, b, :], start=True, stop=True)
                            mm = t.matmul(PS[:, 1, o:o + 16], QCQ[:, tok], K["head"][:, :], start=True, stop=True)
                    mm.then_inc(row_ps, 1)

                @blk.vector
                def _(v):
                    v.wait_ge(raws, nraw[0])
                    v.tensor_copy(rawx[:, 0:3, :].rearrange("o s (d c) -> o s d c", d=2), rawq[:, :, :, :])
                    v.tensor_copy(rawx[:, 3, :].rearrange("o (d c) -> o d c", d=2), rawp[:, :, :])
                    for so in range(3):
                        v.tensor_copy(rawx[:, 4 + 3 * so:7 + 3 * so, :].rearrange("o i (d c) -> o i d c", d=2),
                                      rawpw[:, so, :, :, :].rearrange("o d i c -> o i d c"))
                    v.tensor_copy(rawx[:, 13:15, :].rearrange("o s (d c) -> o s d c", d=2), rawf1[:, :, :, :])
                    v.tensor_copy(rawx[:, 15:17, :].rearrange("o s (d c) -> o s d c", d=2), rawf2[:, :, :, :])
                    v.drain().then_inc(w_sb, 1)
                    v.wait_ge(loads, nload[0])
                    v.tensor_scalar(xh[:, :, :, :].rearrange("p b y x -> p (b y x)"), X[:, :], 0.5, None, ALU.mult)
                    v.drain()
                    q00, q10 = xh[:, :, 0:H:2, 0:W:2], xh[:, :, 1:H:2, 0:W:2]
                    q01, q11 = xh[:, :, 0:H:2, 1:W:2], xh[:, :, 1:H:2, 1:W:2]
                    v.tensor_tensor(su[0][:, :, :, :], q00, q10, ALU.add)
                    v.tensor_tensor(su[1][:, :, :, :], q01, q11, ALU.add)
                    v.tensor_tensor(su[2][:, :, :, :], q10, q00, ALU.subtract)
                    v.tensor_tensor(su[3][:, :, :, :], q11, q01, ALU.subtract)
                    v.drain()
                    v.wait_ge(ll_done, 1)
                    inner = [HI[:, s, :, 1:HW2 + 1, 1:HW2 + 1] for s in range(3)]
                    v.tensor_tensor(LL[:, :].rearrange("p (b y x) -> p b y x", b=NB, y=HW2), su[0][:, :, :, :],
                                    su[1][:, :, :, :], ALU.add)
                    v.tensor_tensor(inner[0], su[1][:, :, :, :], su[0][:, :, :, :], ALU.subtract)
                    v.tensor_tensor(inner[1], su[2][:, :, :, :], su[3][:, :, :, :], ALU.add)
                    v.tensor_tensor(inner[2], su[3][:, :, :, :], su[2][:, :, :, :], ALU.subtract)
                    v.drain().then_inc(ll_done, 1)
                    v.wait_ge(w_ps, 1)
                    for h in range(HALVES):
                        for c in range(3):
                            n = min(8, 17 - 8 * c)
                            v.tensor_scalar(W0[:, 8 * c:8 * c + n, 64 * h:64 * h + 64],
                                            PS[:, 5 + c, 0:64 * n].rearrange("p (s o) -> p s o", o=64),
                                            K["half_nat"][:, h:h + 1], None, ALU.mult)
                    v.drain().then_inc(w_sb, 1)
                    v.wait_ge(qk_ps, 1)
                    v.tensor_copy(qk, PS[:, 0:4, :].rearrange("p (a k) f -> p a (k f)", k=2))
                    v.drain()
                    v.tensor_tensor(sq[:, :, :], qk[:, :, :], qk[:, :, :], ALU.mult)
                    v.drain().then_inc(qk_sq, 1)
                    v.wait_ge(v_ps, 1)
                    for h in range(HALVES):
                        for mt in range(2):
                            v.tensor_copy(VT[:, h:NB * HALVES:2, :, mt, 0:HD],
                                          PS[:, 4 + h, :].rearrange("p (n m e d) -> p n m e d", n=4, m=2, d=HD)[:, :, mt])
                    v.drain().then_inc(v_done, 1)
                    v.wait_ge(qk_nrm, 1)
                    v.tensor_scalar(sq[:, :, :], sq[:, :, :], 1e-12, None, ALU.max)
                    v.drain()
                    v.reciprocal(sq[:, :, :], sq[:, :, :])
                    v.drain()
                    v.tensor_tensor(qk[:, :, :], qk[:, :, :], sq[:, :, :], ALU.mult)
                    v.drain().then_inc(qk_done, 1)

                    for b in range(NB):
                        v.tensor_reduce(ksum[:, b:b + 1], qk[:, 1, b * NTOK:b * NTOK + NTOK], AX.X, ALU.add)
                    v.drain()
                    v.tensor_scalar(ksum[:, :], ksum[:, :], 1.0 / NTOK, None, ALU.mult)
                    v.drain()
                    for b in range(NB):
                        v.tensor_scalar(KM[:, b, :], K["head"][:, :], ksum[:, b:b + 1], None, ALU.mult)
                    v.wait_ge(cov_ps, 1)
                    v.scalar_tensor_tensor(out=COV[:, :, :], in0=PS[:, 0, :].rearrange("p (b c) -> p b c", b=NB),
                                           scalar=1.0 / NTOK,
                                           in1=K["sum8"][:, :].unsqueeze(1).broadcast_to([128, NB, 128]),
                                           op0=ALU.mult, op1=ALU.mult)
                    v.drain().then_inc(cov_sb, 1)
                    v.wait_ge(cq_ps, 1)
                    v.tensor_tensor(QCQ[:, :], qk[:, 0, :], PS[:, 2:4, :].rearrange("p a f -> p (a f)"), ALU.mult)
                    v.drain().then_inc(cq_sb, 1)
                    v.wait_ge(row_ps, 1)

                    def by_group(t, b):
                        return t[:, 32 * b:32 * b + 32].rearrange("p (h n) -> p h n", n=2)

                    def by_tile(k, b):
                        return PS[:, k, 32 * b:32 * b + 32].rearrange("p (n h) -> p h n", n=2)
                    for b in range(NB):
                        v.tensor_copy(by_group(START, b), by_tile(0, b))
                        v.tensor_copy(by_group(row_sq, b), by_tile(1, b))
                    v.drain()
                    v.tensor_tensor(COUNT[:, :], START[:, :], START[:, :], ALU.mult)
                    v.drain()
                    v.tensor_tensor(row_sq[:, :], row_sq[:, :], COUNT[:, :], ALU.subtract)
                    v.drain()
                    v.tensor_scalar(row_sq[:, :], row_sq[:, :], 0.0, None, ALU.max)
                    v.tensor_scalar(START[:, :], START[:, :], float(HD) ** -0.5, None, ALU.mult)
                    v.drain().then_inc(dev_in, 1)
                    v.wait_ge(vecs, nvec[0])
                    for i, n in enumerate(("he_gn1_g", "he_gn1_b", "he_gn2_g", "he_gn2_b")):
                        v.tensor_copy(V12t[:, i, :, :], v0(n, NB))
                    for i, n in enumerate(("ffn_gn1_g", "ffn_gn1_b")):
                        v.tensor_copy(VFt[:, i, :, :], v0(n, NB))
                    v.wait_ge(dev_done, 1)
                    v.scalar_tensor_tensor(out=START[:, :], in0=SLOPE[:, :], scalar=float(TOPK - AIM),
                                           in1=START[:, :], op0=ALU.mult, op1=ALU.add)
                    v.drain()
                    v.scalar_tensor_tensor(out=NEXT[:, :], in0=SLOPE[:, :], scalar=float(NTOK // 2 - AIM),
                                           in1=START[:, :], op0=ALU.mult, op1=ALU.add)
                    v.drain()
                    v.tensor_scalar(SLOPE[:, :], SLOPE[:, :], 0.5, None, ALU.mult)
                    v.drain()

        phase(attention, recycle=True)

        def attend(st, sb, sem, exact):
            staged, s_ps, s_sb, s_used, e_done, p_done, pt_ps, pt_sb, o_ps, redo_in, redo_ps = (
                sem(n) for n in ("staged", "s_ps", "s_sb", "s_used", "e_done", "p_done", "pt_ps", "pt_sb", "o_ps",
                                 "redo_in", "redo_ps"))
            D1 = HD + 1
            stage = sb("stage", [128, 2, 2, 128])
            S = sb("S", [128, 4, NTOK])
            WK = sb("WK", [128, 4, NTOK])
            E = sb("E", [128, 4, NTOK])
            EW = sb("EW", [128, 4, NTOK])
            minus = sb("minus", [128, 128])
            PT = sb("PT", [128, 4, NTOK])
            IND = sb("IND", [128, 4, NTOK])
            signs = sb("signs", [128, 4, NTOK])
            above = sb("above", [128, 4])
            thr, neg = sb("thr", [128, 4]), sb("neg", [128, 4])
            cnt, need = sb("cnt", [128, 4]), sb("need", [128, 4])
            spare = sb("spare", [128, 4, 8 * ROUNDS])
            top = sb("top", [128, 4, 8])
            mark = sb("mark", [128, 2])
            missed = sb("missed", [128, 4 * GROUPS])
            n_missed = sb("n_missed", [128, 1])
            ones = sb("ones", [128, 128])
            if not exact:
                ahead, zeroed, cleared = sem("ahead"), sem("zeroed"), sem("cleared")
                zero = sb("zero", [128, HALVES * DG * NENT * CG // 128])
                part = sb("part", [128, 3, NB, HW2, HW2])

            SUMSf = SUMS[:, :, :, :, :].rearrange("p g a n d -> p (g a n d)")

            def flat(t):
                return t[:, :, :].rearrange("p u n -> p (u n)")

            with nc.Block() as blk:
                if exact:
                    @blk.sync
                    def _(sp):
                        sp.drain()

                    @blk.gpsimd
                    def _(g):
                        g.drain()
                else:
                    @blk.gpsimd
                    def _(g):
                        g.memset(zero[:, :], 0.0)
                        g.drain().then_inc(zeroed, 1)
                        for tap in range(TAPS):
                            for s in range(3):
                                g.tensor_scalar((part if tap else DW)[:, s],
                                                HI[:, s, :, tap // 3:tap // 3 + HW2, tap % 3:tap % 3 + HW2],
                                                HE[:, s, tap:tap + 1], None, ALU.mult)
                            g.drain()
                            if tap:
                                g.tensor_tensor(DW[:, :, :, :, :].rearrange("p s b y x -> p (s b y x)"),
                                                DW[:, :, :, :, :].rearrange("p s b y x -> p (s b y x)"),
                                                part[:, :, :, :, :].rearrange("p s b y x -> p (s b y x)"), ALU.add)
                                g.drain()

                    @blk.sync
                    def _(sp):
                        n = [0]

                        def load(dst, src):
                            sp.dma_start(dst, src).then_inc(ahead, 16)
                            n[0] += 16
                        for q, name in enumerate(("conv1_w", "add1_w", "conv2_w", "add2_w")):
                            w = A["L1_conv_" + name].rearrange("o c ky kx -> o c (ky kx)")
                            for h in range(HALVES):
                                if q == 2:
                                    load(RAW1[:, q, :, :].rearrange("o (j h i) t -> o j h (i t)", j=NJ, h=2)[:, :, h],
                                         w.rearrange("o (j i) t -> o j (i t)", i=NI))
                                else:
                                    load(RAW1[:, q, 64 * h:64 * h + 64, :], w)
                        for i, name in enumerate(("bn1_g", "bn1_b", "bn2_g", "bn2_b")):
                            for j in range(NJ):
                                for h in range(HALVES):
                                    r = 32 * j + NI * h
                                    load(BNV[r:r + NI, i:i + 1], halves(A["L1_conv_" + name][NI * j:NI * j + NI]))
                        for h in range(HALVES):
                            for i in range(2):
                                load(RAW2[:, i, 64 * h:64 * h + 64, :],
                                     A[f"L2_conv_w{i + 1}"].rearrange("o c ky kx -> o c (ky kx)"))
                                for f, name in enumerate(("gamma", "beta", "mean", "var")):
                                    load(BV2[64 * h:64 * h + 64, f, i:i + 1], halves(A[f"L2_conv_{name}{i + 1}"]))
                            for i, name in enumerate(("rb_bn1", "rb_bn2", "bn1", "bn2")):
                                for f in range(4):
                                    load(BV3[64 * h:64 * h + 64, f, i:i + 1],
                                         A["L3_conv_" + name][f:f + 1, :].rearrange("one c -> c one"))
                            for i, name in ((0, "rb_b1"), (1, "rb_b2"), (2, "dc_b"), (4, "off_b")):
                                m = A["L3_conv_" + name].shape[0]
                                load(BIAS3[64 * h:64 * h + m, i:i + 1], halves(A["L3_conv_" + name]))
                        sp.wait_ge(zeroed, 1)
                        for table in tables:
                            for part in table.rearrange("r f -> (r f)").rearrange("(n p f) -> n p f", n=4, p=128):
                                sp.dma_start(part, zero[:, :]).then_inc(cleared, 16)
                        sp.wait_ge(ahead, n[0])
                        sp.wait_ge(cleared, 16 * 4 * NB)

                @blk.scalar
                def _(a):
                    def queries(g):
                        for par in range(2):
                            b, hh = (g >> 3), (g & 7)
                            a.activation(stage[:, par, :, :], qk_all[:, 0, ds(b * NTOK, NTOK)]
                                         .rearrange("p (t n) -> p t n", t=2), ACT.Copy,
                                         scale=K["head"][:, ds(hh * 2 + par, 1)])
                        a.drain().then_inc(staged, 1)

                    def take_scores(g):
                        a.wait_ge(s_ps, g + 1)
                        a.activation(flat(S), PS[:, 0:2, :].rearrange("p a f -> p (a f)"), ACT.Copy,
                                     scale=float(HD) ** -0.5)
                        if not exact:
                            a.activation(neg[:, :], START[:, ds(g * 4, 4)], ACT.Copy, scale=-1.0)
                            a.drain()
                            for u in range(4):
                                a.activation(signs[:, u, :], S[:, u, :], ACT.Sign, bias=neg[:, u:u + 1],
                                             accum_out=above[:, u:u + 1])
                        a.drain().then_inc(s_sb, 1)

                    def exponentials(g):
                        a.activation(flat(E), flat(S), ACT.Exp)
                        a.drain()

                    def finish(g, left):
                        a.wait_ge(p_done, g + 1)
                        a.activation(flat(EW), flat(WK), ACT.Exp)
                        a.drain().then_inc(e_done, 1)
                        a.wait_ge(pt_ps, g + 1)
                        a.activation(flat(PT), PS[:, 2:4, :].rearrange("p a f -> p (a f)"), ACT.Copy).then_inc(pt_sb, 1)
                        if left >= 1:
                            exponentials(g + 1)
                        if left >= 2:
                            a.wait_ge(s_used, g + 2)
                            take_scores(g + 2)
                        if left >= 3:
                            queries(g + 3)
                        a.wait_ge(o_ps, g + 1)
                        a.activation(SUMSf[:, ds(g * 4 * D1, 4 * D1)], PS[:, 4, 0:4 * D1], ACT.Copy)
                        a.drain()

                    queries(0)
                    take_scores(0)
                    queries(1)
                    exponentials(0)
                    a.wait_ge(s_used, 1)
                    take_scores(1)
                    queries(2)
                    with a.Fori(0, GROUPS - 3, 1) as g:
                        finish(g, 3)
                    for g in range(GROUPS - 3, GROUPS):
                        finish(g, GROUPS - 1 - g)

                @blk.tensor
                def _(t):
                    t.sem_inc(e_done, 1)

                    def scores(g):
                        t.wait_ge(staged, g + 1)
                        for par in range(2):
                            for nt in range(2):
                                mm = t.matmul(PS[:, par, NTOK * nt:NTOK * nt + NTOK], stage[:, par, nt, :],
                                              qk_all[:, 1, ds((g >> 3) * NTOK, NTOK)], start=True, stop=True)
                        mm.then_inc(s_ps, 1)

                    def turn(g):
                        t.wait_ge(e_done, g + 2)
                        for u in range(4):
                            for mt in range(2):
                                c = 256 * (u % 2) + 128 * mt
                                tok = slice(128 * mt, 128 * mt + 128)
                                t.matmul(PS[:, 2 + u // 2, c:c + 128], E[:, u, tok], K["ident"][:, :],
                                         start=True, stop=False)
                                mm = t.matmul(PS[:, 2 + u // 2, c:c + 128], EW[:, u, tok], minus[:, :],
                                              start=False, stop=True)
                        mm.then_inc(pt_ps, 1)

                    def values(g):
                        t.wait_ge(pt_sb, g + 1)
                        for par in range(2):
                            for nt in range(2):
                                u = 2 * par + nt
                                for mt in range(2):
                                    mm = t.matmul(PS[:, 4, D1 * u:D1 * u + D1], PT[:, u, 128 * mt:128 * mt + 128],
                                                  VTf[:, ds(g * 4 * D1 + (2 * par + mt) * D1, D1)],
                                                  start=(mt == 0), stop=(mt == 1))
                        mm.then_inc(o_ps, 1)

                    scores(0)
                    t.wait_ge(s_sb, 1)
                    scores(1)
                    with t.Fori(0, GROUPS - 2, 1) as g:
                        t.wait_ge(s_sb, g + 2)
                        scores(g + 2)
                        turn(g)
                        values(g)
                    for g in (GROUPS - 2, GROUPS - 1):
                        turn(g)
                        values(g)
                    if not exact:
                        t.wait_ge(redo_in, 1)
                        t.matmul(PS[:, 5, 0:1], ones[:, :], n_missed[:, :], start=True, stop=True).then_inc(redo_ps, 1)

                @blk.vector
                def _(v):
                    def take_all(g):
                        for u in range(4):
                            v.max(top[:, u, :], S[:, u, :])
                        v.drain()
                        for r in range(TOPK // 8):
                            if r:
                                for u in range(4):
                                    v.max(top[:, u, :], WK[:, u, :])
                                v.drain()
                            for u in range(4):
                                v.match_replace(out=WK[:, u, :], in_to_replace=top[:, u, :],
                                                in_values=(WK if r else S)[:, u, :], imm_value=TAKEN)
                            if r == 0:
                                v.drain().then_inc(s_used, 1)
                            else:
                                v.drain()

                    def take_above(g):
                        v.tensor_tensor(cnt[:, :], above[:, :], SLOPE[:, ds(g * 4, 4)], ALU.mult)
                        v.drain()
                        v.tensor_tensor(thr[:, :], NEXT[:, ds(g * 4, 4)], cnt[:, :], ALU.add)
                        v.drain()
                        for u in range(4):
                            v.tensor_scalar(IND[:, u, :], S[:, u, :], thr[:, u:u + 1], 0.0, ALU.is_ge, ALU.add,
                                            accum_out=cnt[:, u:u + 1])
                        v.drain()
                        v.tensor_scalar(need[:, :], cnt[:, :], -1.0, float(TOPK), ALU.mult, ALU.add)
                        v.tensor_copy(COUNT[:, ds(g * 4, 4)], cnt[:, :])
                        v.wait_ge(e_done, g + 1)
                        v.scalar_tensor_tensor(out=flat(WK), in0=flat(IND), scalar=TAKEN, in1=flat(S),
                                               op0=ALU.mult, op1=ALU.add)
                        v.drain().then_inc(s_used, 1)
                        for u in range(4):
                            v.max(top[:, u, :], WK[:, u, :])
                        v.tensor_tensor(spare[:, :, :], K["slots"][:, :].rearrange("p (u s) -> p u s", u=4),
                                        need[:, :].unsqueeze(2).broadcast_to([128, 4, 8 * ROUNDS]), ALU.is_ge)
                        v.drain()
                        for r in range(ROUNDS):
                            if r:
                                for u in range(4):
                                    v.max(top[:, u, :], WK[:, u, :])
                                v.drain()
                            v.scalar_tensor_tensor(out=top[:, :, :], in0=spare[:, :, 8 * r:8 * r + 8], scalar=TAKEN,
                                                   in1=top[:, :, :], op0=ALU.mult, op1=ALU.add)
                            v.drain()
                            for u in range(4):
                                v.match_replace(out=WK[:, u, :], in_to_replace=top[:, u, :],
                                                in_values=WK[:, u, :], imm_value=TAKEN)
                            v.drain()

                    def select(g):
                        v.wait_ge(s_sb, g + 1)
                        v.memset(mark[:, 0:1], 0.0)
                        if exact:
                            v.wait_ge(e_done, g + 1)
                            v.memset(mark[:, 1:2], 0.0)
                            take_all(g)
                        else:
                            take_above(g)
                        v.sem_inc(p_done, 1)

                    v.tensor_scalar(minus[:, :], K["ident"][:, :], -1.0, None, ALU.mult)
                    v.drain()
                    with v.Fori(0, GROUPS // 2, 1) as pair:
                        select(pair * 2)
                        select(pair * 2 + 1)
                    if not exact:
                        v.memset(ones[:, :], 1.0)
                        v.tensor_scalar(missed[:, :], COUNT[:, :], float(TOPK), None, ALU.is_gt)
                        v.tensor_scalar(COUNT[:, :], COUNT[:, :], float(TOPK - 8 * ROUNDS), None, ALU.is_lt)
                        v.drain()
                        v.tensor_tensor(missed[:, :], missed[:, :], COUNT[:, :], ALU.add)
                        v.drain()
                        v.tensor_reduce(n_missed[:, :], missed[:, :], AX.X, ALU.add)
                        v.drain().then_inc(redo_in, 1)
                        v.wait_ge(redo_ps, 1)
                        v.tensor_scalar(REDO[:, :], PS[:, 5, 0:1], 1.0, None, ALU.min)
                        v.drain()

        def top_k(st, sb, sem):
            attend(st, sb, sem, exact=False)

        phase(top_k)

        def top_k_exact(st, sb, sem):
            attend(st, sb, sem, exact=True)

        redo = nc.values_load(REDO[0:1, 0:1], min_val=0, max_val=1,
                              skip_runtime_bounds_check_because="the chip computes it as min(count, 1)")
        with nc.If(redo):
            phase(top_k_exact)

        def high_bands(st, sb, sem):
            at_ps, at_sb, pr_ps, o_done = (sem(n) for n in ("at_ps", "at_sb", "pr_ps", "o_done"))
            AO = sb("AO", [128, NB * NTOK])
            Y = sb("Y", [128, NB, NTOK])
            O = sb("O", [128, 2, GROUPS, 2, HD])
            rcp = sb("rcp", [128, GROUPS, 2, 2])
            gnp = Stats(sem, sb, "gnp", NB, PS[:, 6, :])
            stp = sb("stp", [128, NB, 6])
            dw = DW
            dwf = dw[:, :, :, :, :].rearrange("p s b y x -> p s b (y x)")
            act = sb("act", [128, 3, NB, NTOK])
            y2 = sb("y2", [128, 3, NB, NTOK])
            st6 = sb("st6", [128, 12, 6])
            gn = Stats(sem, sb, "gn", 12, PS[:, 7, :])
            silu_in, silu_done, pw_ps = sem("silu_in"), sem("silu_done"), sem("pw_ps")

            def stats(v, t):
                for m in range(12):
                    v.bn_stats(st6[:, m, :], t[:, m // NB, m % NB, :])
                v.drain()
                for m in range(12):
                    v.bn_aggr(gn.mv[:, m, :], st6[:, m, :])

            with nc.Block() as blk:
                @blk.vector
                def _(v):
                    v.reciprocal(rcp[:, :, :, :], SUMS[:, :, :, :, HD])
                    v.drain()
                    for par in range(2):
                        for nt in range(2):
                            v.tensor_tensor(O[:, nt, :, par, :], SUMS[:, :, par, nt, 0:HD],
                                            rcp[:, :, par, nt].unsqueeze(2).broadcast_to([128, GROUPS, HD]), ALU.mult)
                    v.drain().then_inc(o_done, 1)
                    stats(v, dwf)
                    gn.dve(v, 12, V12["g"], V12["b"], 1e-6)
                    v.drain().then_inc(silu_in, 1)
                    v.wait_ge(pr_ps, 1)
                    v.tensor_copy(Y[:, :, :].rearrange("p b f -> p (b f)"),
                                  PS[:, 2:4, :].rearrange("p a f -> p (a f)"))
                    v.drain()
                    for b in range(NB):
                        v.bn_stats(stp[:, b, :], Y[:, b, :])
                    v.drain()
                    for b in range(NB):
                        v.bn_aggr(gnp.mv[:, b, :], stp[:, b, :])
                    gnp.dve(v, NB, v0("attn_gn_g", NB)[:, 0, :], v0("attn_gn_b", NB)[:, 0, :], 1e-6)
                    for b in range(NB):
                        v.tensor_scalar(Y[:, b, :], Y[:, b, :], gnp.scale[:, b:b + 1], gnp.bias[:, b:b + 1],
                                        ALU.mult, ALU.add)
                    v.drain()
                    v.tensor_tensor(LL[:, :], LL[:, :], Y[:, :, :].rearrange("p b f -> p (b f)"), ALU.add)
                    v.drain()
                    v.wait_ge(pw_ps, 1)
                    v.tensor_copy(y2[:, :, :, :].rearrange("p s b f -> p (s b f)"),
                                  PS[:, 0:6, :].rearrange("p a f -> p (a f)"))
                    v.drain()
                    stats(v, y2)
                    gn.dve(v, 12, V12["g2"], V12["b2"], 1e-6, n=1)
                    al = V0[:, vec["alpha"][0]:vec["alpha"][0] + 1]
                    v.tensor_scalar(gn.scale[:, :], gn.scale[:, :], al, None, ALU.mult)
                    v.tensor_scalar(gn.bias[:, :], gn.bias[:, :], al, None, ALU.mult)
                    v.drain()
                    for m in range(12):
                        t = y2[:, m // NB, m % NB, :]
                        v.tensor_scalar(t, t, gn.scale[:, m:m + 1], gn.bias[:, m:m + 1], ALU.mult, ALU.add)
                    v.drain()
                    y5 = y2[:, :, :, :].rearrange("p s b (y x) -> p s b y x", y=HW2)
                    for s in range(3):
                        v.tensor_tensor(y5[:, s], y5[:, s], HI[:, s, :, 1:HW2 + 1, 1:HW2 + 1], ALU.add)
                    v.drain()
                    ll = LL[:, :].rearrange("p (b f) -> p b f", b=NB)
                    lh, hl, hh = (y2[:, s] for s in range(3))
                    t0, t1, t2, t3 = act[:, 0], act[:, 1], act[:, 2], dwf[:, 0]
                    v.tensor_tensor(t0, ll, lh, ALU.subtract)
                    v.tensor_tensor(t1, hl, hh, ALU.subtract)
                    v.tensor_tensor(t2, ll, lh, ALU.add)
                    v.tensor_tensor(t3, hl, hh, ALU.add)
                    v.drain()
                    r = dwf[:, 1]
                    r4 = dw[:, 1]
                    for dy, dx, p, q, op in ((0, 0, t0, t1, ALU.subtract), (1, 0, t0, t1, ALU.add),
                                             (0, 1, t2, t3, ALU.subtract), (1, 1, t2, t3, ALU.add)):
                        v.tensor_tensor(r, p, q, op)
                        v.drain()
                        for b in range(NB):
                            at = X4[:, b, dy:H:2, dx:W:2]
                            v.scalar_tensor_tensor(out=at, in0=r4[:, b], scalar=0.1, in1=at, op0=ALU.mult,
                                                   op1=ALU.add)
                        v.drain()

                @blk.scalar
                def _(a):
                    a.wait_ge(at_ps, 1)
                    a.activation(AO[:, :], PS[:, 0:2, :].rearrange("p a f -> p (a f)"), ACT.Copy).then_inc(at_sb, 1)
                    gn.act(a, 12)
                    a.wait_ge(silu_in, 1)
                    for m in range(12):
                        a.activation(act[:, m // NB, m % NB, :], dwf[:, m // NB, m % NB, :], ACT.Silu,
                                     scale=gn.scale[:, m:m + 1], bias=gn.bias[:, m:m + 1])
                    a.drain().then_inc(silu_done, 1)
                    gnp.act(a, NB)
                    gn.act(a, 12, n=1)

                @blk.tensor
                def _(t):
                    t.wait_ge(o_done, 1)
                    Of = O[:, :, :, :, :].rearrange("p n g a d -> p n (g a d)")
                    for b in range(NB):
                        for nt in range(2):
                            c = b * NTOK + nt * 128
                            mm = t.transpose(PS[:, c // BANK, c % BANK:c % BANK + 128],
                                             Of[:, nt, b * 128:b * 128 + 128], K["ident"][:, :])
                    mm.then_inc(at_ps, 1)
                    t.wait_ge(at_sb, 1)
                    for k in range(2):
                        mm = t.matmul(PS[:, 2 + k, :], W0[:, 3, :], AO[:, BANK * k:BANK * k + BANK],
                                      start=True, stop=True)
                    mm.then_inc(pr_ps, 1)
                    gn.pe(t, 12, K["mean8"][:, :])
                    gnp.pe(t, NB, K["mean4"][:, :])
                    t.wait_ge(silu_done, 1)
                    flat = act[:, :, :, :].rearrange("p s b f -> p s (b f)")
                    for so in range(3):
                        for k in range(2):
                            for si in range(3):
                                mm = t.matmul(PS[:, 2 * so + k, :], W0[:, 4 + 3 * so + si, :],
                                              flat[:, si, BANK * k:BANK * k + BANK], start=(si == 0), stop=(si == 2))
                    mm.then_inc(pw_ps, 1)
                    gn.pe(t, 12, K["mean8"][:, :], n=1)

        phase(high_bands)
        atn.close()

        def feed_forward(st, sb, sem):
            f1 = sb("f1", [128, 2, NB * PX])
            f2 = sb("f2", [128, NB * PX])
            st6 = sb("st6", [128, 16, 6])
            gn = Stats(sem, sb, "gn", 8, PS[:, 7, :])
            f_ps, f_sb, gelu_in, gelu_done, r_ps, r_sb = (sem(n) for n in ("f_ps", "f_sb", "gelu_in", "gelu_done",
                                                                          "r_ps", "r_sb"))
            with nc.Block() as blk:
                @blk.tensor
                def _(t):
                    for u in range(16):
                        if u >= 7:
                            t.wait_ge(f_sb, u - 6)
                        t.matmul(PS[:, u % 7, :], W0[:, 13 + u // 8, :], X[:, BANK * (u % 8):BANK * (u % 8) + BANK],
                                 start=True, stop=True).then_inc(f_ps, 1)
                    gn.pe(t, 8, K["mean8"][:, :])
                    t.wait_ge(f_sb, 16)
                    for k in range(NBANK):
                        t.wait_ge(gelu_done, k // 2 + 1)
                        if k >= 7:
                            t.wait_ge(r_sb, k - 6)
                        for e in range(2):
                            mm = t.matmul(PS[:, k % 7, :], W0[:, 15 + e, :], f1[:, e, BANK * k:BANK * k + BANK],
                                          start=(e == 0), stop=(e == 1))
                        mm.then_inc(r_ps, 1)
                    gn.pe(t, 4, K["mean4"][:, :], n=1)

                @blk.scalar
                def _(a):
                    for u in range(16):
                        a.wait_ge(f_ps, u + 1)
                        a.activation(f1[:, u // 8, BANK * (u % 8):BANK * (u % 8) + BANK], PS[:, u % 7, :],
                                     ACT.Copy).then_inc(f_sb, 1)
                    gn.act(a, 8)
                    a.wait_ge(gelu_in, 1)
                    for b in range(NB):
                        for e in range(2):
                            m = e * NB + b
                            t = f1[:, e, PX * b:PX * b + PX]
                            a.activation(t, t, ACT.Gelu, scale=gn.scale[:, m:m + 1], bias=gn.bias[:, m:m + 1])
                        a.drain().then_inc(gelu_done, 1)
                    for k in range(NBANK):
                        a.wait_ge(r_ps, k + 1)
                        a.activation(f2[:, BANK * k:BANK * k + BANK], PS[:, k % 7, :], ACT.Copy).then_inc(r_sb, 1)
                    gn.act(a, 4, n=1)

                @blk.vector
                def _(v):
                    for u in range(16):
                        v.wait_ge(f_sb, u + 1)
                        v.bn_stats(st6[:, u, :], f1[:, u // 8, BANK * (u % 8):BANK * (u % 8) + BANK])
                    v.drain()
                    for m in range(8):
                        v.bn_aggr(gn.mv[:, m, :], st6[:, 2 * m:2 * m + 2, :].rearrange("p a b -> p (a b)"))
                    gn.dve(v, 8, VF["g"], VF["b"], 1e-6)
                    v.drain().then_inc(gelu_in, 1)
                    for k in range(NBANK):
                        v.wait_ge(r_sb, k + 1)
                        v.bn_stats(st6[:, k, :], f2[:, BANK * k:BANK * k + BANK])
                    v.drain()
                    for m in range(4):
                        v.bn_aggr(gn.mv[:, m, :], st6[:, 2 * m:2 * m + 2, :].rearrange("p a b -> p (a b)"))
                    gn.dve(v, 4, v0("ffn_gn2_g", NB)[:, 0, :], v0("ffn_gn2_b", NB)[:, 0, :], 1e-6, n=1)
                    for b in range(NB):
                        t = f2[:, PX * b:PX * b + PX]
                        v.tensor_scalar(t, t, gn.scale[:, b:b + 1], gn.bias[:, b:b + 1], ALU.mult, ALU.add)
                    v.drain()
                    v.scalar_tensor_tensor(out=X[:, :], in0=f2[:, :], scalar=0.1, in1=X[:, :], op0=ALU.mult,
                                           op1=ALU.add)
                    v.drain()
                    v.tensor_copy(XPin, X4)
                    v.drain()

        phase(feed_forward)
        lay0.close()


        lay1 = ExitStack()
        outer.enter_context(lay1)

        def l1(n, s):
            return lay1.enter_context(nc.sbuf_tensor(n, s, F32))

        WC = [l1(f"WC{i}", [128, TAPS, 128]) for i in range(2)]
        AW = [l1(f"AW{i}", [128, TAPS, CH]) for i in range(2)]
        AN = [l1(f"AN{i}", [128, TAPS, CH]) for i in range(2)]
        WSUM = [l1(f"WSUM{i}", [128, 128]) for i in range(2)]

        def block_weights(v, dst, ps9, masks, cols=CH):
            for h in range(HALVES):
                v.tensor_scalar(dst[:, :, 64 * h:64 * h + cols], ps9, K[masks][:, h:h + 1], None, ALU.mult)

        def adder_weights(st, sb, sem):
            loads, w_ps = sem("loads"), sem("w_ps")
            total = sb("total", [128, CH])
            sign, signed = sb("sign", [128, TAPS * CH]), sb("signed", [128, TAPS, CH])
            with nc.Block() as blk:
                @blk.sync
                def _(sp):
                    sp.dma_start(sign[:, :], C["adder_sign"]).then_inc(loads, 16)
                    sp.wait_ge(loads, 16)

                @blk.gpsimd
                def _(g):
                    g.wait_ge(w_ps, 4)
                    g.memset(P2[:, :, :, :], 0.0)
                    g.drain()

                @blk.tensor
                def _(t):
                    for q in range(4):
                        for tap in range(TAPS):
                            mm = t.matmul(PS[:, 2 * q + tap // 8, 64 * (tap % 8):64 * (tap % 8) + 64],
                                          RAW1[:, q, :, tap], K["ident"][0:64, 0:64], start=True, stop=True)
                        mm.then_inc(w_ps, 1)

                @blk.vector
                def _(v):
                    for q in range(4):
                        ps9 = PS[:, 2 * q:2 * q + 2, :].rearrange("p a (t o) -> p (a t) o", o=CH)[:, 0:TAPS, :]
                        v.wait_ge(w_ps, q + 1)
                        i = q // 2
                        if q % 2 == 0:
                            block_weights(v, WC[i], ps9, "half_perm" if q else "half_nat")
                            continue
                        v.tensor_copy(AW[i][:, :, :], ps9)
                        v.tensor_scalar(AN[i][:, :, :], ps9, -1.0, None, ALU.mult)
                        v.drain()
                        v.wait_ge(loads, 16)
                        v.tensor_tensor(signed[:, :, :].rearrange("p t o -> p (t o)"),
                                        AN[i][:, :, :].rearrange("p t o -> p (t o)"), sign[:, :], ALU.mult)
                        v.drain()
                        v.tensor_reduce(total[:, :], signed[:, :, :].rearrange("p t o -> p o t"), AX.X, ALU.add)
                        v.drain()
                        for h in range(HALVES):
                            v.tensor_scalar(WSUM[i][:, :].rearrange("p (j h i) -> p j h i", j=NJ, h=2)[:, :, h],
                                            total[:, :].rearrange("p (j i) -> p j i", i=NI),
                                            K["half_nat"][:, h:h + 1], None, ALU.mult)
                    v.drain()

        phase(adder_weights)

        class Quantiser:

            def __init__(self, sem, spare):
                self.big, self.rcp = spare[0:64, 0, 0:2], spare[:, 0, 4:6]
                self.row = spare[0:1, 1, 0:128].rearrange("p (a b) -> p a b", a=2)
                self.top, self.one = spare[0:1, 1, 128:130], spare[0:1, 2, 0:128]
                self.tanh, self.one_set, self.m_sb, self.m_ps, self.q_sb, self.w_ps = (
                    sem("q_" + n) for n in ("tanh", "one_set", "m_sb", "m_ps", "q_sb", "w_ps"))

            def act(self, a):
                for i in range(2):
                    a.activation(RAW2[:, i, :, :], RAW2[:, i, :, :], ACT.Tanh)
                a.drain().then_inc(self.tanh, 1)

            def gpsimd(self, g):
                g.memset(self.one, 1.0)
                g.drain().then_inc(self.one_set, 1)

            def dve(self, v):
                v.wait_ge(self.tanh, 1)
                for i in range(2):
                    v.tensor_reduce(self.big[:, i:i + 1], RAW2[:, i, :, :], AX.XY, ALU.max,
                                    apply_absolute_value=True)
                v.drain().then_inc(self.m_sb, 1)
                v.wait_ge(self.m_ps, 1)
                v.tensor_copy(self.row.rearrange("p a b -> p (a b)"), PS[0:1, NBANK - 1, 0:128])
                v.drain()
                v.tensor_reduce(self.top, self.row, AX.X, ALU.max)
                v.drain().then_inc(self.m_sb, 1)
                v.wait_ge(self.m_ps, 2)
                v.tensor_scalar(self.rcp, PS[:, NBANK - 1, 128:130], 2.0, None, ALU.mult)
                v.drain()
                v.reciprocal(self.rcp, self.rcp)
                v.drain()
                for f, g, p, q in ((None, 0.5, ALU.mult, ALU.add), (LEVELS, MAGIC, ALU.mult, ALU.add),
                                   (MAGIC, 2.0, ALU.subtract, ALU.mult), (LEVELS, None, ALU.subtract, None)):
                    for i in range(2):
                        t = RAW2[:, i, :, :]
                        s = self.rcp[0:64, i:i + 1] if f is None else f
                        if g is None:
                            v.tensor_scalar(t, t, s, None, p)
                        else:
                            v.tensor_scalar(t, t, s, g, p, q)
                    v.drain()
                v.drain().then_inc(self.q_sb, 1)

            def pe_before(self, t, k):
                if k == 2:
                    t.wait_ge(self.m_sb, 1)
                    for i in range(2):
                        mm = t.matmul(PS[0:1, NBANK - 1, 64 * i:64 * i + 64], self.big[:, i:i + 1],
                                      K["ident"][0:64, 0:64], start=True, stop=True)
                    mm.then_inc(self.m_ps, 1)
                elif k == 4:
                    t.wait_ge(self.m_sb, 2)
                    t.wait_ge(self.one_set, 1)
                    t.matmul(PS[:, NBANK - 1, 128:130], self.one, self.top, start=True,
                             stop=True).then_inc(self.m_ps, 1)
                elif k == NBANK - 1:
                    t.wait_ge(self.q_sb, 1)

            def pe_turn(self, t):
                for i in range(2):
                    for tap in range(TAPS):
                        mm = t.matmul(PS[:, 4 + 2 * i + tap // 8, 64 * (tap % 8):64 * (tap % 8) + 64],
                                      RAW2[:, i, :, tap], K["ident"][0:64, 0:64], start=True, stop=True)
                mm.then_inc(self.w_ps, 1)

            def dve_weights(self, v):
                v.wait_ge(self.w_ps, 1)
                for i, w in enumerate((W1, W2)):
                    block_weights(v, w, PS[:, 4 + 2 * i:6 + 2 * i, :].rearrange("p a (t o) -> p (a t) o", o=CH)
                                  [:, 0:TAPS, :], "half_nat")
                v.drain()

        def adder_layer(layer, src):
            def run(st, sb, sem):
                CP = sb("CP", [128, NB, HP, WP])
                Z = sb("Z", [128, SLOTS, NJ, CHUNK * PX])
                BOX = P2[:, :, 1:H + 1, 1:W + 1]
                SO_all = XP[:, :, :, :].rearrange("p b y x -> p (b y x)")
                rowsum = SO_all[:, 0:NB * HP * W].rearrange("p (b y x) -> p b y x", b=NB, x=W)
                SO = SO_all[:, 0:NB * PX]
                st6 = sb("st6", [128, NBANK, 6])
                ones = sb("ones", [128, 1])
                gn = Stats(sem, sb, "gn", 1, PS[:, 0, :])
                ready, c_ps, c_sb, box = sem("ready"), sem("c_ps"), sem("c_sb"), sem("box")
                quantiser = None if layer else Quantiser(sem, Z[:, SLOTS - 1, 0:3, :])
                z_dve, z_act = sem("z_dve"), sem("z_act")
                z_free = [sem(f"z_free{i}") for i in range(SLOTS)]
                s_ps, s_sb, normed, nat_ps, border = (sem(n) for n in ("s_ps", "s_sb", "normed", "nat_ps", "border"))
                CBANK = CHUNK * PX // BANK
                AWf = AW[layer][:, :, :].rearrange("p t o -> p (t o)")
                ANf = AN[layer][:, :, :].rearrange("p t o -> p (t o)")

                rows = adder_rows()
                mine = {e: [sum(any(m[2] == e for m in row) for row in rows[:r + 1]) for r in range(len(rows))]
                        for e in ("dve", "act")}

                def made(ch, ty, r, engine):
                    return ty * mine[engine][-1] + (ch * 3 * mine[engine][-1] + mine[engine][r])

                def use(ch, ty, r):
                    n = len(rows[r % SLOTS::SLOTS])
                    return ty * n + (ch * 3 * n + r // SLOTS + 1)

                def seen(ch, ty, tx):
                    return CP[:, CHUNK * ch:CHUNK * ch + CHUNK, ds(ty, H), tx:tx + W]

                def z(r, j):
                    return Z[:, r % SLOTS, j, :].rearrange("p (b y x) -> p b y x", b=CHUNK, y=H)

                def weight(ty, tx, j, i):
                    return ds(ty * 3 * CH + (tx * CH + NI * j + i), 1)

                with nc.Block() as blk:
                    @blk.gpsimd
                    def _(g):
                        if quantiser:
                            quantiser.gpsimd(g)
                        g.memset(CP[:, :, :, :], 0.0)
                        g.memset(ones[:, :], 1.0)
                        g.drain().then_inc(ready, 1)
                        g.wait_ge(c_sb, NBANK)
                        g.tensor_tensor(rowsum, CP[:, :, :, 0:W], CP[:, :, :, 1:W + 1], ALU.add).then_inc(box, 1)
                        g.wait_ge(box, 1)
                        g.tensor_tensor(rowsum, rowsum, CP[:, :, :, 2:W + 2], ALU.add).then_inc(box, 1)
                        g.wait_ge(box, 2)
                        g.tensor_tensor(BOX[:, :, :, :], rowsum[:, :, 0:H], rowsum[:, :, 1:H + 1], ALU.add)\
                         .then_inc(box, 1)
                        g.wait_ge(box, 3)
                        g.tensor_tensor(BOX[:, :, :, :], BOX[:, :, :, :], rowsum[:, :, 2:H + 2], ALU.add)\
                         .then_inc(box, 1)
                        if layer:
                            g.wait_ge(nat_ps, NBANK)
                            g.memset(XP[:, :, :, :], 0.0)
                            g.drain().then_inc(border, 1)

                    @blk.tensor
                    def _(t):
                        for slot in range(SLOTS):
                            t.sem_inc(z_free[slot], 1)
                        for k in range(NBANK):
                            if quantiser:
                                quantiser.pe_before(t, k)
                            for tap in range(TAPS):
                                mm = t.matmul(bank(k), WC[layer][:, tap, :], patch(src, k, tap), start=(tap == 0),
                                              stop=(tap == TAPS - 1))
                            mm.then_inc(c_ps, 1)
                        t.wait_ge(ready, 1)
                        if quantiser:
                            t.wait_ge(c_sb, NBANK)
                            quantiser.pe_turn(t)
                        for ch in range(NB // CHUNK):
                            banks = range(CBANK * ch, CBANK * ch + CBANK)
                            t.wait_ge(c_sb, CBANK * ch + CBANK)
                            for k in banks:
                                t.matmul(bank(k), WSUM[layer][:, :], ones[:, :].broadcast_to([128, BANK]),
                                         start=True, stop=False, skip_group_check=True)
                            with t.Fori(0, 3, 1) as ty:
                                for r, row in enumerate(rows):
                                    t.wait_ge(z_dve, made(ch, ty, r, "dve"))
                                    t.wait_ge(z_act, made(ch, ty, r, "act"))
                                    for k in banks:
                                        for j, (i, _, _) in enumerate(row):
                                            c = BANK * (k % CBANK)
                                            mm = t.matmul(PS[32 * j:32 * j + 32, k, :],
                                                          K["adder_out"][:, 32 * i:32 * i + 32],
                                                          Z[:, r % SLOTS, j, c:c + BANK], start=False, stop=False,
                                                          skip_group_check=True)
                                    mm.then_inc(z_free[r % SLOTS], 1)
                            t.wait_ge(box, 4)
                            for k in banks:
                                mm = t.matmul(bank(k), K["adder_x"][:, :], px_bank(BOX, k), start=False, stop=True,
                                              skip_group_check=True)
                            mm.then_inc(s_ps, 1)
                        gn.pe(t, 1, K["mean_pair"][:, :])
                        if layer:
                            t.wait_ge(normed, 1)
                            for k in range(NBANK):
                                t.matmul(bank(k), K["to_nat"][:, :], SO[:, BANK * k:BANK * k + BANK],
                                         start=True, stop=True).then_inc(nat_ps, 1)

                    @blk.scalar
                    def _(a):
                        if quantiser:
                            quantiser.act(a)
                        a.wait_ge(ready, 1)
                        for k in range(NBANK):
                            a.wait_ge(c_ps, k + 1)
                            a.activation(px_bank(CP[:, :, 1:H + 1, 1:W + 1], k), bank2(k), ACT.Copy)\
                             .then_inc(c_sb, 1)
                        a.wait_ge(c_sb, NBANK)
                        for ch in range(NB // CHUNK):
                            with a.Fori(0, 3, 1) as ty:
                                for r, row in enumerate(rows):
                                    maps = [(j, i, taps[0]) for j, (i, taps, e) in enumerate(row) if e == "act"]
                                    if not maps:
                                        continue
                                    a.wait_ge(z_free[r % SLOTS], use(ch, ty, r))
                                    for j, i, tx in maps:
                                        op = a.activation(z(r, j), seen(ch, ty, tx), ACT.Relu,
                                                          bias=ANf[:, weight(ty, tx, j, i)])
                                    op.then_inc(z_act, 1)
                            a.wait_ge(s_ps, ch + 1)
                            for k in range(CBANK * ch, CBANK * ch + CBANK):
                                a.activation(SO[:, BANK * k:BANK * k + BANK], bank(k), ACT.Copy).then_inc(s_sb, 1)
                        gn.act(a, 1)
                        if not layer:
                            a.wait_ge(normed, 1)
                            for b in range(NB):
                                a.activation(P2[:, b, 1:H + 1, 1:W + 1],
                                             SO[:, PX * b:PX * b + PX].rearrange("p (y x) -> p y x", y=H), ACT.Relu,
                                             scale=gn.scale[:, 0:1], bias=gn.bias[:, 0:1])
                            a.drain()

                    @blk.vector
                    def _(v):
                        if quantiser:
                            quantiser.dve(v)
                        v.wait_ge(c_sb, NBANK)
                        if quantiser:
                            quantiser.dve_weights(v)
                        for ch in range(NB // CHUNK):
                            with v.Fori(0, 3, 1) as ty:
                                for r, row in enumerate(rows):
                                    maps = [(j, i, taps) for j, (i, taps, e) in enumerate(row) if e == "dve"]
                                    if not maps:
                                        continue
                                    v.wait_ge(z_free[r % SLOTS], use(ch, ty, r))
                                    for j, i, taps in maps:
                                        op = v.tensor_scalar(z(r, j), seen(ch, ty, taps[0]),
                                                             AWf[:, weight(ty, taps[0], j, i)], 0.0,
                                                             ALU.subtract, ALU.max)
                                    for j, i, taps in maps:
                                        for tx in taps[1:]:
                                            v.drain()
                                            for b in range(CHUNK):
                                                op = v.scalar_tensor_tensor(
                                                    out=z(r, j)[:, b], in0=seen(ch, ty, tx)[:, b],
                                                    scalar=AWf[:, weight(ty, tx, j, i)], in1=z(r, j)[:, b],
                                                    op0=ALU.max, op1=ALU.add)
                                    op.then_inc(z_dve, 1)
                        for k in range(NBANK):
                            v.wait_ge(s_sb, k + 1)
                            v.bn_stats(st6[:, k, :], SO[:, BANK * k:BANK * k + BANK])
                        v.drain()
                        v.bn_aggr(gn.mv[:, 0, :], st6[:, :, :].rearrange("p a b -> p (a b)"))
                        gn.dve(v, 1, BNV[:, 2 * layer:2 * layer + 1], BNV[:, 2 * layer + 1:2 * layer + 2], 1e-5)
                        if not layer:
                            v.drain().then_inc(normed, 1)
                            return
                        v.tensor_scalar(SO, SO, gn.scale[:, 0:1], gn.bias[:, 0:1], ALU.mult, ALU.add)
                        v.drain().then_inc(normed, 1)
                        for k in range(NBANK):
                            v.wait_ge(nat_ps, k + 1)
                            v.tensor_tensor(X[:, BANK * k:BANK * k + BANK], bank(k), X[:, BANK * k:BANK * k + BANK],
                                            ALU.add)
                        v.drain()
                        v.tensor_scalar(X[:, :], X[:, :], 0.0, None, ALU.max)
                        v.drain()
                        v.wait_ge(border, 1)
                        v.tensor_copy(XPin, X4)
                        v.drain()
            run.__name__ = f"adder_layer{layer}"
            return run

        phase(adder_layer(0, XP))
        phase(adder_layer(1, P2))
        lay1.close()

        lay3 = ExitStack()
        outer.enter_context(lay3)

        def l3(n, s, d=F32):
            return lay3.enter_context(nc.sbuf_tensor(n, s, d))

        INV2, SHIFT2 = l3("INV2", [128, 2]), l3("SHIFT2", [128, 2])
        WB = [l3(f"WB{i}", [128, TAPS, 128]) for i in range(3)]
        INV, SHIFT = l3("INV", [128, 4]), l3("SHIFT", [128, 4])
        DC = l3("DC", [128, 5, CH])
        CV2 = l3("CV2", [128, 1, 128])
        AP = l3("AP", [128, NB, HP, WP], BF16)
        T1 = P2
        NG = STEPS * GK
        GR = l3("GR", [128, 3, NG])

        def sampler(st, sb, sem):
            STAGES = 7
            AT_STEP = {0: 0, 1: 1, 3: 2, 4: 3, 6: 4, 7: 5, 8: 6}
            RING = 4
            ws = ("rb_w1", "rb_w2", "off_w")
            G = [sb(f"G{i}", [128, GK, 4 * CG]) for i in range(RING)]
            VAL = sb("VAL", [128, 2, GK, CG])
            VT = sb("VT", [128, 2, 5, 128])
            Y = sb("Y", [128, 2, BANK])
            U = sb("U", [128, 2, BANK])
            T = sb("T", [128, PX])
            H2, OFF = sb("H2", [128, PX]), sb("OFF", [128, PX])
            HT, OT = sb("HT", [128, TILES, 128]), sb("OT", [128, TILES, 128])
            pos, low, above = sb("pos", [128, 2, NG]), sb("low", [128, 2, NG]), sb("above", [128, 2, NG])
            whole = sb("whole", [128, 2, NG], I32)
            mask = sb("mask", [128, STEPS, GK])
            IDX = sb("IDX", [128, 2, STEPS, GK], I32)
            W4 = sb("W4", [128, 2, STEPS, GK, 4])
            raw = [G[i][0:64, :, :].rearrange("p k f -> p (k f)")[:, 0:128 * TAPS].rearrange("p (c t) -> p c t", t=TAPS)
                   for i in range(3)]
            rest = G[3][0:64, :, :].rearrange("p k f -> p (k f)")
            rawdc = rest[:, 0:CH * TAPS].rearrange("p (c t) -> p c t", t=TAPS)
            dcs = rest[:, CH * TAPS:2 * CH * TAPS].rearrange("p (k c) -> p k c", c=CG)
            rawcv = rest[:, 2 * CH * TAPS:2 * CH * TAPS + 128]
            root2, root3 = sb("root2", [128, 2]), sb("root3", [128, 4])
            loads, gridded, cleared, root, rooted, split, w_ps, w_sb, scaled = (
                sem(n) for n in ("loads", "gridded", "cleared", "root", "rooted", "split", "w_ps", "w_sb", "scaled"))
            NLOAD = 16 * (1 + HALVES * (len(ws) + 1))
            quant_ps, quant_sb, acts, layer2_ps, layer2 = (
                sem(n) for n in ("quant_ps", "quant_sb", "acts", "layer2_ps", "layer2"))
            block1_ps, block1, block2_ps, block2 = (sem(n) for n in ("block1_ps", "block1", "block2_ps", "block2"))
            off_ps, off_sb, off_t_ps, off_t, h_t_ps, h_t, masked, indexed = (
                sem(n) for n in ("off_ps", "off_sb", "off_t_ps", "off_t", "h_t_ps", "h_t", "masked", "indexed"))
            stored = [sem(f"stored{b}") for b in range(NB)]
            arrived = [sem(f"arrived{i}") for i in range(RING)]
            used, val, t_ps, t_sb, d_ps, d_sb, leaky, e_ps, e_sb, final, written = (
                sem(n) for n in ("used", "val", "t_ps", "t_sb", "d_ps", "d_sb", "leaky", "e_ps", "e_sb", "final",
                                 "written"))
            off3 = OT[:, :, :].rearrange("p t (h c) -> p (t h) c", h=HALVES)
            PRE = PS[:, 6:8, :]
            PREf = PRE.rearrange("p k f -> p (k f)")
            PREimg = PRE.rearrange("p k (y x) -> p (k y) x", x=W)
            NSTORE = 4 * 4 * HALVES * DG
            per_bank = 4 * HALVES

            def image(b):
                return slice(PX * b, PX * b + PX)

            def inner(t, b):
                return t[:, b, 1:H + 1, 1:W + 1]

            def square(t):
                return t.rearrange("p (y x) -> p y x", x=W)

            def convolve(t, w, src, b):
                for k in range(2):
                    for tap in range(TAPS):
                        mm = t.matmul(PS[:, 6 + k, :], w[:, tap, :], patch(src, 2 * b + k, tap), start=(tap == 0),
                                      stop=(tap == TAPS - 1))
                return mm

            def turn(t, src):
                for tl in range(TILES):
                    mm = t.transpose(PS[:, 6 + tl // 4, 128 * (tl % 4):128 * (tl % 4) + 128],
                                     src[:, 128 * tl:128 * tl + 128], K["ident"][:, :])
                return mm

            def stage_pe(t, b, s):
                if s == 0:
                    if b:
                        t.wait_ge(off_t, b)
                    convolve(t, W1, XP, b).then_inc(quant_ps, 1)
                elif s == 1:
                    t.wait_ge(acts, b + 1)
                    convolve(t, W2, AP, b).then_inc(layer2_ps, 1)
                elif s == 2:
                    if b == 0:
                        t.wait_ge(w_sb, 1)
                    t.wait_ge(layer2, b + 1)
                    convolve(t, WB[0], XP, b).then_inc(block1_ps, 1)
                elif s == 3:
                    t.wait_ge(block1, b + 1)
                    convolve(t, WB[1], T1, b).then_inc(block2_ps, 1)
                elif s == 4:
                    t.wait_ge(block2, b + 1)
                    turn(t, H2).then_inc(h_t_ps, 1)
                elif s == 5:
                    t.wait_ge(h_t, b + 1)
                    convolve(t, WB[2], XP, b).then_inc(off_ps, 1)
                else:
                    t.wait_ge(off_sb, b + 1)
                    turn(t, OFF).then_inc(off_t_ps, 1)

            def stage_act(a, b, s):
                if s == 0:
                    a.wait_ge(quant_ps, b + 1)
                    a.activation(T[:, :], PREf, ACT.Identity, scale=INV2[:, 0:1], bias=SHIFT2[:, 0:1])\
                     .then_inc(quant_sb, 1)
                elif s == 2:
                    a.wait_ge(block1_ps, b + 1)
                    a.activation(inner(T1, b), PREimg, ACT.Relu, scale=INV[:, 0:1], bias=SHIFT[:, 0:1])\
                     .then_inc(block1, 1)
                elif s == 4:
                    a.wait_ge(h_t_ps, b + 1)
                    if b:
                        a.wait_ge(stored[b - 1], 16 * NSTORE)
                    a.activation(HT[:, :, :].rearrange("p t c -> p (t c)"), PREf, ACT.Copy).then_inc(h_t, 1)
                elif s == 5:
                    a.wait_ge(off_ps, b + 1)
                    a.activation(OFF[:, :], PREf, ACT.Identity, bias=BIAS3[:, 4:5]).then_inc(off_sb, 1)
                elif s == 6:
                    a.wait_ge(off_t_ps, b + 1)
                    a.activation(OT[:, :, :].rearrange("p t c -> p (t c)"), PREf, ACT.Copy)
                    a.drain().then_inc(off_t, 1)
                    a.activation(mask[:, :, :], off3[:, :, 2 * GK:3 * GK], ACT.Sigmoid).then_inc(masked, 1)

            def stage_dve(v, b, s):
                if s == 0:
                    v.wait_ge(quant_sb, b + 1)
                    v.tensor_scalar(T[:, :], T[:, :], 0.0, 1.0, ALU.max, ALU.min)
                    v.drain()
                    v.tensor_scalar(T[:, :], T[:, :], LEVELS, MAGIC, ALU.mult, ALU.add)
                    v.drain()
                    v.tensor_scalar(inner(AP, b), square(T[:, :]), MAGIC, None, ALU.subtract)
                    v.drain().then_inc(acts, 1)
                elif s == 1:
                    v.wait_ge(layer2_ps, b + 1)
                    v.scalar_tensor_tensor(out=T[:, :], in0=PREf, scalar=INV2[:, 1:2], in1=X[:, image(b)],
                                           op0=ALU.mult, op1=ALU.add)
                    v.drain()
                    v.tensor_scalar(T[:, :], T[:, :], SHIFT2[:, 1:2], 0.0, ALU.add, ALU.max)
                    v.drain()
                    v.tensor_scalar(T[:, :], T[:, :], 1.0, LEVELS, ALU.min, ALU.mult)
                    v.drain()
                    v.tensor_scalar(T[:, :], T[:, :], MAGIC, MAGIC, ALU.add, ALU.subtract)
                    v.drain()
                    v.tensor_scalar(X[:, image(b)], T[:, :], 1.0 / LEVELS, None, ALU.mult)
                    v.tensor_scalar(inner(XP, b), square(T[:, :]), 1.0 / LEVELS, None, ALU.mult)
                    v.drain().then_inc(layer2, 1)
                elif s == 3:
                    v.wait_ge(block2_ps, b + 1)
                    v.scalar_tensor_tensor(out=H2[:, :], in0=PREf, scalar=INV[:, 1:2], in1=X[:, image(b)],
                                           op0=ALU.mult, op1=ALU.add)
                    v.drain()
                    v.tensor_scalar(H2[:, :], H2[:, :], SHIFT[:, 1:2], 0.0, ALU.add, ALU.max)
                    v.drain()
                    v.tensor_copy(inner(XP, b), square(H2[:, :]))
                    v.drain().then_inc(block2, 1)
                elif s == 6:
                    v.wait_ge(off_t, b + 1)
                    v.wait_ge(gridded, 48)
                    p3 = pos[:, :, :].rearrange("p a (t k) -> p a t k", k=GK)
                    for axis in range(2):
                        v.tensor_tensor(p3[:, axis], off3[:, :, axis:2 * GK:2],
                                        GR[:, axis, :].rearrange("p (t k) -> p t k", k=GK), ALU.add)
                    v.drain()
                    v.tensor_scalar(pos[:, :, :], pos[:, :, :], -1.0, float(H), ALU.max, ALU.min)
                    v.drain()
                    v.tensor_copy(whole[:, :, :], pos[:, :, :])
                    v.drain()
                    v.tensor_copy(low[:, :, :], whole[:, :, :])
                    v.drain()
                    v.tensor_tensor(above[:, :, :], low[:, :, :], pos[:, :, :], ALU.is_gt)
                    v.drain()
                    v.tensor_tensor(low[:, :, :], low[:, :, :], above[:, :, :], ALU.subtract)
                    v.drain()
                    v.tensor_tensor(pos[:, :, :], pos[:, :, :], low[:, :, :], ALU.subtract)
                    v.drain()
                    v.tensor_tensor(low[:, 1, :], low[:, 1, :], GR[:, 2, :], ALU.add)
                    v.tensor_scalar(above[:, :, :], pos[:, :, :], -1.0, 1.0, ALU.mult, ALU.add)
                    v.drain()
                    v.scalar_tensor_tensor(out=low[:, 0, :], in0=low[:, 0, :], scalar=float(TP), in1=low[:, 1, :],
                                           op0=ALU.mult, op1=ALU.add)
                    v.drain()
                    v.tensor_copy(IDX[:, b % 2].rearrange("p t k -> p (t k)"), low[:, 0, :])
                    v.drain().then_inc(indexed, 1)
                    v.wait_ge(masked, b + 1)
                    mk = mask[:, :, :].rearrange("p t k -> p (t k)")
                    w4 = W4[:, b % 2].rearrange("p t k c -> p (t k) c")
                    v.tensor_tensor(above[:, 0, :], above[:, 0, :], mk, ALU.mult)
                    v.tensor_tensor(pos[:, 0, :], pos[:, 0, :], mk, ALU.mult)
                    v.drain()
                    for c, (wy, wx) in enumerate(((above, above), (above, pos), (pos, above), (pos, pos))):
                        v.tensor_tensor(w4[:, :, c], wy[:, 0, :], wx[:, 1, :], ALU.mult)
                    v.drain()

            def weights_pe(t):
                t.wait_ge(loads, NLOAD)
                t.wait_ge(split, 1)
                for i in range(3):
                    m = A["L3_conv_" + ws[i]].shape[0]
                    for tap in range(TAPS):
                        t.matmul(PS[:, 2 * i + tap // 8, 64 * (tap % 8):64 * (tap % 8) + m],
                                 raw[i][0:m, :, tap], K["ident"][0:m, 0:m], start=True, stop=True)
                t.matmul(PS[:, 1, 64:128], rawcv, K["ident"][0:64, 0:64], start=True, stop=True)
                for c in range(5):
                    n = min(4, GK - 4 * c) * CG
                    mm = t.matmul(PS[0:n, 1, 128 + 64 * c:192 + 64 * c],
                                  dcs.rearrange("o g c -> o (g c)")[:, 128 * c:128 * c + n],
                                  K["ident"][0:64, 0:64], start=True, stop=True)
                mm.then_inc(w_ps, 1)

            def weights_dve(v):
                v.wait_ge(w_ps, 1)
                v.wait_ge(cleared, 1)
                for i in range(3):
                    m = A["L3_conv_" + ws[i]].shape[0]
                    block_weights(v, WB[i], PS[:, 2 * i:2 * i + 2, :].rearrange("p a (t o) -> p (a t) o", o=CH)
                                  [:, 0:TAPS, 0:m], "half_nat", m)
                block_weights(v, CV2, PS[:, 1:2, 64:128], "half_nat")
                v.tensor_copy(DC[:, 0:4, :], PS[:, 1, 128:384].rearrange("p (a o) -> p a o", o=CH))
                v.tensor_copy(DC[0:64, 4, :], PS[0:64, 1, 384:448])
                v.drain().then_inc(w_sb, 1)

            def steps(engine, stage, weights, sample):
                for s in range(STAGES):
                    stage(engine, 0, s)
                    if s == 0 and weights:
                        weights(engine)
                for th in range(NB * STEPS):
                    sample(th)
                    b, step = th // STEPS, th % STEPS
                    if b + 1 < NB and step in AT_STEP:
                        stage(engine, b + 1, AT_STEP[step])

            with nc.Block() as blk:
                @blk.gpsimd
                def _(g):
                    g.memset(AP[:, :, :, :], 0.0)
                    g.memset(WB[2][:, :, :], 0.0)
                    g.drain().then_inc(cleared, 1)
                    for th in range(NB * STEPS):
                        b, step = th // STEPS, th % STEPS
                        if step == 0:
                            g.wait_ge(indexed, b + 1)
                            g.wait_ge(stored[b], 16 * NSTORE)
                        if th >= RING:
                            g.wait_ge(used, th - RING + 1)
                        for k in range(GK):
                            g.indirect_dma_start(G[th % RING][:, k, :], None, tables[b],
                                                 bass.IndirectOffsetOnAxis(ap=IDX[:, b % 2, step, k:k + 1], axis=0))\
                             .then_inc(arrived[th % RING], 16)

                @blk.sync
                def _(sp):
                    def load(dst, src):
                        sp.dma_start(dst, src).then_inc(loads, 16)
                    load(rawdc, A["L3_conv_dc_w"].rearrange("o c ky kx -> o c (ky kx)"))
                    for h in range(HALVES):
                        for i, n in enumerate(ws):
                            load(raw[i][0:A["L3_conv_" + n].shape[0], 64 * h:64 * h + 64, :],
                                 A["L3_conv_" + n].rearrange("o c ky kx -> o c (ky kx)"))
                        load(rawcv[:, 64 * h:64 * h + 64], A["L3_conv_cv2_w"].rearrange("o c ky kx -> o (c ky kx)"))
                    for i, g in enumerate(GRIDS):
                        sp.dma_start(GR[:, i, :], C[g]).then_inc(gridded, 16)
                    sp.wait_ge(loads, NLOAD)

                    def write(b):
                        for h in range(HALVES):
                            sp.dma_start(out[NB * h + b].rearrange("c y x -> c (y x)"),
                                         X[64 * h:64 * h + 64, image(b)]).then_inc(written, 16)

                    for b in range(NB):
                        table = tables[b].rearrange("(q ey ex) (k c) -> q ey ex k c", q=HALVES * DG, ey=TP, k=4)
                        sp.wait_ge(h_t, b + 1)
                        for yr in range(4):
                            for dy in range(2):
                                for dx in range(2):
                                    first = yr - dy + 1
                                    for q in range(HALVES * DG):
                                        sp.dma_start(
                                            table[q, first:first + 29:4, 1 - dx:1 - dx + W, 2 * dy + dx, :]
                                            .rearrange("e x c -> x e c"),
                                            HT[32 * yr:32 * yr + 32, :, CG * q:CG * q + CG])\
                                          .then_inc(stored[b], 16)
                        if b:
                            sp.wait_ge(final, 2 * b)
                            write(b - 1)
                    sp.wait_ge(final, 2 * NB)
                    write(NB - 1)
                    sp.wait_ge(written, 16 * HALVES * NB)
                    for b in range(NB):
                        sp.wait_ge(stored[b], 16 * NSTORE)

                @blk.vector
                def _(v):
                    def sample(th):
                        gt, w4 = G[th % RING], W4[:, (th // STEPS) % 2, th % STEPS]
                        v.wait_ge(arrived[th % RING], 16 * GK * (th // RING + 1))
                        g3 = gt[:, :, :].rearrange("p k (q c) -> p (k q) c", q=4)
                        v.tensor_tensor(g3, g3, w4.rearrange("p k q -> p (k q)").unsqueeze(2)
                                        .broadcast_to([128, GK * 4, CG]), ALU.mult)
                        v.drain()
                        if th >= 2:
                            v.wait_ge(t_ps, th - 1)
                        v.tensor_reduce(VAL[:, th % 2, :, :], gt[:, :, :].rearrange("p k (q c) -> p k c q", q=4),
                                        AX.X, ALU.add)
                        v.drain().then_inc(val, 1)
                        v.sem_inc(used, 1)
                        if th % per_bank == per_bank - 1:
                            k = th // per_bank
                            y, u, x = Y[:, k % 2, :], U[:, k % 2, :], X[:, BANK * k:BANK * k + BANK]
                            v.wait_ge(d_sb, k + 1)
                            v.scalar_tensor_tensor(out=y, in0=y, scalar=0.1, in1=y, op0=ALU.mult, op1=ALU.max)
                            v.drain().then_inc(leaky, 1)
                            v.wait_ge(e_sb, k + 1)
                            v.scalar_tensor_tensor(out=u, in0=u, scalar=0.1, in1=u, op0=ALU.mult, op1=ALU.max)
                            v.drain()
                            v.tensor_tensor(x, x, u, ALU.add)
                            v.drain().then_inc(final, 1)
                    v.tensor_scalar(INV2[:, :], BV2[:, 3, :], 1e-5, None, ALU.add)
                    v.tensor_scalar(INV[:, :], BV3[:, 3, :], 1e-5, None, ALU.add)
                    v.drain().then_inc(root, 1)
                    v.wait_ge(rooted, 1)
                    v.reciprocal(INV2[:, :], root2[:, :])
                    v.reciprocal(INV[:, :], root3[:, :])
                    v.tensor_tensor(SHIFT[:, :], BIAS3[:, 0:4], BV3[:, 2, :], ALU.subtract)
                    v.drain()
                    v.tensor_tensor(INV2[:, :], INV2[:, :], BV2[:, 0, :], ALU.mult)
                    v.tensor_tensor(INV[:, :], INV[:, :], BV3[:, 0, :], ALU.mult)
                    v.drain()
                    v.tensor_tensor(SHIFT2[:, :], INV2[:, :], BV2[:, 2, :], ALU.mult)
                    v.tensor_tensor(SHIFT[:, :], SHIFT[:, :], INV[:, :], ALU.mult)
                    v.drain()
                    v.tensor_tensor(SHIFT2[:, :], BV2[:, 1, :], SHIFT2[:, :], ALU.subtract)
                    v.tensor_tensor(SHIFT[:, :], SHIFT[:, :], BV3[:, 1, :], ALU.add)
                    v.tensor_scalar(INV2[:, 0:1], INV2[:, 0:1], 1.0 / LEVELS, None, ALU.mult)
                    v.tensor_scalar(INV2[:, 1:2], INV2[:, 1:2], 1.0 / LEVELS ** 2, None, ALU.mult)
                    v.drain().then_inc(scaled, 1)
                    v.wait_ge(loads, NLOAD)
                    for d in range(DG):
                        v.tensor_copy(dcs[:, TAPS * d:TAPS * d + TAPS, :],
                                      rawdc[:, CG * d:CG * d + CG, :].rearrange("o c k -> o k c"))
                    v.drain().then_inc(split, 1)
                    v.wait_ge(cleared, 1)
                    steps(v, stage_dve, weights_dve, sample)

                @blk.tensor
                def _(t):
                    def sample(th):
                        tl, h, k = th // 2, th % 2, th // per_bank
                        t.wait_ge(val, th + 1)
                        if th >= 2:
                            t.wait_ge(t_sb, th - 1)
                        flat = VAL[:, th % 2, :, :].rearrange("p k c -> p (k c)")
                        for c in range(5):
                            n = min(128, GK * CG - 128 * c)
                            o = 128 * c if c < 4 else 128 * (th % 2)
                            mm = t.transpose(PS[0:n, th % 2 if c < 4 else 2, o:o + 128],
                                             flat[:, 128 * c:128 * c + n], K["ident"][:, :])
                        mm.then_inc(t_ps, 1)
                        t.wait_ge(t_sb, th + 1)
                        if th % per_bank == 0 and k >= 2:
                            t.wait_ge(d_sb, k - 1)
                        for c in range(5):
                            n = min(128, GK * CG - 128 * c)
                            mm = t.matmul(PS[64 * h:64 * h + 64, 3 + k % 2, 128 * (tl % 4):128 * (tl % 4) + 128],
                                          DC[0:n, c, :], VT[0:n, th % 2, c, :], start=(c == 0), stop=(c == 4))
                        if th % per_bank == per_bank - 1:
                            mm.then_inc(d_ps, 1)
                            t.wait_ge(leaky, k + 1)
                            t.matmul(bank(5), CV2[:, 0, :], Y[:, k % 2, :], start=True, stop=True).then_inc(e_ps, 1)
                    steps(t, stage_pe, weights_pe, sample)

                @blk.scalar
                def _(a):
                    def sample(th):
                        k = th // per_bank
                        a.wait_ge(t_ps, th + 1)
                        a.activation(VT[:, th % 2, 0:4, :], PS[:, th % 2, :].rearrange("p (a c) -> p a c", c=128),
                                     ACT.Copy)
                        a.activation(VT[0:64, th % 2, 4, :], PS[0:64, 2, 128 * (th % 2):128 * (th % 2) + 128], ACT.Copy)
                        a.drain().then_inc(t_sb, 1)
                        if th % per_bank == per_bank - 1:
                            a.wait_ge(d_ps, k + 1)
                            a.activation(Y[:, k % 2, :], bank(3 + k % 2), ACT.Identity, scale=INV[:, 2:3],
                                         bias=SHIFT[:, 2:3]).then_inc(d_sb, 1)
                            a.wait_ge(e_ps, k + 1)
                            a.activation(U[:, k % 2, :], bank(5), ACT.Identity, scale=INV[:, 3:4],
                                         bias=SHIFT[:, 3:4]).then_inc(e_sb, 1)
                    a.wait_ge(root, 1)
                    a.activation(root2[:, :], INV2[:, :], ACT.Sqrt)
                    a.activation(root3[:, :], INV[:, :], ACT.Sqrt)
                    a.drain().then_inc(rooted, 1)
                    a.wait_ge(scaled, 1)
                    steps(a, stage_act, None, sample)

        phase(sampler)
        lay3.close()


def kernel(**inputs):
    import numpy as _np
    import concourse.bacc as _bacc
    from concourse import mybir as _mybir
    from concourse.bass_utils import run_bass_kernel_spmd as _run

    nc = _bacc.Bacc("TRN2", target_bir_lowering=False, num_devices=1)
    arrays, args, consts = {}, {}, {}
    for name, value in inputs.items():
        a = _np.ascontiguousarray(value)
        arrays["in_" + name] = a
        args[name] = nc.dram_tensor("in_" + name, a.shape, _mybir.dt.from_np(a.dtype), kind="ExternalInput").ap()
    for name, a in constants().items():
        arrays["const_" + name] = a
        consts[name] = nc.dram_tensor("const_" + name, a.shape, _mybir.dt.from_np(a.dtype), kind="ExternalInput").ap()
    out = nc.dram_tensor("out", (B, CH, H, W), F32, kind="ExternalOutput").ap()
    program(nc, args, consts, out)
    r = _run(nc, [arrays], core_ids=[0])
    return r.results[0]["out"]
```
